# Optimizing a Trainium2 kernel written in Bass

```python
import numpy as np
import jax
import jax.numpy as jnp

def _softmax(x, axis=-1):
    return jax.nn.softmax(x, axis=axis)

def _gelu(x):
    return jax.nn.gelu(x, approximate=True)

def _silu(x):
    return jax.nn.silu(x)

def _sigmoid(x):
    return jax.nn.sigmoid(x)

def _layernorm(x, axis=-1, eps=1e-05):
    m = jnp.mean(x, axis=axis, keepdims=True)
    v = jnp.var(x, axis=axis, keepdims=True)
    return (x - m) / jnp.sqrt(v + eps)

def _scatter_add(tgt, idx, src, axis=0):
    return tgt.at[idx].add(src)

def _segment_sum(src, seg, n):
    return jax.ops.segment_sum(src, seg, n)
kernel_name = 'mk_gps_d1_gnn_r8_12b534'

def setup_inputs(seed: int=0):
    np.random.seed(seed)
    _w = jnp.asarray

    def _rec_inputs():
        import jax
        import jax.numpy as jnp
        _gk = jax.random.key(seed)
        x = -0.0002117 + 1 * jax.random.normal(jax.random.fold_in(_gk, 1), (6250, 256), jnp.float32)
        src = jax.random.randint(jax.random.fold_in(_gk, 2), (100000,), 0, 6250, jnp.int32)
        dst = jax.random.randint(jax.random.fold_in(_gk, 3), (100000,), 0, 6250, jnp.int32)
        _o = jnp.argsort(dst, stable=True)
        src = src[_o]
        dst = dst[_o]
        return (x, src, dst)
    x, src, dst = _rec_inputs()

    def _L0_gnn_setup():
        import jax, jax.numpy as jnp
        import numpy as np
        N_NODES = 12500
        N_EDGES = 400000
        NFEAT = 256
        NHID = 256
        key = jax.random.key(seed)
        k_x, k_ws, k_wn, k_src, k_dst = jax.random.split(key, 5)
        x = jax.random.normal(k_x, (N_NODES, NFEAT), dtype=jnp.float32)
        W_self = jax.random.normal(k_ws, (NFEAT, NHID), dtype=jnp.float32) * (1.0 / np.sqrt(NFEAT))
        W_neigh = jax.random.normal(k_wn, (NFEAT, NHID), dtype=jnp.float32) * (1.0 / np.sqrt(NFEAT))
        b = jnp.zeros((NHID,), dtype=jnp.float32)
        edge_src = jax.random.randint(k_src, (N_EDGES,), 0, N_NODES, dtype=jnp.int32)
        edge_dst = jax.random.randint(k_dst, (N_EDGES,), 0, N_NODES, dtype=jnp.int32)
        return {'x': x, 'W_self': W_self, 'W_neigh': W_neigh, 'b': b, 'edge_src': edge_src, 'edge_dst': edge_dst}
    _L0_gnn_all = _L0_gnn_setup()
    _L0_gnn_in = {k: v for k, v in _L0_gnn_all.items() if k in ('W_self', 'W_neigh', 'b')}
    del _L0_gnn_all

    def _L0_mix_setup():
        import jax, jax.numpy as jnp
        import numpy as np
        B, N, C, H = (8, 2048, 256, 8)
        D = C // H
        GH = C // 4
        key = jax.random.key(seed)
        ks = jax.random.split(key, 6)
        s = 0.02
        return {'x': jax.random.normal(ks[0], (B, N, C), dtype=jnp.float32), 'Wqkv': jax.random.normal(ks[1], (C, 3 * C), dtype=jnp.float32) * s, 'Wproj': jax.random.normal(ks[2], (C, C), dtype=jnp.float32) * s, 'bproj': jnp.zeros((C,), dtype=jnp.float32), 'ln_g': jnp.ones((C,), dtype=jnp.float32), 'ln_b': jnp.zeros((C,), dtype=jnp.float32), 'Wg1': jax.random.normal(ks[3], (C, GH), dtype=jnp.float32) * s, 'bg1': jnp.zeros((GH,), dtype=jnp.float32), 'Wg2': jax.random.normal(ks[4], (GH, C), dtype=jnp.float32) * s, 'bg2': jnp.zeros((C,), dtype=jnp.float32)}
    _L0_mix_all = _L0_mix_setup()
    _L0_mix_in = {k: v for k, v in _L0_mix_all.items() if k in ('Wqkv', 'Wproj', 'bproj', 'ln_g', 'ln_b', 'Wg1', 'bg1', 'Wg2', 'bg2')}
    del _L0_mix_all

    def _L0_ffn_setup():
        import jax, jax.numpy as jnp
        import numpy as np
        B, N, D = (16, 512, 256)
        NUM_EXPERTS, TOP_K, HEADS = (4, 2, 4)
        N_EDGES = 131072
        LN_EPS = 1e-05

        def _layernorm(x, g, b):
            mu = x.mean(-1, keepdims=True)
            var = ((x - mu) ** 2).mean(-1, keepdims=True)
            return (x - mu) * jax.lax.rsqrt(var + LN_EPS) * g + b

        def _forward(x, edge_index, W_gat, att_src, att_dst, b_gat, ln_gamma, ln_beta, W1, b1, W2, b2):
            Bc, Nc, Dc = x.shape
            M = Bc * Nc
            x_flat = x.reshape(M, Dc)
            h = (x_flat @ W_gat).reshape(M, HEADS, NUM_EXPERTS)
            loops = jnp.arange(M, dtype=edge_index.dtype)
            src = jnp.concatenate([edge_index[0], loops])
            dst = jnp.concatenate([edge_index[1], loops])
            a_src = (h * att_src).sum(-1)
            a_dst = (h * att_dst).sum(-1)
            e = jax.nn.leaky_relu(a_src[src] + a_dst[dst], negative_slope=0.2)
            e_max = jax.ops.segment_max(e, dst, num_segments=M)
            ee = jnp.exp(e - e_max[dst])
            denom = jax.ops.segment_sum(ee, dst, num_segments=M)
            alpha = ee / (denom[dst] + 1e-16)
            msg = h[src] * alpha[:, :, None]
            agg = jax.ops.segment_sum(msg, dst, num_segments=M).reshape(M, HEADS * NUM_EXPERTS) + b_gat
            scores = _layernorm(agg, ln_gamma, ln_beta).reshape(M, HEADS, NUM_EXPERTS).mean(1)
            scores = scores.reshape(Bc, Nc, NUM_EXPERTS)
            topk_s, topk_i = jax.lax.top_k(scores, TOP_K)
            w = jax.nn.softmax(topk_s, axis=-1)
            out = jnp.zeros_like(x)
            for ei in range(NUM_EXPERTS):
                g = jnp.where(topk_i == ei, w, 0.0).sum(-1)
                hh = jax.nn.gelu(x @ W1[ei] + b1[ei], approximate=False)
                out = out + g[..., None] * (hh @ W2[ei] + b2[ei])
            return out
        key = jax.random.key(seed)
        ks = jax.random.split(key, 8)
        s = 0.05
        return {'x': jax.random.normal(ks[0], (B, N, D), jnp.float32), 'W_gat': jax.random.normal(ks[1], (D, HEADS * NUM_EXPERTS), jnp.float32) * s, 'att_src': jax.random.normal(ks[2], (HEADS, NUM_EXPERTS), jnp.float32) * s, 'att_dst': jax.random.normal(ks[3], (HEADS, NUM_EXPERTS), jnp.float32) * s, 'b_gat': jnp.zeros((HEADS * NUM_EXPERTS,), jnp.float32), 'ln_gamma': jnp.ones((HEADS * NUM_EXPERTS,), jnp.float32), 'ln_beta': jnp.zeros((HEADS * NUM_EXPERTS,), jnp.float32), 'W1': jax.random.normal(ks[4], (NUM_EXPERTS, D, 2 * D), jnp.float32) * s, 'b1': jnp.zeros((NUM_EXPERTS, 2 * D), jnp.float32), 'W2': jax.random.normal(ks[5], (NUM_EXPERTS, 2 * D, D), jnp.float32) * s, 'b2': jnp.zeros((NUM_EXPERTS, D), jnp.float32), 'edge_index': jax.random.randint(ks[6], (2, N_EDGES), 0, B * N, jnp.int32)}
    _L0_ffn_all = _L0_ffn_setup()
    _L0_ffn_in = {k: v for k, v in _L0_ffn_all.items() if k in ('W_gat', 'att_src', 'att_dst', 'b_gat', 'ln_gamma', 'ln_beta', 'W1', 'b1', 'W2', 'b2', 'edge_index')}
    del _L0_ffn_all
    return {'x': x, 'src': src, 'dst': dst, 'L0_gnn_W_self': _L0_gnn_in['W_self'], 'L0_gnn_W_neigh': _L0_gnn_in['W_neigh'], 'L0_gnn_b': _L0_gnn_in['b'], 'L0_mix_Wqkv': _L0_mix_in['Wqkv'], 'L0_mix_Wproj': _L0_mix_in['Wproj'], 'L0_mix_bproj': _L0_mix_in['bproj'], 'L0_mix_ln_g': _L0_mix_in['ln_g'], 'L0_mix_ln_b': _L0_mix_in['ln_b'], 'L0_mix_Wg1': _L0_mix_in['Wg1'], 'L0_mix_bg1': _L0_mix_in['bg1'], 'L0_mix_Wg2': _L0_mix_in['Wg2'], 'L0_mix_bg2': _L0_mix_in['bg2'], 'L0_ffn_W_gat': _L0_ffn_in['W_gat'], 'L0_ffn_att_src': _L0_ffn_in['att_src'], 'L0_ffn_att_dst': _L0_ffn_in['att_dst'], 'L0_ffn_b_gat': _L0_ffn_in['b_gat'], 'L0_ffn_ln_gamma': _L0_ffn_in['ln_gamma'], 'L0_ffn_ln_beta': _L0_ffn_in['ln_beta'], 'L0_ffn_W1': _L0_ffn_in['W1'], 'L0_ffn_b1': _L0_ffn_in['b1'], 'L0_ffn_W2': _L0_ffn_in['W2'], 'L0_ffn_b2': _L0_ffn_in['b2'], 'L0_ffn_edge_index': _L0_ffn_in['edge_index']}

def reference(x, src, dst, L0_gnn_W_self, L0_gnn_W_neigh, L0_gnn_b, L0_mix_Wqkv, L0_mix_Wproj, L0_mix_bproj, L0_mix_ln_g, L0_mix_ln_b, L0_mix_Wg1, L0_mix_bg1, L0_mix_Wg2, L0_mix_bg2, L0_ffn_W_gat, L0_ffn_att_src, L0_ffn_att_dst, L0_ffn_b_gat, L0_ffn_ln_gamma, L0_ffn_ln_beta, L0_ffn_W1, L0_ffn_b1, L0_ffn_W2, L0_ffn_b2, L0_ffn_edge_index):
    import jax
    import jax.numpy as jnp

    def _L0_gnn_ref(x, W_self, W_neigh, b, edge_src, edge_dst):
        import jax, jax.numpy as jnp
        import numpy as np
        N_NODES = 12500
        N_EDGES = 400000
        NFEAT = 256
        NHID = 256
        n = x.shape[0]
        msg = x[edge_src]
        agg = jax.ops.segment_sum(msg, edge_dst, num_segments=n)
        deg = jax.ops.segment_sum(jnp.ones_like(edge_dst, dtype=x.dtype), edge_dst, num_segments=n)
        h_neigh = agg / jnp.maximum(deg, 1.0)[:, None]
        out = x @ W_self + h_neigh @ W_neigh + b
        return jax.nn.relu(out)

    def _L0_mix_ref(x, Wqkv, Wproj, bproj, ln_g, ln_b, Wg1, bg1, Wg2, bg2):
        import jax, jax.numpy as jnp
        import numpy as np
        B, N, C, H = (8, 2048, 256, 8)
        D = C // H
        GH = C // 4
        b, n, c = x.shape
        h, d = (H, D)
        qkv = (x @ Wqkv).reshape(b, n, 3, h, d)
        q, k, v = (qkv[:, :, 0], qkv[:, :, 1], qkv[:, :, 2])
        k = jax.nn.softmax(k, axis=1)
        context = jnp.einsum('bnhd,bnhv->bhdv', k, v)
        out = jnp.einsum('bnhd,bhdv->bnhv', q, context).reshape(b, n, c)
        mu = jnp.mean(x, axis=-1, keepdims=True)
        var = jnp.var(x, axis=-1, keepdims=True)
        xn = (x - mu) * jax.lax.rsqrt(var + 1e-05) * ln_g + ln_b
        hgate = jax.nn.gelu(xn @ Wg1 + bg1, approximate=False)
        gate = jax.nn.sigmoid(hgate @ Wg2 + bg2)
        return out * gate @ Wproj + bproj

    def _L0_ffn_ref(x, W_gat, att_src, att_dst, b_gat, ln_gamma, ln_beta, W1, b1, W2, b2, edge_index):
        import jax, jax.numpy as jnp
        import numpy as np
        B, N, D = (16, 512, 256)
        NUM_EXPERTS, TOP_K, HEADS = (4, 2, 4)
        N_EDGES = 131072
        LN_EPS = 1e-05

        def _layernorm(x, g, b):
            mu = x.mean(-1, keepdims=True)
            var = ((x - mu) ** 2).mean(-1, keepdims=True)
            return (x - mu) * jax.lax.rsqrt(var + LN_EPS) * g + b

        def _forward(x, edge_index, W_gat, att_src, att_dst, b_gat, ln_gamma, ln_beta, W1, b1, W2, b2):
            Bc, Nc, Dc = x.shape
            M = Bc * Nc
            x_flat = x.reshape(M, Dc)
            h = (x_flat @ W_gat).reshape(M, HEADS, NUM_EXPERTS)
            loops = jnp.arange(M, dtype=edge_index.dtype)
            src = jnp.concatenate([edge_index[0], loops])
            dst = jnp.concatenate([edge_index[1], loops])
            a_src = (h * att_src).sum(-1)
            a_dst = (h * att_dst).sum(-1)
            e = jax.nn.leaky_relu(a_src[src] + a_dst[dst], negative_slope=0.2)
            e_max = jax.ops.segment_max(e, dst, num_segments=M)
            ee = jnp.exp(e - e_max[dst])
            denom = jax.ops.segment_sum(ee, dst, num_segments=M)
            alpha = ee / (denom[dst] + 1e-16)
            msg = h[src] * alpha[:, :, None]
            agg = jax.ops.segment_sum(msg, dst, num_segments=M).reshape(M, HEADS * NUM_EXPERTS) + b_gat
            scores = _layernorm(agg, ln_gamma, ln_beta).reshape(M, HEADS, NUM_EXPERTS).mean(1)
            scores = scores.reshape(Bc, Nc, NUM_EXPERTS)
            topk_s, topk_i = jax.lax.top_k(scores, TOP_K)
            w = jax.nn.softmax(topk_s, axis=-1)
            out = jnp.zeros_like(x)
            for ei in range(NUM_EXPERTS):
                g = jnp.where(topk_i == ei, w, 0.0).sum(-1)
                hh = jax.nn.gelu(x @ W1[ei] + b1[ei], approximate=False)
                out = out + g[..., None] * (hh @ W2[ei] + b2[ei])
            return out
        return _forward(x, edge_index, W_gat, att_src, att_dst, b_gat, ln_gamma, ln_beta, W1, b1, W2, b2)
    xn = _layernorm(x, axis=-1)
    x = x + _L0_gnn_ref(xn, L0_gnn_W_self, L0_gnn_W_neigh, L0_gnn_b, src, dst) + _L0_mix_ref(xn[None], L0_mix_Wqkv, L0_mix_Wproj, L0_mix_bproj, L0_mix_ln_g, L0_mix_ln_b, L0_mix_Wg1, L0_mix_bg1, L0_mix_Wg2, L0_mix_bg2)[0]
    x = x + _L0_ffn_ref(_layernorm(x, axis=-1)[None], L0_ffn_W_gat, L0_ffn_att_src, L0_ffn_att_dst, L0_ffn_b_gat, L0_ffn_ln_gamma, L0_ffn_ln_beta, L0_ffn_W1, L0_ffn_b1, L0_ffn_W2, L0_ffn_b2, L0_ffn_edge_index)[0]
    return x

_drawn_inputs = setup_inputs


def setup_inputs(seed=0):
    import zlib

    import numpy as np

    out = dict(_drawn_inputs(seed))
    spreads = {'L0_gnn_b': (0.0, 0.8),
     'L0_mix_bproj': (0.0, 0.626),
     'L0_mix_ln_g': (1.0, 0.6),
     'L0_mix_ln_b': (0.0, 0.8),
     'L0_mix_bg1': (0.0, 0.8),
     'L0_mix_bg2': (0.0, 0.8),
     'L0_ffn_b_gat': (0.0, 0.363),
     'L0_ffn_ln_gamma': (1.0, 0.6),
     'L0_ffn_ln_beta': (0.0, 0.763),
     'L0_ffn_b1': (0.0, 0.8),
     'L0_ffn_b2': (0.0, 0.8)}
    factors = {'L0_mix_Wqkv': 7.145,
     'L0_mix_Wproj': 8.0,
     'L0_mix_Wg1': 8.0,
     'L0_mix_Wg2': 8.0,
     'L0_gnn_W_neigh': 2.799,
     'L0_ffn_att_src': 8.0,
     'L0_ffn_att_dst': 8.0}
    for name, (base, spread) in spreads.items():
        noise = np.random.default_rng([zlib.crc32(name.encode()), seed]).standard_normal(out[name].shape)
        drawn = base * np.exp(spread * noise) if base else spread * noise
        out[name] = jnp.asarray(drawn.astype(out[name].dtype))
    for name, factor in factors.items():
        out[name] = (out[name] * factor).astype(out[name].dtype)
    return out
```

```python
from contextlib import ExitStack

import numpy as np
import concourse.bass as bass
from concourse import mybir

F32 = mybir.dt.float32
I32 = mybir.dt.int32
ALU = mybir.AluOpType
ACT = mybir.ActivationFunctionType
AX_X = mybir.AxisListType.X
DVE_ENGINE = mybir.EngineType.DVE
ds = bass.ds

P = 128
N_NODES = 6250
D = 256
KC = D // P
TILES = -(-N_NODES // P)
N_PAD = TILES * P
GROUPS = 7
GT = TILES // GROUPS
GN = GT * P
HB = GN // 2
LN_EPS = 1e-5
HEADS_MIX = 8
HD = D // HEADS_MIX
GATE_H = 64

EXPERTS = 4
HEADS = 4
HE = HEADS * EXPERTS
HID = 512
HC = HID // P

E_GNN = 100000
E_GAT = 131072
LANE = 1024
SORT_N = P * LANE
OFF = 1 << 30
SRC_BITS = 14
SELF = (1 << SRC_BITS) - 1
DST_MASK = 8191
PAD_DST = 8191

CH_GNN = -(-E_GNN // P)
STEPS = CH_GNN + TILES - 1
SBLK = 16
SHALF = SBLK // 2
S_ITERS = -(-STEPS // SBLK)
STEP_COLS = -(-(S_ITERS * SBLK + SHALF) // P) * P
STEP_G = STEP_COLS // P

SELF_N = 8192
GAT_N = SORT_N + SELF_N
W = GAT_N // P
G_ITERS = W // SBLK
FENCES = GAT_N // P
FENCE_P = 64
ROW = HE + 2 * HEADS
BIG = 1e30
SENTINEL = float(np.array(OFF | PAD_DST << SRC_BITS, np.int32).view(np.float32))

assert TILES == GROUPS * GT and E_GAT == SORT_N and W % SBLK == 0 and FENCES % FENCE_P == 0


def bcast(ap, axis, n):
    v = ap.unsqueeze(axis)
    return v.to_broadcast([*v.shape[:axis], n, *v.shape[axis + 1:]])


class Core:

    def __init__(self, nc):
        self.nc = nc

    def sem(self, name):
        return self.nc.alloc_semaphore(name)

    def dram(self, name, shape, dt=F32):
        return self.nc.dram_tensor(name, shape, dt, kind="Internal").ap()

    def open(self):
        ctx = ExitStack()
        sb = lambda name, shape, dt=F32: ctx.enter_context(self.nc.sbuf_tensor(name, shape, dt))
        ps = lambda name, shape, dt=F32: ctx.enter_context(self.nc.psum_tensor(name, shape, dt))
        return ctx, sb, ps


def constants(c):
    nc = c.nc
    c.ident = nc.alloc_sbuf_tensor("ident", [P, P], F32)
    c.ones = nc.alloc_sbuf_tensor("ones", [P, P], F32)
    c.iota_row = nc.alloc_sbuf_tensor("iota_row", [P, P], F32)
    c.iota_col = nc.alloc_sbuf_tensor("iota_col", [P, 1], I32)
    c.eps = nc.alloc_sbuf_tensor("eps", [P, 1], F32)
    iota_colf = nc.alloc_sbuf_tensor("iota_colf", [P, 1], F32)
    s_iota = c.sem("const_iota")
    with nc.Block() as block:
        @block.gpsimd
        def _(pool):
            nc.gpsimd.iota(c.iota_row[:], pattern=[[1, P]], base=0, channel_multiplier=0,
                           allow_small_or_imprecise_dtypes=True)
            nc.gpsimd.iota(c.iota_col[:], pattern=[[0, 1]], base=0, channel_multiplier=1).then_inc(s_iota, 1)

        @block.vector
        def _(v):
            nc.vector.memset(c.ones[:], 1.0)
            nc.vector.memset(c.eps[:], LN_EPS)
            v.wait_ge(s_iota, 1)
            nc.vector.tensor_copy(iota_colf[:], c.iota_col[:])
            v.drain()
            nc.vector.tensor_scalar(c.ident[:], c.iota_row[:], iota_colf[:], None, ALU.is_equal)


def normalise(c, a):
    nc = c.nc
    ctx, sb, ps = c.open()
    with ctx:
        xg = sb("xg", [P, GT, D])
        xn = sb("xn", [P, GT, D])
        xnn = sb("xnn", [P, GT, D])
        stats = sb("stats", [P, GT, 6])
        mv = sb("mv", [P, GT, 2])
        std = sb("std", [P, GT])
        rstd = sb("rstd", [P, GT])
        xnT = sb("xnT", [P, KC, GN])
        xn2T = sb("xn2T", [P, KC, GN])
        ln_g = sb("ln_g", [P, KC])
        ln_b = sb("ln_b", [P, KC])
        psA = [ps(f"psA{i}", [P, 512]) for i in range(2)]
        psB = [ps(f"psB{i}", [P, 512]) for i in range(2)]
        s_x = c.sem("ln_x")
        s_mv, s_std, s_xn, s_xnn = c.sem("ln_mv"), c.sem("ln_std"), c.sem("ln_xn"), c.sem("ln_xnn")
        s_tA, s_evA, s_tB, s_evB = c.sem("ln_tA"), c.sem("ln_evA"), c.sem("ln_tB"), c.sem("ln_evB")
        s_row, s_row_free, s_outA, s_outB = c.sem("ln_row"), c.sem("ln_row_free"), c.sem("ln_outA"), c.sem("ln_outB")
        x_v = a["x"].rearrange("(t p) d -> t p d", p=P)
        xn_v = c.xn_tab.rearrange("(t p) d -> p t d", p=P)

        with nc.Block() as block:
            @block.gpsimd
            def _(pool):
                with pool.Fori(0, GROUPS) as g:
                    for u in range(GT):
                        pool.wait_ge(s_xn, g * GT + u + 1)
                        pool.dma_start(xg[:, u, :], x_v[ds(g * GT + u, 1)].rearrange("t p d -> (t p) d")).then_inc(s_x, 16)

            @block.sync
            def _(sp):
                sp.sem_inc(s_row_free, 1)
                with sp.Fori(0, GROUPS) as g:
                    sp.wait_ge(s_xn, g * GT + 2 * GT)
                    sp.dma_start(xn_v[:, ds(g * GT, GT), :], xn[:]).then_inc(s_row, 16)
                    sp.wait_ge(s_row, 16 * g + 16)
                    sp.sem_inc(s_row_free, 1)

            @block.vector
            def _(v):
                v.sem_inc(s_xn, GT)

                def moments(rows):
                    for u in range(GT):
                        nc.vector.bn_stats(stats[:, u, :], rows[:, u, :])
                    v.drain()
                    for u in range(GT):
                        last = nc.vector.bn_aggr(mv[:, u, :], stats[:, u, :])
                    return last

                with v.Fori(0, GROUPS) as g:
                    v.wait_ge(s_x, 16 * GT * g + 16 * GT)
                    moments(xg).then_inc(s_mv, 1)
                    v.wait_ge(s_std, 2 * g + 1)
                    nc.vector.reciprocal(rstd[:], std[:])
                    v.drain()
                    v.wait_ge(s_tA, g * GT + GT)
                    v.wait_ge(s_row_free, g + 1)
                    for u in range(GT):
                        nc.vector.tensor_scalar(xn[:, u, :], xg[:, u, :], mv[:, u, 0:1], rstd[:, u:u + 1],
                                                ALU.subtract, ALU.mult).then_inc(s_xn, 1)
                    v.drain()
                    moments(xn).then_inc(s_mv, 1)
                    v.wait_ge(s_std, 2 * g + 2)
                    nc.vector.reciprocal(rstd[:], std[:])
                    v.drain()
                    v.wait_ge(s_tB, g * GT + GT)
                    for u in range(GT):
                        nc.vector.tensor_scalar(xnn[:, u, :], xn[:, u, :], mv[:, u, 0:1], rstd[:, u:u + 1],
                                                ALU.subtract, ALU.mult).then_inc(s_xnn, 1)
                    v.drain()

            @block.tensor
            def _(pe):
                with pe.Fori(0, GROUPS) as g:
                    for rows, bank, s_in, s_t, s_ev in ((xn, psA, s_xn, s_tA, s_evA), (xnn, psB, s_xnn, s_tB, s_evB)):
                        credit = GT if s_in is s_xn else 0
                        for u in range(GT):
                            pe.wait_ge(s_in, g * GT + u + 1 + credit)
                            pe.wait_ge(s_ev, g * GT + u + (2 if u == 0 else 1))
                            for k in range(KC):
                                last = nc.tensor.transpose(bank[u % 2][:, k * P:(k + 1) * P],
                                                           rows[:, u, k * P:(k + 1) * P], c.ident[:])
                            last.then_inc(s_t, 1)

            @block.scalar
            def _(act):
                act.sem_inc(s_tA, GT)
                act.sem_inc(s_tB, GT)
                act.sem_inc(s_evA, 2)
                act.sem_inc(s_evB, 2)
                act.dma_start(ln_g[:], a["ln_g"]).then_inc(s_outA, 16)
                act.dma_start(ln_b[:], a["ln_b"]).then_inc(s_outB, 16)
                with act.Fori(0, GROUPS) as g:
                    act.wait_ge(s_mv, 2 * g + 1)
                    nc.scalar.activation(std[:], mv[:, :, 1], ACT.Sqrt, bias=c.eps[:]).then_inc(s_std, 1)
                    act.wait_ge(s_mv, 2 * g + 2)
                    nc.scalar.activation(std[:], mv[:, :, 1], ACT.Sqrt, bias=c.eps[:]).then_inc(s_std, 1)
                    act.wait_ge(s_outA, 16 * g + 16)
                    for u in range(GT):
                        act.wait_ge(s_tA, g * GT + u + 1 + GT)
                        nc.scalar.copy(xnT[:, :, u * P:(u + 1) * P],
                                       psA[u % 2][:, 0:D].rearrange("p (k n) -> p k n", k=KC)).then_inc(s_evA, 1)
                    act.wait_ge(s_outB, 16 * g + 16)
                    for u in range(GT):
                        act.wait_ge(s_tB, g * GT + u + 1 + GT)
                        for k in range(KC):
                            last = nc.scalar.activation(xn2T[:, k, u * P:(u + 1) * P], psB[u % 2][:, k * P:(k + 1) * P],
                                                        ACT.Identity, bias=ln_b[:, k:k + 1], scale=ln_g[:, k:k + 1])
                        last.then_inc(s_evB, 1)
                    act.wait_ge(s_evA, g * GT + GT + 2)
                    act.dma_start(c.xnT_d[:, :, ds(g * GN, GN)], xnT[:]).then_inc(s_outA, 16)
                    act.wait_ge(s_evB, g * GT + GT + 2)
                    act.dma_start(c.xn2T_d[:, :, ds(g * GN, GN)], xn2T[:]).then_inc(s_outB, 16)
                act.wait_ge(s_outA, 16 * GROUPS + 16)
                act.wait_ge(s_outB, 16 * GROUPS + 16)


def mix(c, a):
    nc = c.nc
    ctx, sb, ps = c.open()
    with ctx:
        wqkv = sb("wqkv", [P, KC, 3 * D])
        wproj = sb("wproj", [P, KC, D])
        wself = sb("wself", [P, KC, D])
        wg1 = sb("wg1", [P, KC, GATE_H])
        wg2 = sb("wg2", [GATE_H, D])
        bg1 = sb("bg1", [GATE_H, 1])
        bg2 = sb("bg2", [P, KC])
        brow = sb("brow", [1, 2 * D])
        valid = sb("valid", [P, TILES])
        bd = sb("bd", [P, P])
        blk_i = sb("blk_i", [P, P], I32)
        blk_f = sb("blk_f", [P, P])
        own_i = sb("own_i", [P, 1], I32)
        own_f = sb("own_f", [P, 1])
        xa = sb("xa", [P, 2, KC, HB])
        x2a = sb("x2a", [P, 2, KC, HB])
        hg = sb("hg", [GATE_H, N_PAD])
        bmax = sb("bmax", [P, KC, 2 * GROUPS])
        cmax = sb("cmax", [P, KC])
        dg = sb("dg", [P, KC, P])
        cmaxb = sb("cmaxb", [P, D])
        zeros = sb("zeros", [P, 2 * P + 1])
        ks = sb("ks", [P, 2, D])
        ke = sb("ke", [P, 2, D])
        vm = sb("vm", [P, 2, D + 1])
        rz = sb("rz", [P, KC])
        ctxbd = sb("ctxbd", [P, KC, P])
        wqT = sb("wqT", [P, KC, D])
        m_sb = sb("m_sb", [P, KC, D])
        xT = [sb("xT0", [P, KC, 4 * P]), sb("xT1", [P, KC, 3 * P])]
        gate = sb("gate", [P, KC, 4 * P])
        prod = sb("prod", [P, KC, 4 * P])
        xr = sb("xr", [P, GT, D])
        rows = sb("rows", [P, GT, 2 * D])

        s_w, s_bd, s_diag = c.sem("mix_w"), c.sem("mix_bd"), c.sem("mix_diag")
        s_xa = [c.sem(f"mix_xa{i}") for i in range(2)]
        s_k, s_hgp, s_kmax, s_hg = c.sem("mix_k"), c.sem("mix_hgp"), c.sem("mix_kmax"), c.sem("mix_hg")
        s_cm, s_cmb = c.sem("mix_cm"), c.sem("mix_cmb")

        psK = [ps(f"psK{i}", [P, 512]) for i in range(4)]
        psG = [ps(f"psG{i}", [P, 512]) for i in range(2)]
        psM = [ps(f"psM{i}", [P, 512]) for i in range(2)]
        with nc.Block() as block:
            @block.sync
            def _(sp):
                for dst, src in ((wqkv, "wqkv"), (wproj, "wproj"), (wself, "wself"), (wg1, "wg1")):
                    sp.dma_start(dst[:], a[src].rearrange("(k p) n -> p k n", p=P)).then_inc(s_w, 16)
                for dst, src in ((wg2, "wg2"), (bg1, "bg1"), (bg2, "bg2"), (valid, "valid")):
                    sp.dma_start(dst[:], a[src]).then_inc(s_w, 16)
                sp.dma_start(brow[:, 0:D], a["bproj"]).then_inc(s_w, 16)
                sp.dma_start(brow[:, D:2 * D], a["b_gnn"]).then_inc(s_w, 16)
                with sp.Fori(0, GROUPS) as g:
                    for i in range(2):
                        sp.wait_ge(s_hgp, 2 * g + i + 1)
                        at = ds(g * GN + i * HB, HB)
                        sp.dma_start(xa[:, i], c.xnT_d[:, :, at]).then_inc(s_xa[i], 16)
                        sp.dma_start(x2a[:, i], c.xn2T_d[:, :, at]).then_inc(s_xa[i], 16)

            @block.gpsimd
            def _(pool):
                nc.gpsimd.iota(blk_i[:], pattern=[[1, P]], base=0, channel_multiplier=0).then_inc(s_bd, 1)

            @block.tensor
            def _(pe):
                pe.sem_inc(s_hgp, 2)
                pe.wait_ge(s_w, 160)
                with pe.Fori(0, GROUPS) as g:
                    for i in range(2):
                        pe.wait_ge(s_xa[i], 32 * g + 32)
                        pe.wait_ge(s_kmax, 2 * g + i + 1)
                        for h in range(KC):
                            for k in range(KC):
                                last = nc.tensor.matmul(psK[2 * i + h][:, 0:HB], wqkv[:, k, D + h * P:D + (h + 1) * P],
                                                        xa[:, i, k, :], start=(k == 0), stop=(k == KC - 1))
                        last.then_inc(s_k, 1)
                        pe.wait_ge(s_hg, 2 * g + i + 1)
                        for k in range(KC):
                            last = nc.tensor.matmul(psG[i][0:GATE_H, 0:HB], wg1[:, k, :], x2a[:, i, k, :],
                                                    start=(k == 0), stop=(k == KC - 1))
                        last.then_inc(s_hgp, 1)
                pe.wait_ge(s_cm, 1)
                for h in range(KC):
                    last = nc.tensor.matmul(psM[0][:, h * P:(h + 1) * P], c.ones[:], dg[:, h, :], start=True, stop=True)
                last.then_inc(s_cmb, 1)

            @block.vector
            def _(v):
                v.sem_inc(s_kmax, 2)
                nc.vector.memset(zeros[:], 0.0)
                with v.Fori(0, GROUPS) as g:
                    for i in range(2):
                        v.wait_ge(s_k, 2 * g + i + 1)
                        for h in range(KC):
                            last = nc.vector.tensor_reduce(bmax[:, h, ds(2 * g + i, 1)], psK[2 * i + h][:, 0:HB], AX_X, ALU.max)
                        last.then_inc(s_kmax, 1)
                v.drain()
                nc.vector.tensor_reduce(cmax[:], bmax[:], AX_X, ALU.max)
                v.drain()
                for h in range(KC):
                    last = nc.vector.tensor_scalar(dg[:, h, :], c.ident[:], cmax[:, h:h + 1], None, ALU.mult)
                last.then_inc(s_cm, 1)
                v.wait_ge(s_bd, 1)
                nc.vector.tensor_scalar(blk_i[:], blk_i[:], HD.bit_length() - 1, None, ALU.arith_shift_right)
                nc.vector.tensor_scalar(own_i[:], c.iota_col[:], HD.bit_length() - 1, None, ALU.arith_shift_right)
                v.drain()
                nc.vector.tensor_copy(blk_f[:], blk_i[:])
                nc.vector.tensor_copy(own_f[:], own_i[:])
                v.drain()
                nc.vector.tensor_scalar(bd[:], blk_f[:], own_f[:], None, ALU.is_equal)
                v.wait_ge(s_cmb, 1)
                nc.vector.tensor_copy(cmaxb[:], psM[0][:, 0:D])

            @block.scalar
            def _(act):
                act.sem_inc(s_hg, 2)
                with act.Fori(0, GROUPS) as g:
                    for i in range(2):
                        act.wait_ge(s_hgp, 2 * g + i + 3)
                        nc.scalar.activation(hg[:, ds(g * GN + i * HB, HB)], psG[i][0:GATE_H, 0:HB], ACT.Gelu,
                                             bias=bg1[:]).then_inc(s_hg, 1)

        s_xT = [c.sem(f"mix_xT{i}") for i in range(2)]
        s_kv, s_ks, s_vm, s_ke, s_ctx, s_use = (c.sem("mix_kv"), c.sem("mix_ks"), c.sem("mix_vm"), c.sem("mix_ke"),
                                                c.sem("mix_ctx"), c.sem("mix_use"))
        s_wq, s_wqc, s_bdc, s_m = c.sem("mix_wq"), c.sem("mix_wqc"), c.sem("mix_bdc"), c.sem("mix_m")
        HALF = [(0, 4), (4, 3)]

        def tile_of(u):
            i = int(u >= 4)
            return i, (u - HALF[i][0]) * P

        with nc.Block() as block:
            @block.sync
            def _(sp):
                with sp.Fori(0, GROUPS) as g:
                    for i, (u0, n) in enumerate(HALF):
                        sp.wait_ge(s_kv, g * GT + u0 + n)
                        sp.dma_start(xT[i][:], c.xnT_d[:, :, ds(g * GN + u0 * P, n * P)]).then_inc(s_xT[i], 16)

            @block.tensor
            def _(pe):
                pe.sem_inc(s_kv, GT)
                for h in range(KC):
                    nc.tensor.matmul(psM[h][:, 0:D + 1], zeros[:, 0:P], zeros[:, 0:D + 1], start=True, stop=False,
                                     skip_group_check=True)

                def kv(g, u):
                    i, at = tile_of(u)
                    if u in (0, 4):
                        pe.wait_ge(s_xT[i], 16 * g + 16)
                    pe.wait_ge(s_vm, g * GT + u + (2 if u == 0 else 1))
                    for k in range(KC):
                        last = nc.tensor.matmul(psK[u % 2][:, :], xT[i][:, k, at:at + P], wqkv[:, k, D:3 * D],
                                                start=(k == 0), stop=(k == KC - 1))
                    last.then_inc(s_kv, 1)

                def context(g, u):
                    pe.wait_ge(s_ke, g * GT + u + 1)
                    for h in range(KC):
                        last = nc.tensor.matmul(psM[h][:, 0:D + 1], ke[:, u % 2, h * P:(h + 1) * P], vm[:, u % 2, :],
                                                start=False, stop=False, skip_group_check=True)
                    last.then_inc(s_ctx, 1)

                with pe.Fori(0, GROUPS) as g:
                    kv(g, 0)
                    for u in range(GT):
                        if u + 1 < GT:
                            kv(g, u + 1)
                        context(g, u)
                for k in range(KC):
                    for h in range(KC):
                        last = nc.tensor.transpose(psK[2 + h][:, k * P:(k + 1) * P], wqkv[:, k, h * P:(h + 1) * P], c.ident[:])
                last.then_inc(s_wq, 1)
                pe.wait_ge(s_wqc, 1)
                pe.wait_ge(s_bdc, 1)
                for k in range(KC):
                    for h in range(KC):
                        last = nc.tensor.matmul(psG[k][:, h * P:(h + 1) * P], wqT[:, h, k * P:(k + 1) * P], ctxbd[:, h, :],
                                                start=True, stop=True)
                last.then_inc(s_m, 1)

            @block.vector
            def _(v):
                v.sem_inc(s_vm, 2)
                v.sem_inc(s_ctx, 2)
                with v.Fori(0, GROUPS) as g:
                    for u in range(GT):
                        b = u % 2
                        v.wait_ge(s_kv, g * GT + u + 1 + GT)
                        v.wait_ge(s_ctx, g * GT + u + (2 if u == 0 else 1))
                        nc.vector.tensor_tensor(ks[:, b, :], psK[b][:, 0:D], cmaxb[:], ALU.subtract).then_inc(s_ks, 1)
                        one = valid[:, ds(g * GT + u, 1)]
                        nc.vector.tensor_copy(vm[:, b, D:D + 1], one)
                        nc.vector.tensor_scalar(vm[:, b, 0:D], psK[b][:, D:2 * D], one, None, ALU.mult).then_inc(s_vm, 1)
                v.wait_ge(s_ctx, TILES + 2)
                for h in range(KC):
                    nc.vector.reciprocal(rz[:, h:h + 1], psM[h][:, D:D + 1])
                v.drain()
                for h in range(KC):
                    last = nc.vector.scalar_tensor_tensor(ctxbd[:, h, :], psM[h][:, h * P:(h + 1) * P], rz[:, h:h + 1],
                                                          bd[:], ALU.mult, ALU.mult)
                last.then_inc(s_bdc, 1)
                v.wait_ge(s_m, 1)
                for k in range(KC):
                    nc.vector.tensor_copy(m_sb[:, k, :], psG[k][:, 0:D])

            @block.scalar
            def _(act):
                with act.Fori(0, GROUPS) as g:
                    for u in range(GT):
                        act.wait_ge(s_ks, g * GT + u + 1)
                        act.wait_ge(s_vm, g * GT + u + 3)
                        act.wait_ge(s_ctx, g * GT + u + (2 if u == 0 else 1))
                        nc.scalar.activation(ke[:, u % 2, :], ks[:, u % 2, :], ACT.Exp).then_inc(s_ke, 1)
                act.wait_ge(s_wq, 1)
                for h in range(KC):
                    last = nc.scalar.copy(wqT[:, h, :], psK[2 + h][:, 0:D])
                last.then_inc(s_wqc, 1)

        s_xT = [c.sem(f"mixo_xT{i}") for i in range(2)]
        s_xr = [c.sem(f"mixo_xr{i}") for i in range(2)]
        s_at, s_gp, s_gate, s_prod, s_mm = c.sem("mixo_at"), c.sem("mixo_gp"), c.sem("mixo_gate"), c.sem("mixo_prod"), c.sem("mixo_mm")
        s_base, s_self, s_row, s_rowfree = c.sem("mixo_base"), c.sem("mixo_self"), c.sem("mixo_row"), c.sem("mixo_rowfree")
        x_v = a["x"].rearrange("(t p) d -> p t d", p=P)
        rows_v = c.base_d.rearrange("(t p) d -> p t d", p=P)
        with nc.Block() as block:
            @block.sync
            def _(sp):
                with sp.Fori(0, GROUPS) as g:
                    for i, (u0, n) in enumerate(HALF):
                        sp.wait_ge(s_base, g * GT + u0 + n)
                        sp.dma_start(xT[i][:], c.xnT_d[:, :, ds(g * GN + u0 * P, n * P)]).then_inc(s_xT[i], 16)
                        sp.dma_start(xr[:, u0:u0 + n, :], x_v[:, ds(g * GT + u0, n), :]).then_inc(s_xr[i], 16)

            @block.gpsimd
            def _(pool):
                pool.sem_inc(s_rowfree, 2)
                with pool.Fori(0, GROUPS) as g:
                    for i, (u0, n) in enumerate(HALF):
                        pool.wait_ge(s_base, g * GT + u0 + n + GT)
                        pool.wait_ge(s_self, g * GT + u0 + n + 2)
                        pool.dma_start(rows_v[:, ds(g * GT + u0, n), :], rows[:, u0:u0 + n, :]).then_inc(s_row, 16)
                        pool.wait_ge(s_row, 32 * g + 16 * i + 16)
                        pool.sem_inc(s_rowfree, 1)

            @block.tensor
            def _(pe):
                def attention(g, i):
                    n = HALF[i][1] * P
                    pe.wait_ge(s_xT[i], 16 * g + 16)
                    pe.wait_ge(s_prod, 2 * g + i + 1)
                    for h in range(KC):
                        for k in range(KC):
                            last = nc.tensor.matmul(psK[h][:, 0:n], m_sb[:, k, h * P:(h + 1) * P], xT[i][:, k, :],
                                                    start=(k == 0), stop=(k == KC - 1))
                    last.then_inc(s_at, 1)
                    for h in range(KC):
                        last = nc.tensor.matmul(psG[h][:, 0:n], wg2[:, h * P:(h + 1) * P],
                                                hg[:, ds(g * GN + HALF[i][0] * P, n)], start=True, stop=True)
                    last.then_inc(s_gp, 1)

                def project(g, i):
                    u0, n = HALF[i]
                    pe.wait_ge(s_prod, 2 * g + i + 2)
                    for u in range(u0, u0 + n):
                        bank = psM[u % 2]
                        back = 2 if u == 0 else 1
                        pe.wait_ge(s_base, g * GT + u + back + GT - 2)
                        pe.wait_ge(s_self, g * GT + u + back)
                        at = (u - u0) * P
                        nc.tensor.matmul(bank[:, :], c.ones[0:1, :], brow[:], start=True, stop=False, skip_group_check=True)
                        for k in range(KC):
                            nc.tensor.matmul(bank[:, 0:D], prod[:, k, at:at + P], wproj[:, k, :], start=False, stop=False,
                                             skip_group_check=True)
                        for k in range(KC):
                            last = nc.tensor.matmul(bank[:, D:2 * D], xT[i][:, k, at:at + P], wself[:, k, :], start=False,
                                                    stop=(k == KC - 1), skip_group_check=True)
                        last.then_inc(s_mm, 1)

                with pe.Fori(0, GROUPS) as g:
                    for i in range(2):
                        attention(g, i)
                        project(g, i)

            @block.vector
            def _(v):
                v.sem_inc(s_base, GT)
                v.sem_inc(s_prod, 1)
                with v.Fori(0, GROUPS) as g:
                    for i, (u0, n) in enumerate(HALF):
                        v.wait_ge(s_gate, 2 * g + i + 1)
                        for h in range(KC):
                            last = nc.vector.tensor_tensor(prod[:, h, 0:n * P], psK[h][:, 0:n * P], gate[:, h, 0:n * P], ALU.mult)
                        last.then_inc(s_prod, 1)
                        v.wait_ge(s_xr[i], 16 * g + 16)
                        v.wait_ge(s_rowfree, 2 * g + i + 1)
                        for u in range(u0, u0 + n):
                            v.wait_ge(s_mm, g * GT + u + 1)
                            nc.vector.tensor_tensor(rows[:, u, 0:D], psM[u % 2][:, 0:D], xr[:, u, :], ALU.add).then_inc(s_base, 1)

            @block.scalar
            def _(act):
                act.sem_inc(s_self, 2)
                with act.Fori(0, GROUPS) as g:
                    for i, (u0, n) in enumerate(HALF):
                        act.wait_ge(s_gp, 2 * g + i + 1)
                        act.wait_ge(s_at, 2 * g + i + 1)
                        act.wait_ge(s_prod, 2 * g + i + 1)
                        for h in range(KC):
                            last = nc.scalar.activation(gate[:, h, 0:n * P], psG[h][:, 0:n * P], ACT.Sigmoid, bias=bg2[:, h:h + 1])
                        last.then_inc(s_gate, 1)
                        act.wait_ge(s_rowfree, 2 * g + i + 1)
                        for u in range(u0, u0 + n):
                            act.wait_ge(s_base, g * GT + u + 1 + GT)
                            nc.scalar.copy(rows[:, u, D:2 * D], psM[u % 2][:, D:2 * D]).then_inc(s_self, 1)


def half_clean_psum(nc, dst, src, dist):
    s = src.rearrange("p (n two d) -> p n two d", two=2, d=dist)
    t = dst.rearrange("p (n two d) -> p n two d", two=2, d=dist)
    nc.vector.tensor_copy(t[:, :, 1, :], s[:, :, 1, :])
    nc.vector.drain()
    nc.vector.tensor_tensor(t[:, :, 0, :], s[:, :, 0, :], t[:, :, 1, :], ALU.min)
    return nc.vector.tensor_tensor(t[:, :, 1, :], s[:, :, 0, :], t[:, :, 1, :], ALU.max)


def half_clean(nc, dst, src, dist):
    s = src.rearrange("p (n two d) -> p n two d", two=2, d=dist)
    t = dst.rearrange("p (n two d) -> p n two d", two=2, d=dist)
    nc.vector.tensor_tensor(t[:, :, 0, :], s[:, :, 0, :], s[:, :, 1, :], ALU.min)
    return nc.vector.tensor_tensor(t[:, :, 1, :], s[:, :, 0, :], s[:, :, 1, :], ALU.max)


def flip_clean(nc, dst, src, size):
    half = size // 2
    s = src.rearrange("p (n z) -> p n z", z=size)
    t = dst.rearrange("p (n z) -> p n z", z=size)
    nc.vector.tensor_tensor(t[:, :, 0:half], s[:, :, 0:half], s[:, :, half:size][:, :, ::-1], ALU.min)
    return nc.vector.tensor_tensor(t[:, :, half:size], s[:, :, half:size], s[:, :, 0:half][:, :, ::-1], ALU.max)


class Sorter:

    def __init__(self, c, name, sb, ps):
        self.c = c
        self.buf = [sb(f"{name}_keys{i}", [P, LANE]) for i in range(2)]
        self.ps_turned = ps(f"{name}_psT", [P, LANE])
        self.ps_back = ps(f"{name}_psL", [P, LANE])
        self.small = [sb(f"{name}_self{i}", [P, SELF_N // P]) for i in range(2)]
        self.small_t = [sb(f"{name}_selft{i}", [SELF_N // P, P]) for i in range(2)]
        self.s_ready, self.s_turned = c.sem(f"{name}_ready"), c.sem(f"{name}_turned")
        self.turns = 0
        self.served = 0
        self.now = 0

    def step(self, v, op, arg, src=None):
        op(self.c.nc, self.buf[1 - self.now][:], self.buf[self.now][:] if src is None else src, arg)
        self.now = 1 - self.now
        v.drain()

    def turn(self, v):
        self.turns += 1
        v.sem_inc(self.s_ready, 1)
        v.wait_ge(self.s_turned, self.turns)

    def sign(self, v, m):
        cur = self.buf[self.now]
        self.c.nc.vector.tensor_scalar(cur[:], cur[:], self.c.signs[:, m:m + 1], None, ALU.mult)
        v.drain()

    def across(self, v, lanes):
        self.turn(v)
        for i in range(lanes):
            self.step(v, half_clean if i else half_clean_psum, 1 << (lanes - 1 - i), None if i else self.ps_turned[:])
        self.turn(v)
        dist = LANE // 2
        while dist:
            if dist == LANE // 2:
                self.step(v, half_clean_psum, dist, self.ps_back[:])
            else:
                self.step(v, half_clean, dist)
            dist //= 2

    def sort(self, v):
        self.sign(v, 0)
        size = 2
        while size <= LANE:
            self.step(v, flip_clean, size)
            dist = size // 4
            while dist:
                self.step(v, half_clean, dist)
                dist //= 2
            size *= 2
        for m in range(1, 8):
            self.sign(v, m)
            self.across(v, m)

    def merge_selves(self, v):
        nc = self.c.nc
        self.turn(v)
        src, now = self.ps_turned[0:SELF_N // P, 0:P], 0
        dist = P // 2
        while dist:
            (half_clean_psum if dist == P // 2 else half_clean)(nc, self.small_t[now][:], src, dist)
            v.drain()
            src, now = self.small_t[now][:], 1 - now
            dist //= 2
        assert now == 1
        self.turn(v)
        src, now = self.ps_back[:, 0:SELF_N // P], 0
        dist = SELF_N // P // 2
        while dist:
            (half_clean if now or dist < SELF_N // P // 2 else half_clean_psum)(nc, self.small[now][:], src, dist)
            v.drain()
            src, now = self.small[now][:], 1 - now
            dist //= 2
        return self.small[1 - now]

    def serve(self, pe, cur):
        nc = self.c.nc
        for turned, src in ((self.ps_turned, self.buf[cur[0]]), (self.ps_back, self.buf[cur[1]])):
            self.served += 1
            pe.wait_ge(self.s_ready, self.served)
            for b in range(LANE // P):
                last = nc.tensor.transpose(turned[:, b * P:(b + 1) * P], src[:, b * P:(b + 1) * P], self.c.ident[:])
            last.then_inc(self.s_turned, 1)

    def serve_selves(self, pe, first):
        nc = self.c.nc
        n = SELF_N // P
        self.served += 1
        pe.wait_ge(self.s_ready, self.served)
        nc.tensor.transpose(self.ps_turned[0:n, 0:P], first[:], self.c.ident[:]).then_inc(self.s_turned, 1)
        self.served += 1
        pe.wait_ge(self.s_ready, self.served)
        nc.tensor.transpose(self.ps_back[:, 0:n], self.small_t[0][:], self.c.ident[0:n, 0:n]).then_inc(self.s_turned, 1)


def lanes_left(start, m):
    mid = (start + m) % 2
    return mid, (mid + LANE.bit_length() - 1) % 2


IN_LANES = sum(range(1, LANE.bit_length()))


def key_signs(c):
    nc = c.nc
    c.signs = nc.alloc_sbuf_tensor("signs", [P, 8], F32)
    bits = nc.alloc_sbuf_tensor("sign_bits", [P, 8], I32)
    per = nc.alloc_sbuf_tensor("sign_block", [P, 8], F32)
    with nc.Block() as block:
        @block.vector
        def _(v):
            for b in range(8):
                nc.vector.tensor_scalar(bits[:, b:b + 1], c.iota_col[:], b, 1, ALU.logical_shift_right, ALU.bitwise_and)
            v.drain()
            nc.vector.tensor_scalar(per[:], bits[:], -2.0, 1.0, ALU.mult, ALU.add)
            v.drain()
            nc.vector.tensor_copy(c.signs[:, 0:1], per[:, 0:1])
            nc.vector.tensor_tensor(c.signs[:, 1:8], per[:, 0:7], per[:, 1:8], ALU.mult)


def sort_edges(c, a):
    nc = c.nc
    ctx, sb, ps = c.open()
    with ctx:
        src = [sb("edge_src0", [P, LANE], I32), sb("edge_src1", [P, LANE], I32)]
        dst = [sb("edge_dst0", [P, LANE], I32), sb("edge_dst1", [P, LANE], I32)]
        gnn = Sorter(c, "gnnsort", sb, ps)
        gat = Sorter(c, "gatsort", sb, ps)
        selves = sb("selves", [P, SELF_N // P], I32)
        pad = sb("selves_pad", [P, SELF_N // P], I32)
        tail = sb("sort_tail", [P, SELF_N // P])
        first = sb("sentinel", [1, P])
        s_in, s_gnn, s_tail_st, s_tail_ld = c.sem("sort_in"), c.sem("sort_gnn"), c.sem("sort_tail_st"), c.sem("sort_tail_ld")
        s_ids, s_sorted, s_low, s_low_st, s_low_ld, s_merged, s_out = (
            c.sem("sort_ids"), c.sem("sort_sorted"), c.sem("sort_low"), c.sem("sort_low_st"), c.sem("sort_low_ld"),
            c.sem("sort_merged"), c.sem("sort_out"))
        tail_lanes = P - SELF_N // LANE
        end = (IN_LANES + sum(m + LANE.bit_length() - 1 for m in range(1, 8))) % 2

        with nc.Block() as block:
            @block.sync
            def _(sp):
                sp.dma_start(src[0][:], a["src"]).then_inc(s_in, 16)
                sp.dma_start(dst[0][:], a["dst"]).then_inc(s_in, 16)
                sp.dma_start(src[1][:], a["gat_src"]).then_inc(s_in, 16)
                sp.dma_start(dst[1][:], a["gat_dst"]).then_inc(s_in, 16)
                sp.wait_ge(s_sorted, 1)
                sp.dma_start(c.skey_gnn.rearrange("(p j) -> p j", p=P), gnn.buf[end][:]).then_inc(s_out, 16)
                sp.wait_ge(s_sorted, 2)
                sp.dma_start(c.tail_d.rearrange("(p j) -> p j", j=LANE), gat.buf[end][tail_lanes:P, :]).then_inc(s_tail_st, 16)
                sp.wait_ge(s_tail_st, 16)
                sp.dma_start(tail[:], c.tail_d.rearrange("(p j) -> p j", p=P)).then_inc(s_tail_ld, 16)
                sp.wait_ge(s_low, 1)
                sp.dma_start(c.low_d.rearrange("(p j) -> p j", p=P), gat.small[1][:]).then_inc(s_low_st, 16)
                sp.wait_ge(s_low_st, 16)
                sp.dma_start(gat.buf[end][tail_lanes:P, :], c.low_d.rearrange("(p j) -> p j", j=LANE)).then_inc(s_low_ld, 16)
                sp.wait_ge(s_merged, 1)
                sp.dma_start(c.skey_gat[P + SORT_N:P + GAT_N].rearrange("(p j) -> p j", p=P), gat.small[1][:]).then_inc(s_out, 16)
                sp.dma_start(c.skey_gat[0:P].rearrange("(p j) -> p j", p=1), first[:]).then_inc(s_out, 16)
                sp.wait_ge(s_merged, 2)
                sp.dma_start(c.skey_gat[P:P + SORT_N].rearrange("(p j) -> p j", p=P),
                             gat.buf[lanes_left(end, 7)[1]][:]).then_inc(s_out, 16)
                sp.wait_ge(s_out, 64)

            @block.gpsimd
            def _(pool):
                nc.gpsimd.iota(selves[:], pattern=[[-1, SELF_N // P]], base=SELF_N - 1,
                               channel_multiplier=-(SELF_N // P)).then_inc(s_ids, 1)

            @block.vector
            def _(v):
                v.wait_ge(s_in, 64)
                for s, d, srt in ((src[0], dst[0], gnn), (src[1], dst[1], gat)):
                    nc.vector.tensor_scalar(d[:], d[:], SRC_BITS, OFF, ALU.logical_shift_left, ALU.bitwise_or)
                    v.drain()
                    nc.vector.tensor_tensor(srt.buf[0][:].bitcast(I32), s[:], d[:], ALU.bitwise_or)
                    v.drain()
                    srt.sort(v)
                    assert srt.now == end
                    v.sem_inc(s_sorted, 1)
                v.wait_ge(s_ids, 1)
                nc.vector.tensor_scalar(pad[:], selves[:], N_NODES, PAD_DST, ALU.is_ge, ALU.mult)
                v.drain()
                nc.vector.tensor_tensor(selves[:], selves[:], pad[:], ALU.max)
                v.drain()
                nc.vector.tensor_scalar(selves[:], selves[:], SRC_BITS, OFF | SELF, ALU.logical_shift_left, ALU.bitwise_or)
                nc.vector.memset(first[:], SENTINEL)
                v.drain()
                v.wait_ge(s_tail_ld, 16)
                nc.vector.tensor_tensor(gat.small[1][:], tail[:], selves[:].bitcast(F32), ALU.min)
                nc.vector.tensor_tensor(tail[:], tail[:], selves[:].bitcast(F32), ALU.max)
                v.drain()
                v.sem_inc(s_low, 1)
                v.wait_ge(s_low_ld, 16)
                assert gat.merge_selves(v) is gat.small[1]
                v.sem_inc(s_merged, 1)
                gat.across(v, 7)
                v.sem_inc(s_merged, 1)

            @block.tensor
            def _(pe):
                for srt in (gnn, gat):
                    now = IN_LANES % 2
                    for m in range(1, 8):
                        mid, left = lanes_left(now, m)
                        srt.serve(pe, (now, mid))
                        now = left
                gat.serve_selves(pe, tail)
                mid, left = lanes_left(now, 7)
                gat.serve(pe, (now, mid))


def gnn_steps(c, t):
    nc = c.nc
    ctx, sb, ps = c.open()
    with ctx:
        keys = sb("st_keys", [P, LANE], I32)
        last_i = sb("st_last_i", [P, LANE // P], I32)
        ends = sb("st_ends", [P, LANE // P])
        ch_i = sb("st_ch_i", [P, LANE // P], I32)
        ch_f = sb("st_ch_f", [P, LANE // P])
        all_ends = sb("st_all_ends", [P, CH_GNN])
        before = sb("st_before", [P, CH_GNN])
        step_i = sb("st_step_i", [P, STEP_G], I32)
        step_f = sb("st_step_f", [P, STEP_G])
        chunk = sb("st_chunk", [P, STEP_G])
        chunk_i = sb("st_chunk_i", [P, STEP_G], I32)
        tile = sb("st_tile", [P, STEP_G])
        t_rows = sb("st_t_rows", [STEP_G, P], I32)
        row = sb("st_row", [P, STEP_G, P], I32)
        src_i = sb("st_src_i", [P, STEP_G, P], I32)
        src_f = sb("st_src_f", [P, STEP_G, P])
        dst_f = sb("st_dst_f", [P, STEP_G, P])
        ps_src = ps("st_ps_src", [P, 8 * P])
        ps_loc = ps("st_ps_loc", [P, 8 * P])
        ps_tile = ps("st_ps_tile", [P, P])
        s_keys, s_num, s_ends, s_st, s_all = c.sem("st_keys_in"), c.sem("st_num"), c.sem("st_ends"), c.sem("st_st"), c.sem("st_all")
        s_chunk, s_row, s_dec, s_turn, s_t, s_t_st = (c.sem("st_chunk"), c.sem("st_row"), c.sem("st_dec"), c.sem("st_turn"),
                                                      c.sem("st_t"), c.sem("st_t_st"))
        ends_d = c.dram("step_ends_d", [LANE])
        tile_d = c.dram("step_tile_d", [STEP_COLS])
        with nc.Block() as block:
            @block.sync
            def _(sp):
                sp.dma_start(keys[:], c.skey_gnn.rearrange("(p j) -> p j", p=P).bitcast(I32)).then_inc(s_keys, 16)
                sp.wait_ge(s_ends, 1)
                sp.dma_start(ends_d.rearrange("(p q) -> p q", p=P), ends[:]).then_inc(s_st, 16)
                sp.wait_ge(s_st, 16)
                sp.dma_start(all_ends[:], ends_d[0:CH_GNN].rearrange("(o n) -> o n", o=1).to_broadcast([P, CH_GNN])).then_inc(s_all, 16)
                sp.wait_ge(s_t, 1)
                sp.dma_start(tile_d.rearrange("(g p) -> g p", p=P).bitcast(I32), t_rows[:]).then_inc(s_t_st, 16)
                sp.wait_ge(s_t_st, 16)
                sp.dma_start(t.tile[:], tile_d.rearrange("(o n) -> o n", o=1).bitcast(I32)).then_inc(s_t_st, 16)
                sp.wait_ge(s_t_st, 32)

            @block.gpsimd
            def _(pool):
                nc.gpsimd.iota(ch_i[:], pattern=[[1, LANE // P]], base=0, channel_multiplier=LANE // P)
                nc.gpsimd.iota(step_i[:], pattern=[[P, STEP_G]], base=0, channel_multiplier=1).then_inc(s_num, 1)
                pool.wait_ge(s_chunk, 1)
                for g in range(STEP_G):
                    pool.indirect_dma_start(row[:, g, :], None, c.skey_gnn.rearrange("(c e) -> c e", e=P).bitcast(I32),
                                            bass.IndirectOffsetOnAxis(ap=chunk_i[:, g:g + 1], axis=0)).then_inc(s_row, 16)

            @block.vector
            def _(v):
                v.wait_ge(s_num, 1)
                nc.vector.tensor_copy(ch_f[:], ch_i[:])
                nc.vector.tensor_copy(step_f[:], step_i[:])
                v.wait_ge(s_keys, 16)
                nc.vector.tensor_scalar(last_i[:], keys[:].rearrange("p (q e) -> p q e", e=P)[:, :, P - 1], SRC_BITS + 7,
                                        DST_MASK >> 7, ALU.logical_shift_right, ALU.bitwise_and)
                v.drain()
                nc.vector.tensor_copy(ends[:], last_i[:])
                v.drain()
                nc.vector.scalar_tensor_tensor(ends[:], ends[:], float(TILES - 1), ch_f[:], ALU.min, ALU.add).then_inc(s_ends, 1)
                v.wait_ge(s_all, 16)
                for g in range(STEP_G):
                    nc.vector.tensor_scalar(before[:], all_ends[:], step_f[:, g:g + 1], None, ALU.is_lt, ALU.add,
                                            accum_out=chunk[:, g:g + 1])
                    v.drain()
                nc.vector.tensor_copy(chunk_i[:], chunk[:]).then_inc(s_chunk, 1)
                nc.vector.tensor_tensor(tile[:], step_f[:], chunk[:], ALU.subtract)
                v.drain()
                nc.vector.tensor_scalar(tile[:], tile[:], float(TILES - 1), None, ALU.min)
                v.drain()
                v.wait_ge(s_row, 16 * STEP_G)
                nc.vector.tensor_scalar(src_i[:], row[:], SELF, None, ALU.bitwise_and)
                nc.vector.tensor_scalar(row[:], row[:], SRC_BITS, DST_MASK, ALU.logical_shift_right, ALU.bitwise_and)
                v.drain()
                nc.vector.tensor_scalar(src_f[:], src_i[:], float(N_NODES - 1), None, ALU.min)
                nc.vector.tensor_copy(dst_f[:], row[:])
                v.drain()
                nc.vector.scalar_tensor_tensor(dst_f[:], bcast(tile[:], 2, P), -float(P), dst_f[:], ALU.mult, ALU.add).then_inc(s_dec, 1)
                v.wait_ge(s_turn, 1)
                nc.vector.tensor_copy(t.idx[:], ps_src[:, 0:STEP_COLS])
                nc.vector.tensor_copy(t.loc[:], ps_loc[:, 0:STEP_COLS])
                nc.vector.tensor_copy(t_rows[:], ps_tile[0:STEP_G, :]).then_inc(s_t, 1)

            @block.tensor
            def _(pe):
                pe.wait_ge(s_dec, 1)
                for g in range(STEP_G):
                    nc.tensor.transpose(ps_src[:, g * P:(g + 1) * P], src_f[:, g, :], c.ident[:])
                    nc.tensor.transpose(ps_loc[:, g * P:(g + 1) * P], dst_f[:, g, :], c.ident[:])
                nc.tensor.transpose(ps_tile[0:STEP_G, :], tile[:], c.ident[:]).then_inc(s_turn, 1)


class StepTables:
    def __init__(self, sb):
        self.idx = sb("step_src", [P, STEP_COLS], I32)
        self.loc = sb("step_loc", [P, STEP_COLS])
        self.tile = sb("step_tile", [1, STEP_COLS], I32)


def gnn_sum(c, t, acc):
    nc = c.nc
    ROWW = D + 1
    BANKS = 4
    ctx, sb, ps = c.open()
    with ctx:
        msg = sb("gs_msg", [P, SBLK, ROWW])
        hot = sb("gs_hot", [P, 2, SHALF, P])
        ixs = sb("gs_ixs", [P, 2, SHALF], I32)
        tick = sb("gs_tick", [P, 2])
        bank = [ps(f"gs_ps{i}", [P, 512]) for i in range(BANKS)]
        s_ix, s_hot, s_mm, s_acc, s_init = c.sem("gs_ix"), c.sem("gs_hot"), c.sem("gs_mm"), c.sem("gs_acc"), c.sem("gs_init")
        s_tick = c.sem("gs_tick_done")
        s_g = [c.sem(f"gs_rows{h}") for h in range(2)]
        with nc.Block() as block:
            @block.scalar
            def _(act):
                act.sem_inc(s_tick, 2)
                with act.Fori(0, S_ITERS) as b:
                    for h in range(2):
                        act.wait_ge(s_tick, 2 * b + h + 1)
                        act.wait_ge(s_mm, b * SBLK + (h + 1) * SHALF)
                        nc.scalar.copy(ixs[:, h, :], t.idx[:, ds(b * SBLK + h * SHALF, SHALF)]).then_inc(s_ix, 1)

            @block.gpsimd
            def _(pool):
                nc.gpsimd.memset(msg[:, :, D:ROWW], 1.0)
                nc.gpsimd.memset(acc[:], 0.0).then_inc(s_init, 1)
                pool.drain()
                with pool.Fori(0, S_ITERS) as b:
                    for h in range(2):
                        pool.wait_ge(s_ix, 2 * b + h + 1)
                        nc.gpsimd.tensor_tensor(tick[:, h:h + 1], c.eps[:], c.eps[:], ALU.add).then_inc(s_tick, 1)
                        for u in range(SHALF):
                            pool.indirect_dma_start(msg[:, h * SHALF + u, 0:D], None, c.xn_tab,
                                                    bass.IndirectOffsetOnAxis(ap=ixs[:, h, u:u + 1], axis=0)
                                                    ).then_inc(s_g[h], 16)

            @block.vector
            def _(v):
                v.sem_inc(s_acc, BANKS)

                def one_hots(h, at):
                    nc.vector.tensor_tensor(hot[:, h], bcast(c.iota_row[:], 1, SHALF), bcast(t.loc[:, ds(at, SHALF)], 2, P),
                                            ALU.is_equal).then_inc(s_hot, 1)

                v.wait_ge(s_init, 1)
                one_hots(0, 0)
                with v.Fori(0, S_ITERS) as b:
                    _, tiles = nc.values_load_multi_w_load_instructions(
                        t.tile[0:1, ds(b * SBLK, SBLK)], engines=[DVE_ENGINE], min_val=0, max_val=TILES - 1,
                        skip_runtime_bounds_check_because="at most the last tile by a min")
                    for u in range(SBLK):
                        if u % SHALF == 0:
                            one_hots(1 - u // SHALF, b * SBLK + u + SHALF)
                        v.drain()
                        v.wait_ge(s_mm, b * SBLK + u + 1 + SBLK)
                        own = acc[:, ds(tiles[u] * ROWW, ROWW)]
                        nc.vector.tensor_tensor(own, own, bank[u % BANKS][:, 0:ROWW], ALU.add).then_inc(s_acc, 1)

            @block.tensor
            def _(pe):
                pe.sem_inc(s_mm, SBLK)
                pe.wait_ge(s_init, 1)
                with pe.Fori(0, S_ITERS) as b:
                    for u in range(SBLK):
                        if u % SHALF == 0:
                            pe.wait_ge(s_hot, 2 * b + u // SHALF + 1)
                            pe.wait_ge(s_g[u // SHALF], 16 * SHALF * b + 16 * SHALF)
                        pe.wait_ge(s_acc, b * SBLK + u + 1)
                        nc.tensor.matmul(bank[u % BANKS][:, 0:ROWW], hot[:, u // SHALF, u % SHALF, :], msg[:, u, :],
                                         start=True, stop=True).then_inc(s_mm, 1)




def gnn_out(c, a, acc):
    nc = c.nc
    ROWW = D + 1
    ctx, sb, ps = c.open()
    with ctx:
        wneigh = sb("go_wneigh", [P, KC, D])
        wg = sb("go_wg", [P, KC, ROW])
        att = sb("go_att", [P, 2, HE])
        prod = sb("go_att_prod", [P, HE])
        rdeg = sb("go_rdeg", [P, TILES])
        hn = sb("go_hn", [P, 2, D])
        hnT = sb("go_hnT", [P, 2, KC, P])
        base = sb("go_base", [P, GT, 2 * D])
        z = sb("go_z", [P, 2, D])
        x2 = sb("go_x2", [P, GT, D])
        y = sb("go_y", [P, GT, D])
        yT = sb("go_yT", [P, KC, GN])
        hx = sb("go_hx", [P, GT, ROW])
        stats = sb("go_stats", [P, GT, 6])
        mv = sb("go_mv", [P, GT, 2])
        std = sb("go_std", [P, GT])
        rstd = sb("go_rstd", [P, GT])
        psT = [ps(f"go_psT{i}", [P, 512]) for i in range(2)]
        psZ = [ps(f"go_psZ{i}", [P, 512]) for i in range(2)]
        psY = [ps(f"go_psY{i}", [P, 512]) for i in range(2)]
        psH = [ps(f"go_psH{i}", [P, 512]) for i in range(2)]
        s_w, s_wg, s_base, s_hn, s_hnT, s_hnc, s_z, s_x2 = (c.sem("go_" + n) for n in (
            "w", "wg", "base_in", "hn", "hnT", "hnc", "z", "x2"))
        s_mv, s_std, s_y, s_yT, s_yc, s_hx, s_hxc, s_read = (c.sem("go_" + n) for n in (
            "mv", "std", "y", "yT", "yc", "hx", "hxc", "read"))
        s_x2st, s_x2free, s_yst, s_yfree, s_hxst, s_hxfree = (c.sem("go_" + n) for n in (
            "x2st", "x2free", "yst", "yfree", "hxst", "hxfree"))
        base_v = c.base_d.rearrange("(t p) d -> p t d", p=P)
        x2_v = c.x2_d.rearrange("(t p) d -> p t d", p=P)
        hx_v = c.hx_d.rearrange("(t p) d -> p t d", p=P)
        acc_v = acc[:].rearrange("p (t d) -> p t d", t=TILES)

        def slot(g, u):
            return g * GT + u + (2 if u == 0 else 1)

        with nc.Block() as block:
            @block.sync
            def _(sp):
                sp.dma_start(wneigh[:], a["wneigh"].rearrange("(k p) n -> p k n", p=P)).then_inc(s_w, 16)
                sp.dma_start(wg[:, :, 0:HE], a["w_gat"].rearrange("(k p) n -> p k n", p=P)).then_inc(s_w, 16)
                sp.dma_start(att[:, 0, :], a["att_src"].to_broadcast([P, HE])).then_inc(s_w, 16)
                sp.dma_start(att[:, 1, :], a["att_dst"].to_broadcast([P, HE])).then_inc(s_w, 16)
                sp.sem_inc(s_x2free, 1)
                sp.sem_inc(s_read, 1)
                with sp.Fori(0, GROUPS) as g:
                    sp.wait_ge(s_read, g + 1)
                    sp.dma_start(base[:], base_v[:, ds(g * GT, GT), :]).then_inc(s_base, 16)
                    sp.wait_ge(s_x2, g * GT + GT + 2)
                    sp.dma_start(x2_v[:, ds(g * GT, GT), :], x2[:]).then_inc(s_x2st, 16)
                    sp.wait_ge(s_x2st, 16 * g + 16)
                    sp.sem_inc(s_x2free, 1)

            @block.gpsimd
            def _(pool):
                pool.sem_inc(s_yfree, 1)
                pool.sem_inc(s_hxfree, 1)
                with pool.Fori(0, GROUPS) as g:
                    pool.wait_ge(s_yc, g * GT + GT + 2)
                    pool.dma_start(c.x2nT_d[:, :, ds(g * GN, GN)], yT[:]).then_inc(s_yst, 16)
                    pool.wait_ge(s_hxc, g * GT + GT + 2)
                    pool.dma_start(hx_v[:, ds(g * GT, GT), :], hx[:]).then_inc(s_hxst, 16)
                    pool.wait_ge(s_yst, 16 * g + 16)
                    pool.sem_inc(s_yfree, 1)
                    pool.wait_ge(s_hxst, 16 * g + 16)
                    pool.sem_inc(s_hxfree, 1)

            @block.vector
            def _(v):
                v.sem_inc(s_x2, 2)
                nc.vector.tensor_scalar(rdeg[:], acc_v[:, :, D], 1.0, None, ALU.max)
                v.drain()
                nc.vector.reciprocal(rdeg[:], rdeg[:])
                v.wait_ge(s_w, 64)
                for i in range(2):
                    for k in range(KC):
                        nc.vector.tensor_tensor(prod[:], wg[:, k, 0:HE], att[:, i, :], ALU.mult)
                        v.drain()
                        last = nc.vector.tensor_reduce(wg[:, k, HE + i * HEADS:HE + (i + 1) * HEADS],
                                                       prod[:].rearrange("p (h e) -> p h e", h=HEADS), AX_X, ALU.add)
                        v.drain()
                v.sem_inc(s_wg, 1)

                def mean(g, u):
                    v.wait_ge(s_hnT, slot(g, u))
                    at = g * GT + u
                    nc.vector.tensor_scalar(hn[:, u % 2, :], acc[:, ds(at * ROWW, D)], rdeg[:, ds(at, 1)], None,
                                            ALU.mult).then_inc(s_hn, 1)

                with v.Fori(0, GROUPS) as g:
                    v.wait_ge(s_base, 16 * g + 16)
                    v.wait_ge(s_x2free, g + 1)
                    mean(g, 0)
                    for u in range(GT):
                        if u + 1 < GT:
                            mean(g, u + 1)
                        v.wait_ge(s_z, g * GT + u + 3)
                        nc.vector.tensor_tensor(z[:, u % 2, :], psZ[u % 2][:, 0:D], base[:, u, D:2 * D], ALU.add)
                        v.drain()
                        nc.vector.scalar_tensor_tensor(x2[:, u, :], z[:, u % 2, :], 0.0, base[:, u, 0:D], ALU.max,
                                                       ALU.add).then_inc(s_x2, 1)
                        v.drain()
                        nc.vector.bn_stats(stats[:, u, :], x2[:, u, :])
                    v.drain()
                    v.sem_inc(s_read, 1)
                    for u in range(GT):
                        last = nc.vector.bn_aggr(mv[:, u, :], stats[:, u, :])
                    last.then_inc(s_mv, 1)
                    v.wait_ge(s_std, g + 1)
                    nc.vector.reciprocal(rstd[:], std[:])
                    v.drain()
                    v.wait_ge(s_yT, g * GT + 2)
                    for u in range(GT):
                        nc.vector.tensor_scalar(y[:, u, :], x2[:, u, :], mv[:, u, 0:1], rstd[:, u:u + 1],
                                                ALU.subtract, ALU.mult).then_inc(s_y, 1)
                    v.drain()

            @block.scalar
            def _(act):
                act.sem_inc(s_hnc, 2)
                act.sem_inc(s_yc, 2)
                act.sem_inc(s_hxc, 2)
                with act.Fori(0, GROUPS) as g:
                    for u in range(GT):
                        act.wait_ge(s_hnT, g * GT + u + 3)
                        act.wait_ge(s_z, slot(g, u))
                        nc.scalar.copy(hnT[:, u % 2], psT[u % 2][:, 0:D].rearrange("p (k n) -> p k n", k=KC)).then_inc(s_hnc, 1)
                    act.wait_ge(s_mv, g + 1)
                    nc.scalar.activation(std[:], mv[:, :, 1], ACT.Sqrt, bias=c.eps[:]).then_inc(s_std, 1)
                    act.wait_ge(s_yfree, g + 1)
                    act.wait_ge(s_hxfree, g + 1)
                    for u in range(GT):
                        act.wait_ge(s_yT, g * GT + u + 3)
                        nc.scalar.copy(yT[:, :, u * P:(u + 1) * P],
                                       psY[u % 2][:, 0:D].rearrange("p (k n) -> p k n", k=KC)).then_inc(s_yc, 1)
                        if u:
                            act.wait_ge(s_hx, g * GT + u)
                            nc.scalar.copy(hx[:, u - 1, :], psH[(u - 1) % 2][:, 0:ROW]).then_inc(s_hxc, 1)
                    act.wait_ge(s_hx, g * GT + GT)
                    nc.scalar.copy(hx[:, GT - 1, :], psH[(GT - 1) % 2][:, 0:ROW]).then_inc(s_hxc, 1)

            @block.tensor
            def _(pe):
                pe.sem_inc(s_hnT, 2)
                pe.sem_inc(s_z, 2)
                pe.sem_inc(s_yT, 2)
                pe.wait_ge(s_wg, 1)

                def turn_mean(g, u):
                    pe.wait_ge(s_hn, g * GT + u + 1)
                    pe.wait_ge(s_hnc, slot(g, u))
                    for k in range(KC):
                        last = nc.tensor.transpose(psT[u % 2][:, k * P:(k + 1) * P], hn[:, u % 2, k * P:(k + 1) * P], c.ident[:])
                    last.then_inc(s_hnT, 1)

                def rows_of(g, u):
                    pe.wait_ge(s_yc, g * GT + u + 3)
                    pe.wait_ge(s_hxc, slot(g, u))
                    for k in range(KC):
                        last = nc.tensor.matmul(psH[u % 2][:, 0:ROW], yT[:, k, u * P:(u + 1) * P], wg[:, k, :],
                                                start=(k == 0), stop=(k == KC - 1))
                    last.then_inc(s_hx, 1)

                with pe.Fori(0, GROUPS) as g:
                    turn_mean(g, 0)
                    for u in range(GT):
                        if u + 1 < GT:
                            turn_mean(g, u + 1)
                        pe.wait_ge(s_hnc, g * GT + u + 3)
                        pe.wait_ge(s_x2, slot(g, u))
                        for k in range(KC):
                            last = nc.tensor.matmul(psZ[u % 2][:, 0:D], hnT[:, u % 2, k, :], wneigh[:, k, :],
                                                    start=(k == 0), stop=(k == KC - 1))
                        last.then_inc(s_z, 1)
                    for u in range(GT):
                        pe.wait_ge(s_y, g * GT + u + 1)
                        pe.wait_ge(s_yc, slot(g, u))
                        for k in range(KC):
                            last = nc.tensor.transpose(psY[u % 2][:, k * P:(k + 1) * P], y[:, u, k * P:(k + 1) * P], c.ident[:])
                        last.then_inc(s_yT, 1)
                        if u:
                            rows_of(g, u - 1)
                    rows_of(g, GT - 1)


def gat_ends(c, endpos):
    nc = c.nc
    ctx, sb, ps = c.open()
    with ctx:
        keys = sb("ge_keys", [FENCE_P, FENCES // FENCE_P, P], I32)
        first_i = sb("ge_first_i", [FENCE_P, FENCES // FENCE_P], I32)
        first_f = sb("ge_first_f", [FENCE_P, FENCES // FENCE_P])
        firsts = sb("ge_firsts", [P, FENCES])
        reached = sb("ge_reached", [P, FENCES])
        node_i = sb("ge_node_i", [P, TILES], I32)
        node_f = sb("ge_node_f", [P, TILES])
        chunk = sb("ge_chunk", [P, TILES])
        chunk_i = sb("ge_chunk_i", [P, TILES], I32)
        rows = sb("ge_rows", [P, TILES, P])
        upto = sb("ge_upto", [P, TILES, P])
        place = sb("ge_place", [P, TILES])
        s_first, s_node, s_dec, s_dec_st, s_all, s_chunk, s_row = (c.sem("ge_" + n) for n in (
            "first", "node", "dec", "dec_st", "all", "chunk", "row"))
        first_d = c.dram("ge_first_d", [FENCES])
        chunks_v = c.skey_gat[P:P + GAT_N].rearrange("(c e) -> c e", e=P)
        with nc.Block() as block:
            @block.sync
            def _(sp):
                sp.dma_start(keys[:], chunks_v.rearrange("(p w) e -> p w e", p=FENCE_P).bitcast(I32)).then_inc(s_first, 16)
                sp.wait_ge(s_dec, 1)
                sp.dma_start(first_d.rearrange("(p w) -> p w", p=FENCE_P), first_f[:]).then_inc(s_dec_st, 16)
                sp.wait_ge(s_dec_st, 16)
                sp.dma_start(firsts[:], first_d.rearrange("(o n) -> o n", o=1).to_broadcast([P, FENCES])).then_inc(s_all, 16)

            @block.gpsimd
            def _(pool):
                nc.gpsimd.iota(node_i[:], pattern=[[P, TILES]], base=0, channel_multiplier=1).then_inc(s_node, 1)
                pool.wait_ge(s_chunk, 1)
                for t in range(TILES):
                    pool.indirect_dma_start(rows[:, t, :], None, c.skey_gat.rearrange("(c e) -> c e", e=P),
                                            bass.IndirectOffsetOnAxis(ap=chunk_i[:, t:t + 1], axis=0)).then_inc(s_row, 16)

            @block.vector
            def _(v):
                v.wait_ge(s_node, 1)
                nc.vector.tensor_copy(node_f[:], node_i[:])
                v.wait_ge(s_first, 16)
                nc.vector.tensor_scalar(first_i[:], keys[:, :, 0], SRC_BITS, DST_MASK, ALU.logical_shift_right, ALU.bitwise_and)
                v.drain()
                nc.vector.tensor_copy(first_f[:], first_i[:]).then_inc(s_dec, 1)
                v.wait_ge(s_all, 16)
                for t in range(TILES):
                    nc.vector.tensor_scalar(reached[:], firsts[:], node_f[:, t:t + 1], None, ALU.is_le, ALU.add,
                                            accum_out=chunk[:, t:t + 1])
                    v.drain()
                nc.vector.tensor_scalar(chunk[:], chunk[:], -1.0, None, ALU.add)
                nc.vector.tensor_scalar(node_i[:], node_i[:], SRC_BITS, OFF | SELF, ALU.logical_shift_left, ALU.bitwise_or)
                v.drain()
                nc.vector.tensor_scalar(chunk_i[:], chunk[:], 1.0, None, ALU.add).then_inc(s_chunk, 1)
                v.wait_ge(s_row, 16 * TILES)
                nc.vector.tensor_tensor(upto[:], rows[:], bcast(node_i[:].bitcast(F32), 2, P), ALU.is_le)
                v.drain()
                nc.vector.tensor_reduce(place[:], upto[:], AX_X, ALU.add)
                v.drain()
                nc.vector.scalar_tensor_tensor(place[:], chunk[:], float(P), place[:], ALU.mult, ALU.add)
                v.drain()
                nc.vector.tensor_scalar(endpos[:], place[:], -1.0, None, ALU.add)


def gat_gather_experts(c, a, G):
    nc = c.nc
    FB, YB = 4, 4
    ctx, sb, ps = c.open()
    with ctx:
        keys = sb("gg_keys", [P, W], I32)
        num_i = sb("gg_num_i", [P, W], I32)
        src_f = sb("gg_src_f", [P, W])
        dst_f = sb("gg_dst_f", [P, W])
        self_f = sb("gg_self_f", [P, W])
        idx = sb("gg_idx", [P, W + SBLK], I32)
        ring = sb("gg_ring", [P, 2, SHALF, ROW])
        ixs = sb("gg_ixs", [P, 2, SHALF], I32)
        tick = sb("gg_tick", [P, 2])
        s_keys, s_ix, s_tick = c.sem("gg_keys_in"), c.sem("gg_ix"), c.sem("gg_tick_done")
        s_g = [c.sem(f"gg_rows{h}") for h in range(2)]

        w1 = sb("ex_w1", [P, EXPERTS, KC, HID])
        w2 = sb("ex_w2", [P, EXPERTS, HC, D])
        b1 = sb("ex_b1", [P, EXPERTS * HC])
        b2 = sb("ex_b2", [1, EXPERTS * D])
        yT = sb("ex_yT", [P, KC, GN])
        hh = sb("ex_hh", [P, HC, 2, GN // 2])
        yo = sb("ex_yo", [P, GT, D])
        psF = [ps(f"ex_psF{i}", [P, 512]) for i in range(FB)]
        psY = [ps(f"ex_psY{i}", [P, 512]) for i in range(YB)]
        s_w, s_yT, s_f, s_ge, s_s, s_yc, s_yst, s_yfree = (c.sem("ex_" + n) for n in (
            "w", "yT", "f", "ge", "s", "yc", "yst", "yfree"))
        NF, NS = 2 * HC, GT
        with nc.Block() as block:
            @block.sync
            def _(sp):
                sp.dma_start(keys[:], c.skey_gat[P:P + GAT_N].rearrange("(p w) -> p w", p=P).bitcast(I32)).then_inc(s_keys, 16)
                for e in range(EXPERTS):
                    sp.dma_start(w1[:, e], a["w1"][e].rearrange("(k p) n -> p k n", p=P)).then_inc(s_w, 16)
                    sp.dma_start(w2[:, e], a["w2"][e].rearrange("(k p) n -> p k n", p=P)).then_inc(s_w, 16)
                sp.dma_start(b1[:], a["b1"]).then_inc(s_w, 16)
                sp.dma_start(b2[:], a["b2"]).then_inc(s_w, 16)
                sp.sem_inc(s_yfree, 1)
                with sp.Fori(0, GROUPS) as g:
                    sp.wait_ge(s_f, g * EXPERTS * NF + 1)
                    sp.dma_start(yT[:], c.x2nT_d[:, :, ds(g * GN, GN)]).then_inc(s_yT, 16)
                    for e in range(EXPERTS):
                        n = g * EXPERTS + e
                        sp.wait_ge(s_yc, n * NS + NS + YB)
                        sp.dma_start(c.y_d[e].rearrange("(t p) d -> p t d", p=P)[:, ds(g * GT, GT), :], yo[:]).then_inc(s_yst, 16)
                        sp.wait_ge(s_yst, 16 * n + 16)
                        sp.sem_inc(s_yfree, 1)

            @block.gpsimd
            def _(pool):
                with pool.Fori(0, G_ITERS) as b:
                    for h in range(2):
                        pool.wait_ge(s_ix, 2 * b + h + 1)
                        nc.gpsimd.tensor_tensor(tick[:, h:h + 1], c.eps[:], c.eps[:], ALU.add).then_inc(s_tick, 1)
                        for u in range(SHALF):
                            pool.indirect_dma_start(ring[:, h, u, :], None, c.hx_d,
                                                    bass.IndirectOffsetOnAxis(ap=ixs[:, h, u:u + 1], axis=0)).then_inc(s_g[h], 16)

            @block.vector
            def _(v):
                nc.vector.memset(idx[:, W:W + SBLK], 0)
                v.wait_ge(s_keys, 16)
                nc.vector.tensor_scalar(num_i[:], keys[:], SELF, None, ALU.bitwise_and)
                nc.vector.tensor_scalar(keys[:], keys[:], SRC_BITS, DST_MASK, ALU.logical_shift_right, ALU.bitwise_and)
                v.drain()
                nc.vector.tensor_copy(src_f[:], num_i[:])
                nc.vector.tensor_copy(dst_f[:], keys[:])
                v.drain()
                nc.vector.tensor_scalar(self_f[:], src_f[:], float(SELF), None, ALU.is_equal)
                v.drain()
                nc.vector.tensor_tensor(dst_f[:], dst_f[:], src_f[:], ALU.subtract)
                v.drain()
                nc.vector.tensor_tensor(dst_f[:], dst_f[:], self_f[:], ALU.mult)
                v.drain()
                nc.vector.tensor_tensor(src_f[:], src_f[:], dst_f[:], ALU.add)
                v.drain()
                nc.vector.tensor_scalar(idx[:, 0:W], src_f[:], float(N_NODES - 1), None, ALU.min)
                v.drain()
                for h in range(2):
                    nc.vector.tensor_copy(ixs[:, h, :], idx[:, h * SHALF:(h + 1) * SHALF]).then_inc(s_ix, 1)
                with v.Fori(0, G_ITERS) as b:
                    for h in range(2):
                        v.wait_ge(s_tick, 2 * b + h + 1)
                        v.wait_ge(s_g[h], 16 * SHALF * b + 16 * SHALF)
                        nc.vector.tensor_copy(G[:, ds(b * SBLK + h * SHALF, SHALF), :], ring[:, h])
                        nc.vector.tensor_copy(ixs[:, h, :], idx[:, ds(b * SBLK + h * SHALF + SBLK, SHALF)]).then_inc(s_ix, 1)

            @block.tensor
            def _(pe):
                pe.sem_inc(s_s, 1)
                pe.sem_inc(s_f, 1)
                pe.wait_ge(s_w, 160)

                def first(g, e):
                    for i in range(NF):
                        n = (g * EXPERTS + e) * NF + i
                        pe.wait_ge(s_ge, n + 1)
                        for k in range(KC):
                            last = nc.tensor.matmul(psF[i % FB][:, 0:HB], w1[:, e, k, (i // 2) * P:(i // 2 + 1) * P],
                                                    yT[:, k, (i % 2) * HB:(i % 2 + 1) * HB], start=(k == 0), stop=(k == KC - 1))
                        last.then_inc(s_f, 1)

                def second(g, e):
                    pe.wait_ge(s_ge, (g * EXPERTS + e) * NF + NF + FB)
                    for u in range(NS):
                        n = (g * EXPERTS + e) * NS + u
                        bank = psY[(e * NS + u) % YB]
                        pe.wait_ge(s_yc, n + 1)
                        nc.tensor.matmul(bank[:, 0:D], c.ones[0:1, :], b2[:, e * D:(e + 1) * D], start=True, stop=False)
                        for k in range(HC):
                            last = nc.tensor.matmul(bank[:, 0:D], hh[:, k].rearrange("p a b -> p (a b)")[:, u * P:(u + 1) * P],
                                                    w2[:, e, k, :], start=False, stop=(k == HC - 1))
                        last.then_inc(s_s, 1)

                with pe.Fori(0, GROUPS) as g:
                    pe.wait_ge(s_yT, 16 * g + 16)
                    for e in range(EXPERTS):
                        first(g, e)
                        second(g, e)

            @block.scalar
            def _(act):
                act.sem_inc(s_ge, FB)
                act.sem_inc(s_yc, YB)
                act.wait_ge(s_w, 160)
                with act.Fori(0, GROUPS) as g:
                    for e in range(EXPERTS):
                        n = g * EXPERTS + e
                        act.wait_ge(s_s, n * NS + 1)
                        for i in range(NF):
                            act.wait_ge(s_f, n * NF + i + 2)
                            nc.scalar.activation(hh[:, i // 2, i % 2, :], psF[i % FB][:, 0:HB], ACT.Gelu,
                                                 bias=b1[:, e * HC + i // 2:e * HC + i // 2 + 1]).then_inc(s_ge, 1)
                        act.wait_ge(s_yfree, n + 1)
                        for u in range(NS):
                            act.wait_ge(s_s, n * NS + u + 2)
                            nc.scalar.copy(yo[:, u, :], psY[(e * NS + u) % YB][:, 0:D]).then_inc(s_yc, 1)


def gat_softmax(c, a, G, endpos, gates):
    nc = c.nc
    NV = HE + HEADS
    ctx, sb, ps = c.open()
    with ctx:
        start = sb("gs2_start", [P, W])
        keep = sb("gs2_keep", [P, W])
        other = sb("gs2_other", [P, W])
        selfm = sb("gs2_self", [P, W])
        pen = sb("gs2_pen", [P, W])
        keys = pen[:].bitcast(I32)
        top = sb("gs2_top", [P, W, HEADS])
        dlog = sb("gs2_dlog", [P, W, HEADS])
        lanes = sb("gs2_lanes", [P, 2, NV])
        turned = sb("gs2_turned", [NV, 2, P])
        chain = sb("gs2_chain", [NV, P + 2])
        carry = sb("gs2_carry", [P, NV])
        num = sb("gs2_num", [P, TILES, ROW])
        den = sb("gs2_den", [P, TILES, HEADS])
        par = sb("gs2_par", [P, 3, HE])
        dev = sb("gs2_dev", [P, TILES, HE])
        sq = sb("gs2_sq", [P, TILES, HE])
        mu = sb("gs2_mu", [P, TILES])
        var = sb("gs2_var", [P, TILES])
        score = sb("gs2_score", [P, TILES, EXPERTS])
        wins = sb("gs2_wins", [P, TILES])
        rank = sb("gs2_rank", [P, TILES, EXPERTS])
        ps_in = ps("gs2_ps_in", [P, 512])
        ps_out = ps("gs2_ps_out", [P, 512])
        s_in, s_lanes, s_turned, s_chain, s_back, s_exp_in, s_exp, s_done, s_st, s_num, s_std = (c.sem("gs2_" + n) for n in (
            "in", "lanes", "turned", "chain", "back", "exp_in", "exp", "done", "st", "num", "std"))
        prev = top[:].rearrange("p w h -> p (w h)")[:, 0:W].bitcast(I32)
        zero = dlog[:].rearrange("p w h -> p (w h)")[:, 0:W]
        widths = (HEADS, 2 * HEADS, NV)

        with nc.Block() as block:
            @block.sync
            def _(sp):
                sp.dma_start(keys, c.skey_gat[P:P + GAT_N].rearrange("(p w) -> p w", p=P).bitcast(I32)).then_inc(s_in, 16)
                sp.dma_start(prev, c.skey_gat[P - 1:P + GAT_N - 1].rearrange("(p w) -> p w", p=P).bitcast(I32)).then_inc(s_in, 16)
                for i, name in enumerate(("b_gat", "gamma", "beta")):
                    sp.dma_start(par[:, i, :], a[name].to_broadcast([P, HE])).then_inc(s_in, 16)
                sp.wait_ge(s_done, 1)
                sp.dma_start(c.sums_d.rearrange("(p w) r -> p w r", p=P), G[:]).then_inc(s_st, 16)
                sp.wait_ge(s_st, 16)

            @block.gpsimd
            def _(pool):
                pool.wait_ge(s_st, 16)
                for t in range(TILES):
                    pool.indirect_dma_start(num[:, t, :], None, c.sums_d,
                                            bass.IndirectOffsetOnAxis(ap=endpos[:, t:t + 1], axis=0)).then_inc(s_num, 16)

            @block.tensor
            def _(pe):
                for r, n in enumerate(widths):
                    pe.wait_ge(s_lanes, r + 1)
                    for i in range(2):
                        last = nc.tensor.transpose(ps_in[0:n, i * P:(i + 1) * P], lanes[:, i, 0:n], c.ident[:])
                    last.then_inc(s_turned, 1)
                    pe.wait_ge(s_chain, r + 1)
                    nc.tensor.transpose(ps_out[:, 0:n], chain[0:n, 0:P] if r != 1 else chain[0:n, 2:P + 2],
                                        c.ident[0:n, 0:n]).then_inc(s_back, 1)

            @block.scalar
            def _(act):
                act.wait_ge(s_exp_in, 1)
                nc.scalar.activation(top[:], top[:], ACT.Exp).then_inc(s_exp, 1)
                act.wait_ge(s_std, 1)
                nc.scalar.activation(var[:], var[:], ACT.Sqrt, bias=c.eps[:], scale=1.0 / HE).then_inc(s_std, 1)
                act.wait_ge(s_exp_in, 2)
                nc.scalar.activation(score[:], score[:], ACT.Exp).then_inc(s_exp, 1)

            @block.vector
            def _(v):
                V = nc.vector

                def carries(r, op0, op1, first, backward=False):
                    n = widths[r]
                    v.drain()
                    v.sem_inc(s_lanes, 1)
                    v.wait_ge(s_turned, r + 1)
                    V.tensor_copy(turned[0:n].rearrange("p a b -> p (a b)"), ps_in[0:n, 0:2 * P])
                    V.memset(chain[:, 0:1] if not backward else chain[:, P + 1:P + 2], first)
                    v.drain()
                    flags, vals = turned[0:n, 0, :], turned[0:n, 1, :]
                    if backward:
                        V.tensor_tensor_scan(chain[0:n, 1:P + 1][:, ::-1], flags[:, ::-1], vals[:, ::-1], first, op0, op1)
                    else:
                        V.tensor_tensor_scan(chain[0:n, 1:P + 1], flags, vals, first, op0, op1)
                    v.drain()
                    v.sem_inc(s_chain, 1)
                    v.wait_ge(s_back, r + 1)
                    V.tensor_copy(carry[:, 0:n], ps_out[:, 0:n])
                    v.drain()

                v.wait_ge(s_in, 80)
                V.tensor_scalar(selfm[:].bitcast(I32), keys, SELF, None, ALU.bitwise_and)
                V.tensor_scalar(keys, keys, SRC_BITS, None, ALU.logical_shift_right)
                V.tensor_scalar(prev, prev, SRC_BITS, None, ALU.logical_shift_right)
                v.drain()
                V.tensor_copy(start[:], keys)
                V.tensor_copy(keep[:], prev)
                V.tensor_copy(other[:], selfm[:].bitcast(I32))
                v.drain()
                V.tensor_tensor(keep[:], start[:], keep[:], ALU.is_equal)
                V.tensor_scalar(selfm[:], other[:], float(SELF), None, ALU.is_equal)
                v.drain()
                V.tensor_scalar(other[:], selfm[:], -1.0, 1.0, ALU.mult, ALU.add)
                V.tensor_scalar(start[:], keep[:], BIG, -BIG, ALU.mult, ALU.add)
                V.memset(zero, 0.0)
                v.drain()

                for h in range(HEADS):
                    V.tensor_tensor_scan(top[:, :, h], start[:], G[:, :, HE + h], -BIG, ALU.add, ALU.max)
                V.tensor_tensor_scan(pen[:], start[:], zero, 0.0, ALU.min, ALU.add)
                v.drain()
                V.tensor_copy(lanes[:, 0, 0:HEADS], bcast(pen[:, W - 1], 1, HEADS))
                V.tensor_copy(lanes[:, 1, 0:HEADS], top[:, W - 1, :])
                carries(0, ALU.add, ALU.max, -BIG)
                for h in range(HEADS):
                    V.scalar_tensor_tensor(top[:, :, h], pen[:], carry[:, h:h + 1], top[:, :, h], ALU.add, ALU.max)
                v.drain()

                V.tensor_tensor(top[:], top[:], bcast(selfm[:], 2, HEADS), ALU.mult)
                V.tensor_tensor(dlog[:], G[:, :, HE + HEADS:ROW], bcast(selfm[:], 2, HEADS), ALU.mult)
                V.memset(pen[:], 0.0)
                v.drain()
                V.tensor_tensor_scan(start[:, ::-1], other[:, ::-1], pen[:, ::-1], 1.0, ALU.mult, ALU.add)
                for t in (top, dlog):
                    for h in range(HEADS):
                        V.tensor_tensor_scan(t[:, ::-1, h], other[:, ::-1], t[:, ::-1, h], 0.0, ALU.mult, ALU.add)
                v.drain()
                V.tensor_copy(lanes[:, 0, 0:2 * HEADS], bcast(start[:, 0], 1, 2 * HEADS))
                V.tensor_copy(lanes[:, 1, 0:HEADS], top[:, 0, :])
                V.tensor_copy(lanes[:, 1, HEADS:2 * HEADS], dlog[:, 0, :])
                carries(1, ALU.mult, ALU.add, 0.0, backward=True)
                for i, t in enumerate((top, dlog)):
                    for h in range(HEADS):
                        V.scalar_tensor_tensor(t[:, :, h], start[:], carry[:, i * HEADS + h:i * HEADS + h + 1], t[:, :, h],
                                               ALU.mult, ALU.add)
                v.drain()

                V.tensor_tensor(top[:], top[:], dlog[:], ALU.add)
                V.tensor_tensor(dlog[:], dlog[:], G[:, :, HE:HE + HEADS], ALU.add)
                v.drain()
                for t in (top, dlog):
                    V.scalar_tensor_tensor(t[:], t[:], 0.2, t[:], ALU.mult, ALU.max)
                v.drain()
                V.tensor_tensor(top[:], dlog[:], top[:], ALU.subtract).then_inc(s_exp_in, 1)
                V.tensor_tensor_scan(start[:], keep[:], pen[:], 1.0, ALU.mult, ALU.add)
                v.wait_ge(s_exp, 1)
                V.tensor_tensor(G[:, :, 0:HE].rearrange("p w (h e) -> p w h e", h=HEADS),
                                G[:, :, 0:HE].rearrange("p w (h e) -> p w h e", h=HEADS), bcast(top[:], 3, EXPERTS), ALU.mult)
                V.tensor_copy(G[:, :, HE:NV], top[:])
                v.drain()

                for i in range(NV):
                    V.tensor_tensor_scan(G[:, :, i], keep[:], G[:, :, i], 0.0, ALU.mult, ALU.add)
                v.drain()
                V.tensor_copy(lanes[:, 0, :], bcast(start[:, W - 1], 1, NV))
                V.tensor_copy(lanes[:, 1, :], G[:, W - 1, 0:NV])
                carries(2, ALU.mult, ALU.add, 0.0)
                for i in range(NV):
                    V.scalar_tensor_tensor(G[:, :, i], start[:], carry[:, i:i + 1], G[:, :, i], ALU.mult, ALU.add)
                v.drain()
                v.sem_inc(s_done, 1)

                v.wait_ge(s_num, 16 * TILES)
                V.tensor_scalar(den[:], num[:, :, HE:NV], 1e-16, None, ALU.add)
                v.drain()
                V.reciprocal(den[:], den[:])
                v.drain()
                V.tensor_tensor(dev[:].rearrange("p t (h e) -> p t h e", h=HEADS),
                                num[:, :, 0:HE].rearrange("p t (h e) -> p t h e", h=HEADS), bcast(den[:], 3, EXPERTS), ALU.mult)
                v.drain()
                V.tensor_tensor(dev[:], dev[:], bcast(par[:, 0, :], 1, TILES), ALU.add)
                v.drain()
                V.tensor_reduce(mu[:], dev[:], AX_X, ALU.add)
                v.drain()
                V.scalar_tensor_tensor(dev[:], bcast(mu[:], 2, HE), -1.0 / HE, dev[:], ALU.mult, ALU.add)
                v.drain()
                V.tensor_tensor(sq[:], dev[:], dev[:], ALU.mult)
                v.drain()
                V.tensor_reduce(var[:], sq[:], AX_X, ALU.add).then_inc(s_std, 1)
                v.wait_ge(s_std, 2)
                V.reciprocal(var[:], var[:])
                v.drain()
                V.tensor_tensor(dev[:], dev[:], bcast(var[:], 2, HE), ALU.mult)
                v.drain()
                V.tensor_tensor(dev[:], dev[:], bcast(par[:, 1, :], 1, TILES), ALU.mult)
                v.drain()
                V.tensor_tensor(dev[:], dev[:], bcast(par[:, 2, :], 1, TILES), ALU.add)
                v.drain()
                V.tensor_reduce(score[:], dev[:].rearrange("p t (h e) -> p t e h", h=HEADS), AX_X, ALU.add)
                v.drain()
                V.tensor_scalar(score[:], score[:], 1.0 / HEADS, None, ALU.mult)
                for e in range(EXPERTS):
                    V.memset(rank[:, :, e], float(e))
                v.drain()
                for e in range(EXPERTS):
                    for f in range(e + 1, EXPERTS):
                        V.tensor_tensor(wins[:], score[:, :, f], score[:, :, e], ALU.is_gt)
                        v.drain()
                        V.tensor_tensor(rank[:, :, e], rank[:, :, e], wins[:], ALU.add)
                        V.tensor_tensor(rank[:, :, f], rank[:, :, f], wins[:], ALU.subtract)
                        v.drain()
                V.tensor_reduce(mu[:], score[:], AX_X, ALU.max)
                V.tensor_scalar(rank[:], rank[:], 2.0, None, ALU.is_lt)
                v.drain()
                V.tensor_tensor(score[:], score[:], bcast(mu[:], 2, EXPERTS), ALU.subtract).then_inc(s_exp_in, 1)
                v.wait_ge(s_exp, 2)
                V.tensor_tensor(score[:], score[:], rank[:], ALU.mult)
                v.drain()
                V.tensor_reduce(mu[:], score[:], AX_X, ALU.add)
                v.drain()
                V.reciprocal(mu[:], mu[:])
                v.drain()
                V.tensor_tensor(gates[:], score[:], bcast(mu[:], 2, EXPERTS), ALU.mult)


def combine(c, out, gates):
    nc = c.nc
    ctx, sb, ps = c.open()
    with ctx:
        x2 = [sb(f"co_x2{i}", [P, GT, D]) for i in range(2)]
        y = [sb(f"co_y{i}", [P, EXPERTS, GT, D]) for i in range(2)]
        s_in = [c.sem(f"co_in{i}") for i in range(2)]
        s_sum, s_st = c.sem("co_sum"), c.sem("co_st")
        x2_v = c.x2_d.rearrange("(t p) d -> p t d", p=P)
        out_v = out.rearrange("(t p) d -> p t d", p=P)
        with nc.Block() as block:
            @block.sync
            def _(sp):
                for g in range(GROUPS):
                    at = slice(g * GT, (g + 1) * GT)
                    if g >= 2:
                        sp.wait_ge(s_st, 16 * (g - 1))
                    sp.dma_start(x2[g % 2][:], x2_v[:, at, :]).then_inc(s_in[g % 2], 16)
                    for e in range(EXPERTS):
                        sp.dma_start(y[g % 2][:, e], c.y_d[e].rearrange("(t p) d -> p t d", p=P)[:, at, :]).then_inc(s_in[g % 2], 16)

            @block.vector
            def _(v):
                for g in range(GROUPS):
                    v.wait_ge(s_in[g % 2], 16 * (EXPERTS + 1) * (g // 2 + 1))
                    for e in range(EXPERTS):
                        for u in range(GT):
                            last = nc.vector.scalar_tensor_tensor(x2[g % 2][:, u, :], y[g % 2][:, e, u, :],
                                                                  gates[:, g * GT + u, e:e + 1], x2[g % 2][:, u, :], ALU.mult, ALU.add)
                        v.drain()
                    v.sem_inc(s_sum, 1)

            @block.scalar
            def _(act):
                for g in range(GROUPS):
                    act.wait_ge(s_sum, g + 1)
                    act.dma_start(out_v[:, g * GT:(g + 1) * GT, :], x2[g % 2][:]).then_inc(s_st, 16)
                    act.wait_ge(s_st, 16 * (g + 1))


def lay_out(inputs):
    col = lambda v: np.ascontiguousarray(v.reshape(-1, P).T)
    valid = np.zeros((N_PAD,), np.float32)
    valid[:N_NODES] = 1.0
    i = {k: np.asarray(v) for k, v in inputs.items()}
    pad = SORT_N - E_GNN
    edges = i["L0_ffn_edge_index"]
    return {
        "x": np.pad(i["x"], ((0, N_PAD - N_NODES), (0, 0)), mode="edge"),
        "src": np.pad(i["src"], (0, pad)).reshape(P, LANE),
        "dst": np.pad(i["dst"], (0, pad), constant_values=PAD_DST).reshape(P, LANE),
        "gat_src": edges[0].reshape(P, LANE), "gat_dst": edges[1].reshape(P, LANE),
        "ln_g": col(i["L0_mix_ln_g"]), "ln_b": col(i["L0_mix_ln_b"]),
        "wqkv": i["L0_mix_Wqkv"], "wproj": i["L0_mix_Wproj"], "wself": i["L0_gnn_W_self"],
        "wneigh": i["L0_gnn_W_neigh"], "wg1": i["L0_mix_Wg1"], "wg2": i["L0_mix_Wg2"],
        "bg1": i["L0_mix_bg1"].reshape(GATE_H, 1), "bg2": col(i["L0_mix_bg2"]),
        "bproj": i["L0_mix_bproj"].reshape(1, D), "b_gnn": i["L0_gnn_b"].reshape(1, D),
        "valid": col(valid),
        "w_gat": i["L0_ffn_W_gat"], "att_src": i["L0_ffn_att_src"].reshape(1, HE), "att_dst": i["L0_ffn_att_dst"].reshape(1, HE),
        "b_gat": i["L0_ffn_b_gat"].reshape(1, HE), "gamma": i["L0_ffn_ln_gamma"].reshape(1, HE),
        "beta": i["L0_ffn_ln_beta"].reshape(1, HE),
        "w1": i["L0_ffn_W1"], "w2": i["L0_ffn_W2"],
        "b1": col(i["L0_ffn_b1"]), "b2": i["L0_ffn_b2"].reshape(1, EXPERTS * D),
    }




def program(nc, a, out):
    c = Core(nc)
    c.skey_gnn = c.dram("skey_gnn", [SORT_N])
    c.skey_gat = c.dram("skey_gat", [P + GAT_N])
    c.tail_d = c.dram("tail_d", [SELF_N])
    c.low_d = c.dram("low_d", [SELF_N])
    c.xn_tab = c.dram("xn_tab", [N_PAD, D])
    c.xnT_d = c.dram("xnT_d", [P, KC, N_PAD])
    c.xn2T_d = c.dram("xn2T_d", [P, KC, N_PAD])
    c.base_d = c.dram("base_d", [N_PAD, 2 * D])
    c.x2_d = c.dram("x2_d", [N_PAD, D])
    c.x2nT_d = c.dram("x2nT_d", [P, KC, N_PAD])
    c.hx_d = c.dram("hx_d", [N_PAD, ROW])
    c.y_d = c.dram("y_d", [EXPERTS, N_PAD, D])
    c.sums_d = c.dram("sums_d", [GAT_N, ROW])
    constants(c)
    key_signs(c)
    endpos = nc.alloc_sbuf_tensor("endpos", [P, TILES], I32)
    gates = nc.alloc_sbuf_tensor("gates", [P, TILES, EXPERTS], F32)
    sort_edges(c, a)
    gat_ends(c, endpos)
    normalise(c, a)
    mix(c, a)
    ctx, sb, ps = c.open()
    with ctx:
        t = StepTables(sb)
        acc = sb("acc", [P, TILES * (D + 1)])
        gnn_steps(c, t)
        gnn_sum(c, t, acc)
        gnn_out(c, a, acc)
    ctx, sb, ps = c.open()
    with ctx:
        G = sb("edge_rows", [P, W, ROW])
        gat_gather_experts(c, a, G)
        gat_softmax(c, a, G, endpos, gates)
    combine(c, out, gates)


def kernel(**inputs):
    import concourse.bacc as _bacc
    from concourse.bass_utils import run_bass_kernel_spmd as _run

    nc = _bacc.Bacc("TRN2", target_bir_lowering=False, num_devices=1)
    arrays, aps = {}, {}
    for name, array in lay_out(inputs).items():
        array = np.ascontiguousarray(array)
        arrays[f"in_{name}_dram"] = array
        aps[name] = nc.dram_tensor(f"in_{name}_dram", array.shape, mybir.dt.from_np(array.dtype), kind="ExternalInput").ap()
    out = nc.dram_tensor("out_0_dram", (N_PAD, D), F32, kind="ExternalOutput").ap()
    program(nc, aps, out)
    r = _run(nc, [arrays], core_ids=[0])
    return r.results[0]["out_0_dram"][:N_NODES]
```

```python
from contextlib import ExitStack

import numpy as np
import concourse.bass as bass
from concourse import mybir

F32 = mybir.dt.float32
I32 = mybir.dt.int32
ALU = mybir.AluOpType
ACT = mybir.ActivationFunctionType
AX_X = mybir.AxisListType.X
DVE_ENGINE = mybir.EngineType.DVE
ds = bass.ds

P = 128
N_NODES = 6250
D = 256
KC = D // P
TILES = -(-N_NODES // P)
N_PAD = TILES * P
GROUPS = 7
GT = TILES // GROUPS
GN = GT * P
HB = GN // 2
LN_EPS = 1e-5
HEADS_MIX = 8
HD = D // HEADS_MIX
GATE_H = 64

EXPERTS = 4
HEADS = 4
HE = HEADS * EXPERTS
HID = 512
HC = HID // P

E_GNN = 100000
E_GAT = 131072
LANE = 1024
SORT_N = P * LANE
OFF = 1 << 30
SRC_BITS = 14
SELF = (1 << SRC_BITS) - 1
DST_MASK = 8191
PAD_DST = 8191

CH_GNN = -(-E_GNN // P)
STEPS = CH_GNN + TILES - 1
SBLK = 16
SHALF = SBLK // 2
S_ITERS = -(-STEPS // SBLK)
STEP_COLS = -(-(S_ITERS * SBLK + SHALF) // P) * P
STEP_G = STEP_COLS // P

SELF_N = 8192
GAT_N = SORT_N + SELF_N
W = GAT_N // P
G_ITERS = W // SBLK
LOW_ITERS = 53
W_LOW = LOW_ITERS * SBLK
FENCES = GAT_N // P
FENCE_P = 64
ROW = HE + 2 * HEADS
BIG = 1e30
SENTINEL = float(np.array(OFF | PAD_DST << SRC_BITS, np.int32).view(np.float32))

LANE_BITS = P.bit_length() - 1
ALONG = LANE.bit_length() - 1
MERGES = LANE_BITS + 1

assert TILES == GROUPS * GT and E_GAT == SORT_N and W % SBLK == 0 and FENCES % FENCE_P == 0


def bcast(ap, axis, n):
    v = ap.unsqueeze(axis)
    return v.to_broadcast([*v.shape[:axis], n, *v.shape[axis + 1:]])


class Core:

    def __init__(self, nc):
        self.nc = nc

    def sem(self, name):
        return self.nc.alloc_semaphore(name)

    def dram(self, name, shape, dt=F32):
        return self.nc.dram_tensor(name, shape, dt, kind="Internal").ap()

    def open(self):
        ctx = ExitStack()
        sb = lambda name, shape, dt=F32: ctx.enter_context(self.nc.sbuf_tensor(name, shape, dt))
        ps = lambda name, shape, dt=F32: ctx.enter_context(self.nc.psum_tensor(name, shape, dt))
        return ctx, sb, ps


def constants(c):
    nc = c.nc
    c.ident = nc.alloc_sbuf_tensor("ident", [P, P], F32)
    c.ones = nc.alloc_sbuf_tensor("ones", [P, P], F32)
    c.iota_row = nc.alloc_sbuf_tensor("iota_row", [P, P], F32)
    c.iota_col = nc.alloc_sbuf_tensor("iota_col", [P, 1], I32)
    c.eps = nc.alloc_sbuf_tensor("eps", [P, 1], F32)
    iota_colf = nc.alloc_sbuf_tensor("iota_colf", [P, 1], F32)
    s_iota = c.sem("const_iota")
    with nc.Block() as block:
        @block.gpsimd
        def _(pool):
            nc.gpsimd.iota(c.iota_row[:], pattern=[[1, P]], base=0, channel_multiplier=0,
                           allow_small_or_imprecise_dtypes=True)
            nc.gpsimd.iota(c.iota_col[:], pattern=[[0, 1]], base=0, channel_multiplier=1).then_inc(s_iota, 1)

        @block.vector
        def _(v):
            nc.vector.memset(c.ones[:], 1.0)
            nc.vector.memset(c.eps[:], LN_EPS)
            v.wait_ge(s_iota, 1)
            nc.vector.tensor_copy(iota_colf[:], c.iota_col[:])
            v.drain()
            nc.vector.tensor_scalar(c.ident[:], c.iota_row[:], iota_colf[:], None, ALU.is_equal)


def key_tables(c):
    nc = c.nc
    c.signs = nc.alloc_sbuf_tensor("signs", [P, MERGES + 1], F32)
    c.off = nc.alloc_sbuf_tensor("merge_off", [P, MERGES + 1, LANE_BITS], F32)
    c.noff = nc.alloc_sbuf_tensor("merge_noff", [P, MERGES + 1, LANE_BITS], F32)
    bits = nc.alloc_sbuf_tensor("sign_bits", [P, LANE_BITS + 1], I32)
    per = nc.alloc_sbuf_tensor("sign_block", [P, LANE_BITS + 1], F32)
    with nc.Block() as block:
        @block.vector
        def _(v):
            for b in range(LANE_BITS + 1):
                nc.vector.tensor_scalar(bits[:, b:b + 1], c.iota_col[:], b, 1, ALU.logical_shift_right, ALU.bitwise_and)
            nc.vector.memset(c.signs[:], 1.0)
            nc.vector.memset(c.off[:], 0.0)
            nc.vector.memset(c.noff[:], 0.0)
            v.drain()
            nc.vector.tensor_scalar(per[:], bits[:], -2.0, 1.0, ALU.mult, ALU.add)
            for m in range(1, LANE_BITS):
                nc.vector.memset(c.off[:, m, 0:LANE_BITS - m], BIG)
                nc.vector.memset(c.noff[:, m, 0:LANE_BITS - m], -BIG)
            v.drain()
            nc.vector.tensor_copy(c.signs[:, 0:1], per[:, 0:1])
            nc.vector.tensor_tensor(c.signs[:, 1:LANE_BITS + 1], per[:, 0:LANE_BITS], per[:, 1:LANE_BITS + 1], ALU.mult)


def pairs(ap, dist):
    v = ap.rearrange("p (n two d) -> p n two d", two=2, d=dist)
    return v[:, :, 0, :], v[:, :, 1, :]


def lane_stages():
    stages, size = [], 2
    while size <= LANE:
        stages.append((size, None))
        dist = size // 4
        while dist:
            stages.append((size, dist))
            dist //= 2
        size *= 2
    return stages


class Sorter:

    STAGES = lane_stages()

    def __init__(self, c, name, sb, turned):
        self.c = c
        self.buf = [sb(f"{name}_keys{i}", [P, LANE]) for i in range(2)]
        self.turned = turned
        self.s_ready, self.s_turned = c.sem(f"{name}_ready"), c.sem(f"{name}_turned")

    def compare(self, v, dst, src, dist):
        nc = self.c.nc
        s, t = pairs(src, dist), pairs(dst, dist)
        nc.vector.tensor_tensor(t[0], s[0], s[1], ALU.min)
        nc.vector.tensor_tensor(t[1], s[0], s[1], ALU.max)
        v.drain()

    def compare_psum(self, v, dst, src, dist):
        nc = self.c.nc
        s, t = pairs(src, dist), pairs(dst, dist)
        nc.vector.tensor_copy(t[1], s[1])
        v.drain()
        nc.vector.tensor_tensor(t[0], s[0], t[1], ALU.min)
        nc.vector.tensor_tensor(t[1], s[0], t[1], ALU.max)
        v.drain()

    def first_sign(self, v):
        self.c.nc.vector.tensor_scalar(self.buf[0][:], self.buf[0][:], self.c.signs[:, 0:1], None, ALU.mult)
        v.drain()

    def lane_stage(self, v, i):
        nc = self.c.nc
        size, dist = self.STAGES[i]
        src, dst = self.buf[i % 2][:], self.buf[1 - i % 2][:]
        if dist:
            self.compare(v, dst, src, dist)
        else:
            half = size // 2
            s, t = (x.rearrange("p (n z) -> p n z", z=size) for x in (src, dst))
            nc.vector.tensor_tensor(t[:, :, 0:half], s[:, :, 0:half], s[:, :, half:size][:, :, ::-1], ALU.min)
            nc.vector.tensor_tensor(t[:, :, half:size], s[:, :, half:size], s[:, :, 0:half][:, :, ::-1], ALU.max)
            v.drain()

    def ask(self, v, m):
        self.c.nc.vector.tensor_scalar(self.buf[0][:], self.buf[1][:], self.c.signs[:, ds(m, 1)], None, ALU.mult)
        v.drain()
        v.sem_inc(self.s_ready, 1)

    def across_stage(self, v, m, i):
        nc, c = self.c.nc, self.c
        off, noff = c.off[:, ds(m, 1), i], c.noff[:, ds(m, 1), i]
        dst = pairs(self.buf[1 - i % 2][:], P >> (i + 1))
        if i == 0:
            src = pairs(self.turned, P >> 1)
            nc.vector.tensor_copy(dst[1], src[1])
            v.drain()
            nc.vector.scalar_tensor_tensor(dst[0], dst[1], off, src[0], ALU.add, ALU.min)
            nc.vector.scalar_tensor_tensor(dst[1], src[0], noff, dst[1], ALU.add, ALU.max)
        else:
            src = pairs(self.buf[i % 2][:], P >> (i + 1))
            nc.vector.scalar_tensor_tensor(dst[0], src[1], off, src[0], ALU.add, ALU.min)
            nc.vector.scalar_tensor_tensor(dst[1], src[0], noff, src[1], ALU.add, ALU.max)
        v.drain()

    def ask_back(self, v):
        v.sem_inc(self.s_ready, 1)

    def along_stage(self, v, i):
        if i == 0:
            self.compare_psum(v, self.buf[0][:], self.turned, LANE >> 1)
        else:
            self.compare(v, self.buf[i % 2][:], self.buf[1 - i % 2][:], LANE >> (i + 1))

    def merge(self, v, m):
        self.ask(v, m)
        v.wait_ge(self.s_turned, 2 * m - 1)
        for i in range(LANE_BITS):
            self.across_stage(v, m, i)
        self.ask_back(v)
        v.wait_ge(self.s_turned, 2 * m)
        for i in range(ALONG):
            self.along_stage(v, i)

    def turn_from(self, pe, b, count):
        nc = self.c.nc
        pe.wait_ge(self.s_ready, count)
        for k in range(LANE // P):
            last = nc.tensor.transpose(self.turned[:, k * P:(k + 1) * P], self.buf[b][:, k * P:(k + 1) * P], self.c.ident[:])
        last.then_inc(self.s_turned, 1)


class StepTables:
    def __init__(self, sb):
        self.idx = sb("step_src", [P, STEP_COLS], I32)
        self.nloc = sb("step_nloc", [P, STEP_COLS])
        self.tile = sb("step_tile", [1, STEP_COLS], I32)


def prepare(c, a, t, ncm):
    nc = c.nc
    Q = LANE // P
    ctx, sb, ps = c.open()
    with ctx:
        xg = sb("xg", [P, GT, D])
        xn = sb("xn", [P, GT, D])
        xnn = sb("xnn", [P, GT, D])
        stats = sb("stats", [P, GT, 6])
        mv = sb("mv", [P, GT, 2])
        std = sb("std", [P, GT])
        rstd = sb("rstd", [P, GT])
        xnT = sb("xnT", [P, KC, GN])
        xn2T = sb("xn2T", [P, KC, GN])
        ln_g = sb("ln_g", [P, KC])
        ln_b = sb("ln_b", [P, KC])
        wk = sb("ln_wk", [P, KC, 3 * D])
        bmax = sb("bmax", [P, KC, 2 * GROUPS])
        cmax = sb("cmax", [P, KC])
        psA = [ps(f"psA{i}", [P, 512]) for i in range(2)]
        psB = [ps(f"psB{i}", [P, 512]) for i in range(2)]
        psK = ps("psK", [P, 4 * 512])
        bankK = [psK[:, i * 512:(i + 1) * 512] for i in range(4)]
        s_x, s_mv, s_std, s_xn, s_xnn = c.sem("ln_x"), c.sem("ln_mv"), c.sem("ln_std"), c.sem("ln_xn"), c.sem("ln_xnn")
        s_tA, s_evA, s_tB, s_evB = c.sem("ln_tA"), c.sem("ln_evA"), c.sem("ln_tB"), c.sem("ln_evB")
        s_row, s_outA, s_outB, s_k, s_kmax, s_cm, s_cmT = (c.sem("ln_" + n) for n in (
            "row", "outA", "outB", "k", "kmax", "cm", "cmT"))
        x_v = a["x"].rearrange("(t p) d -> p t d", p=P)
        xn_v = c.xn_tab.rearrange("(t p) d -> p t d", p=P)

        src = sb("edge_src", [P, LANE], I32)
        dst = sb("edge_dst", [P, LANE], I32)
        nxt = sb("edge_next", [P, LANE], I32)
        less = sb("edge_less", [P, LANE])
        drops = sb("edge_drops", [P, 1])
        unsorted = sb("edge_unsorted", [1, 1], I32)
        srt = Sorter(c, "gnnsort", sb, psK[:, 0:LANE])
        s_edges, s_drops, s_bad, s_keys, s_flag, s_sorted, s_st = (c.sem("eg_" + n) for n in (
            "in", "drops", "bad", "keys", "flag", "sorted", "st"))

        keys = sb("st_keys", [P, LANE], I32)
        last_i = sb("st_last_i", [P, Q], I32)
        ends = sb("st_ends", [P, Q])
        ch_i = sb("st_ch_i", [P, Q], I32)
        ch_f = sb("st_ch_f", [P, Q])
        all_ends = sb("st_all_ends", [P, CH_GNN])
        before = sb("st_before", [P, CH_GNN])
        step_i = sb("st_step_i", [P, STEP_G], I32)
        step_f = sb("st_step_f", [P, STEP_G])
        chunk = sb("st_chunk", [P, STEP_G])
        chunk_i = sb("st_chunk_i", [P, STEP_G], I32)
        tile = sb("st_tile", [P, STEP_G])
        t_rows = sb("st_t_rows", [STEP_G, P], I32)
        row = sb("st_row", [P, STEP_G, P], I32)
        src_i = sb("st_src_i", [P, STEP_G, P], I32)
        src_f = sb("st_src_f", [P, STEP_G, P])
        dst_f = sb("st_dst_f", [P, STEP_G, P])
        s_keysin, s_num, s_ends, s_endst, s_all, s_chunk, s_rows, s_dec, s_turn, s_t, s_tst = (c.sem("st_" + n) for n in (
            "keys_in", "num", "ends", "end_st", "all", "chunk", "rows", "dec", "turn", "t", "t_st"))
        ends_d = c.dram("step_ends_d", [LANE])
        tile_d = c.dram("step_tile_d", [STEP_COLS])
        sorted_v = c.skey_gnn.rearrange("(p j) -> p j", p=P)
        dst_flat = a["dst"].rearrange("p j -> (p j)")

        with nc.Block() as block:
            @block.sync
            def _(sp):
                sp.dma_start(xg[:], x_v[:, 0:GT, :]).then_inc(s_x, 16)
                sp.dma_start(wk[:], a["wqkv"].rearrange("(k p) n -> p k n", p=P)).then_inc(s_row, 16)
                with sp.Fori(1, GROUPS) as g:
                    sp.wait_ge(s_xn, g * GT)
                    sp.dma_start(xg[:], x_v[:, ds(g * GT, GT), :]).then_inc(s_x, 16)
                    sp.dma_start(xn_v[:, ds(g * GT - GT, GT), :], xn[:]).then_inc(s_row, 16)
                sp.wait_ge(s_xn, TILES)
                sp.dma_start(xn_v[:, TILES - GT:TILES, :], xn[:]).then_inc(s_row, 16)
                sp.wait_ge(s_row, 16 * GROUPS + 16)

            @block.gpsimd
            def _(pool):
                pool.dma_start(dst[:], a["dst"]).then_inc(s_edges, 16)
                pool.dma_start(nxt[0:P - 1, :], dst_flat[1:SORT_N - LANE + 1].rearrange("(p j) -> p j", p=P - 1)).then_inc(s_edges, 16)
                pool.dma_start(nxt[P - 1:P, 0:LANE - 1], dst_flat[SORT_N - LANE + 1:SORT_N].rearrange("(p j) -> p j", p=1)).then_inc(s_edges, 16)
                pool.dma_start(src[:], a["src"]).then_inc(s_edges, 16)
                nc.gpsimd.iota(ch_i[:], pattern=[[1, Q]], base=0, channel_multiplier=Q)
                nc.gpsimd.iota(step_i[:], pattern=[[P, STEP_G]], base=0, channel_multiplier=1).then_inc(s_num, 1)
                pool.wait_ge(s_keys, 1)
                pool.dma_start(sorted_v, srt.buf[0][:]).then_inc(s_st, 16)
                pool.wait_ge(s_st, 16)
                pool.wait_ge(s_flag, 1)
                with pool.If(pool.value_load(unsorted[0:1, 0:1], min_val=0, max_val=P) > 0):
                    pool.wait_ge(s_sorted, 1)
                    pool.dma_start(sorted_v, srt.buf[1][:]).then_inc(s_st, 16)
                    pool.wait_ge(s_st, 32)
                pool.dma_start(keys[:], sorted_v.bitcast(I32)).then_inc(s_keysin, 16)
                pool.wait_ge(s_ends, 1)
                pool.dma_start(ends_d.rearrange("(p q) -> p q", p=P), ends[:]).then_inc(s_endst, 16)
                pool.wait_ge(s_endst, 16)
                pool.dma_start(all_ends[:], ends_d[0:CH_GNN].rearrange("(o n) -> o n", o=1).to_broadcast([P, CH_GNN])).then_inc(s_all, 16)
                pool.wait_ge(s_chunk, 1)
                for g in range(STEP_G):
                    pool.indirect_dma_start(row[:, g, :], None, c.skey_gnn.rearrange("(c e) -> c e", e=P).bitcast(I32),
                                            bass.IndirectOffsetOnAxis(ap=chunk_i[:, g:g + 1], axis=0)).then_inc(s_rows, 16)
                pool.wait_ge(s_t, 1)
                pool.dma_start(tile_d.rearrange("(g p) -> g p", p=P).bitcast(I32), t_rows[:]).then_inc(s_tst, 16)
                pool.wait_ge(s_tst, 16)
                pool.dma_start(t.tile[:], tile_d.rearrange("(o n) -> o n", o=1).bitcast(I32)).then_inc(s_tst, 16)
                pool.wait_ge(s_tst, 32)

            @block.vector
            def _(v):
                V = nc.vector

                def moments(rows):
                    for u in range(GT):
                        V.bn_stats(stats[:, u, :], rows[:, u, :])
                    v.drain()
                    for u in range(GT):
                        last = V.bn_aggr(mv[:, u, :], stats[:, u, :])
                    return last

                def maxima(g, count):
                    v.wait_ge(s_k, count)
                    for i in range(2):
                        for h in range(KC):
                            last = V.tensor_reduce(bmax[:, h, ds(2 * g + i, 1)], bankK[2 * i + h][:, 0:HB], AX_X, ALU.max)
                    last.then_inc(s_kmax, 1)
                    v.drain()

                def group(g, behind):
                    v.wait_ge(s_x, 16 * g + 16)
                    moments(xg).then_inc(s_mv, 1)
                    v.wait_ge(s_std, 2 * g + 1)
                    V.reciprocal(rstd[:], std[:])
                    v.drain()
                    v.wait_ge(s_tA, g * GT + GT)
                    v.wait_ge(s_row, 16 * g + 16)
                    for u in range(GT):
                        V.tensor_scalar(xn[:, u, :], xg[:, u, :], mv[:, u, 0:1], rstd[:, u:u + 1],
                                        ALU.subtract, ALU.mult).then_inc(s_xn, 1)
                    v.drain()
                    moments(xn).then_inc(s_mv, 1)
                    if behind:
                        maxima(g - 1, g)
                    v.wait_ge(s_std, 2 * g + 2)
                    V.reciprocal(rstd[:], std[:])
                    v.drain()
                    v.wait_ge(s_tB, g * GT + GT)
                    for u in range(GT):
                        V.tensor_scalar(xnn[:, u, :], xn[:, u, :], mv[:, u, 0:1], rstd[:, u:u + 1],
                                        ALU.subtract, ALU.mult).then_inc(s_xnn, 1)
                    v.drain()

                V.memset(less[:, LANE - 1:LANE], 0.0)
                v.drain()
                v.wait_ge(s_edges, 64)
                V.tensor_tensor(less[:, 0:LANE - 1], dst[:, 0:LANE - 1], nxt[:, 0:LANE - 1], ALU.is_gt)
                V.tensor_tensor(less[0:P - 1, LANE - 1:LANE], dst[0:P - 1, LANE - 1:LANE], nxt[0:P - 1, LANE - 1:LANE], ALU.is_gt)
                v.drain()
                V.tensor_scalar(dst[:], dst[:], SRC_BITS, OFF, ALU.logical_shift_left, ALU.bitwise_or)
                V.tensor_reduce(drops[:], less[:], AX_X, ALU.max).then_inc(s_drops, 1)
                v.drain()
                V.tensor_tensor(srt.buf[0][:].bitcast(I32), src[:], dst[:], ALU.bitwise_or).then_inc(s_keys, 1)
                v.wait_ge(s_bad, 1)
                V.tensor_copy(unsorted[:], psA[0][0:1, 0:1])
                v.drain()
                v.sem_inc(s_flag, 1)
                v.wait_ge(s_flag, 1)
                with v.If(v.value_load(unsorted[0:1, 0:1], min_val=0, max_val=P) > 0):
                    v.wait_ge(s_st, 16)
                    srt.first_sign(v)
                    for i in range(len(srt.STAGES)):
                        srt.lane_stage(v, i)
                    with v.Fori(1, MERGES) as m:
                        srt.merge(v, m)
                    v.sem_inc(s_sorted, 1)

                v.wait_ge(s_num, 1)
                V.tensor_copy(ch_f[:], ch_i[:])
                V.tensor_copy(step_f[:], step_i[:])
                v.wait_ge(s_keysin, 16)
                V.tensor_scalar(last_i[:], keys[:].rearrange("p (q e) -> p q e", e=P)[:, :, P - 1], SRC_BITS + LANE_BITS,
                                DST_MASK >> LANE_BITS, ALU.logical_shift_right, ALU.bitwise_and)
                v.drain()
                V.tensor_copy(ends[:], last_i[:])
                v.drain()
                V.scalar_tensor_tensor(ends[:], ends[:], float(TILES - 1), ch_f[:], ALU.min, ALU.add).then_inc(s_ends, 1)
                group(0, False)
                with v.Fori(1, 3) as g:
                    group(g, True)
                v.wait_ge(s_all, 16)
                for g in range(STEP_G):
                    V.tensor_scalar(before[:], all_ends[:], step_f[:, g:g + 1], None, ALU.is_lt, ALU.add,
                                    accum_out=chunk[:, g:g + 1])
                    v.drain()
                V.tensor_copy(chunk_i[:], chunk[:]).then_inc(s_chunk, 1)
                V.tensor_tensor(tile[:], step_f[:], chunk[:], ALU.subtract)
                v.drain()
                V.tensor_scalar(tile[:], tile[:], float(TILES - 1), None, ALU.min)
                v.drain()
                with v.Fori(3, 5) as g:
                    group(g, True)
                maxima(4, 5)
                v.wait_ge(s_rows, 16 * STEP_G)
                V.tensor_scalar(src_i[:], row[:], SELF, None, ALU.bitwise_and)
                V.tensor_scalar(row[:], row[:], SRC_BITS, DST_MASK, ALU.logical_shift_right, ALU.bitwise_and)
                v.drain()
                V.tensor_scalar(src_f[:], src_i[:], float(N_NODES - 1), None, ALU.min)
                V.tensor_copy(dst_f[:], row[:])
                v.drain()
                V.scalar_tensor_tensor(dst_f[:], bcast(tile[:], 2, P), float(P), dst_f[:], ALU.mult, ALU.subtract)
                v.drain()
                v.sem_inc(s_dec, 1)
                v.wait_ge(s_turn, 1)
                V.tensor_copy(t.idx[:], psK[:, 0:STEP_COLS])
                V.tensor_copy(t.nloc[:], psK[:, 1024:1024 + STEP_COLS])
                V.tensor_copy(t_rows[:], psK[0:STEP_G, 2048 - P:2048])
                v.drain()
                v.sem_inc(s_t, 1)
                group(5, False)
                group(6, True)
                maxima(6, GROUPS)

                V.tensor_reduce(cmax[:], bmax[:], AX_X, ALU.max)
                v.drain()
                v.sem_inc(s_cm, 1)
                v.wait_ge(s_cmT, 1)
                V.tensor_scalar(ncm[:], psA[0][0:1, 0:D], -1.0, None, ALU.mult)

            @block.tensor
            def _(pe):
                pe.wait_ge(s_drops, 1)
                nc.tensor.matmul(psA[0][0:1, 0:1], drops[:], c.ones[:, 0:1], start=True, stop=True).then_inc(s_bad, 1)
                pe.wait_ge(s_flag, 1)
                with pe.If(pe.value_load(unsorted[0:1, 0:1], min_val=0, max_val=P) > 0):
                    with pe.Fori(1, MERGES) as m:
                        srt.turn_from(pe, 0, 2 * m - 1)
                        srt.turn_from(pe, 1, 2 * m)
                pe.wait_ge(s_row, 16)

                def turn(g, rows, bank, s_in, s_t, s_ev):
                    for u in range(GT):
                        pe.wait_ge(s_in, g * GT + u + 1)
                        pe.wait_ge(s_ev, g * GT + u + (2 if u == 0 else 1))
                        for k in range(KC):
                            last = nc.tensor.transpose(bank[u % 2][:, k * P:(k + 1) * P],
                                                       rows[:, u, k * P:(k + 1) * P], c.ident[:])
                        last.then_inc(s_t, 1)

                def group(g, behind):
                    turn(g, xn, psA, s_xn, s_tA, s_evA)
                    if behind:
                        turn(g - 1, xnn, psB, s_xnn, s_tB, s_evB)
                    pe.wait_ge(s_evA, g * GT + GT + 2)
                    pe.wait_ge(s_kmax, g + 1)
                    for i in range(2):
                        for h in range(KC):
                            for k in range(KC):
                                last = nc.tensor.matmul(bankK[2 * i + h][:, 0:HB], wk[:, k, D + h * P:D + (h + 1) * P],
                                                        xnT[:, k, i * HB:(i + 1) * HB], start=(k == 0), stop=(k == KC - 1))
                    last.then_inc(s_k, 1)

                group(0, False)
                with pe.Fori(1, 5) as g:
                    group(g, True)
                pe.wait_ge(s_dec, 1)
                for g in range(STEP_G):
                    nc.tensor.transpose(psK[:, g * P:(g + 1) * P], src_f[:, g, :], c.ident[:])
                    nc.tensor.transpose(psK[:, 1024 + g * P:1024 + (g + 1) * P], dst_f[:, g, :], c.ident[:])
                nc.tensor.transpose(psK[0:STEP_G, 2048 - P:2048], tile[:], c.ident[:]).then_inc(s_turn, 1)
                pe.wait_ge(s_t, 1)
                with pe.Fori(5, GROUPS) as g:
                    group(g, True)
                turn(GROUPS - 1, xnn, psB, s_xnn, s_tB, s_evB)
                pe.wait_ge(s_cm, 1)
                for h in range(KC):
                    last = nc.tensor.transpose(psA[0][0:1, h * P:(h + 1) * P], cmax[:, h:h + 1], c.ident[:])
                last.then_inc(s_cmT, 1)

            @block.scalar
            def _(act):
                act.sem_inc(s_tA, GT)
                act.sem_inc(s_tB, GT)
                act.sem_inc(s_evA, 2)
                act.sem_inc(s_evB, 2)
                act.sem_inc(s_kmax, 1)
                act.dma_start(ln_g[:], a["ln_g"]).then_inc(s_outA, 16)
                act.dma_start(ln_b[:], a["ln_b"]).then_inc(s_outB, 16)

                def root(count):
                    act.wait_ge(s_mv, count)
                    nc.scalar.activation(std[:], mv[:, :, 1], ACT.Sqrt, bias=c.eps[:]).then_inc(s_std, 1)

                def rows(g):
                    act.wait_ge(s_outA, 16 * g + 16)
                    for u in range(GT):
                        act.wait_ge(s_tA, g * GT + u + 1 + GT)
                        nc.scalar.copy(xnT[:, :, u * P:(u + 1) * P],
                                       psA[u % 2][:, 0:D].rearrange("p (k n) -> p k n", k=KC)).then_inc(s_evA, 1)
                    act.wait_ge(s_evA, g * GT + GT + 2)
                    act.dma_start(c.xnT_d[:, :, ds(g * GN, GN)], xnT[:]).then_inc(s_outA, 16)

                def mixer_rows(g):
                    act.wait_ge(s_outB, 16 * g + 16)
                    for u in range(GT):
                        act.wait_ge(s_tB, g * GT + u + 1 + GT)
                        for k in range(KC):
                            last = nc.scalar.activation(xn2T[:, k, u * P:(u + 1) * P], psB[u % 2][:, k * P:(k + 1) * P],
                                                        ACT.Identity, bias=ln_b[:, k:k + 1], scale=ln_g[:, k:k + 1])
                        last.then_inc(s_evB, 1)
                    act.wait_ge(s_evB, g * GT + GT + 2)
                    act.dma_start(c.xn2T_d[:, :, ds(g * GN, GN)], xn2T[:]).then_inc(s_outB, 16)

                root(1)
                rows(0)
                root(2)
                root(3)
                with act.Fori(1, GROUPS - 1) as g:
                    rows(g)
                    root(2 * g + 2)
                    mixer_rows(g - 1)
                    root(2 * g + 3)
                rows(GROUPS - 1)
                root(2 * GROUPS)
                mixer_rows(GROUPS - 2)
                mixer_rows(GROUPS - 1)
                act.wait_ge(s_outA, 16 * GROUPS + 16)
                act.wait_ge(s_outB, 16 * GROUPS + 16)


LANE_PAIRS = 2
MID_PAIR = LANE_PAIRS + GROUPS
C_PAIR = MID_PAIR + 1
R_PAIR = C_PAIR + 2 * GROUPS
PAIRS = S_ITERS // 2
QUART = 4
assert S_ITERS % 2 == 0 and PAIRS - R_PAIR == 2
HALF = [(0, 4), (4, 3)]


def aggregate(c, a, t, ncm, acc):
    nc = c.nc
    ROWW = D + 1
    BANKS = 4
    CW = P + 1
    NS = SELF_N // P
    ctx, sb, ps = c.open()
    with ctx:
        msg = sb("ag_msg", [P, QUART, SHALF, ROWW])
        hot = sb("ag_hot", [P, QUART, SHALF, P])
        dif = sb("ag_dif", [P, SHALF, P])
        ixs = sb("ag_ixs", [P, QUART, SHALF], I32)
        tick = sb("ag_tick", [P, QUART])
        bank = [ps(f"ag_ps{i}", [P, 512]) for i in range(BANKS)]
        s_ix, s_tick, s_hot, s_mm, s_acc, s_init = (c.sem("ag_" + n) for n in ("ix", "tick", "hot", "mm", "acc", "init"))
        s_g = [c.sem(f"ag_rows{q}") for q in range(QUART)]

        wqkv = sb("wqkv", [P, KC, 3 * D])
        wproj = sb("wproj", [P, KC, D])
        wself = sb("wself", [P, KC, D])
        wg1 = sb("wg1", [P, KC, GATE_H])
        wg2 = sb("wg2", [GATE_H, D])
        bg1 = sb("bg1", [GATE_H, 1])
        bg2 = sb("bg2", [P, KC])
        bproj = sb("bproj", [1, D])
        valid = sb("valid", [P, TILES])
        bd = sb("bd", [P, P])
        blk_i = sb("blk_i", [P, P], I32)
        blk_f = sb("blk_f", [P, P])
        own_i = sb("own_i", [P, 1], I32)
        own_f = sb("own_f", [P, 1])
        zeros = sb("zeros", [P, KC * CW])
        xT = [sb(f"xT{i}", [P, KC, n * P]) for i, (_, n) in enumerate(HALF)]
        x2T = [sb(f"x2T{i}", [P, KC, n * P]) for i, (_, n) in enumerate(HALF)]
        xr = sb("xr", [P, GT, D])
        ke = sb("ke", [P, 2, D])
        vm = sb("vm", [P, 2, KC, CW])
        rz = sb("rz", [P, KC])
        ctxbd = sb("ctxbd", [P, KC, P])
        wqT = sb("wqT", [P, KC, D])
        m_sb = sb("m_sb", [P, KC, D])
        hg = sb("hg", [GATE_H, 4 * P])
        gate = sb("gate", [P, KC, 4 * P])
        prod = sb("prod", [P, KC, 4 * P])
        rows = sb("rows", [P, GT, 2 * D])
        mix = [ps(f"mx_ps{i}", [P, 512]) for i in range(2)]
        s_w, s_wq, s_wqc, s_kv, s_ev, s_ctx, s_bd, s_m, s_msb = (c.sem("mx_" + n) for n in (
            "w", "wq", "wqc", "kv", "ev", "ctx", "bd", "m", "msb"))
        s_xT = [c.sem(f"mx_xT{i}") for i in range(2)]
        s_in = [c.sem(f"mx_in{i}") for i in range(2)]
        s_rst = [c.sem(f"mx_rowst{i}") for i in range(2)]
        s_hgp, s_hg, s_gp, s_gate, s_at, s_prod, s_rows, s_copied = (c.sem("mx_" + n) for n in (
            "hgp", "hg", "gp", "gate", "at", "prod", "rows", "copied"))
        x_v = a["x"].rearrange("(t p) d -> p t d", p=P)
        rows_v = c.base_d.rearrange("(t p) d -> p t d", p=P)

        psS = ps("srt_ps", [P, LANE])
        srt = Sorter(c, "gatsort", sb, psS[:])
        dst = srt.buf[1][:].bitcast(I32)
        selves = sb("selves", [P, NS], I32)
        pad = sb("selves_pad", [P, NS], I32)
        tail = sb("sort_tail", [P, NS])
        upper = [sb(f"sort_upper{i}", [P, NS]) for i in range(2)]
        upper_t = [sb(f"sort_uppert{i}", [NS, P]) for i in range(2)]
        first = sb("sentinel", [1, P])
        s_edges, s_ids, s_sorted, s_tail, s_tail_ld, s_low, s_low_ld, s_up, s_all, s_out = (c.sem("srt_" + n) for n in (
            "in", "ids", "sorted", "tail", "tail_ld", "low", "low_ld", "up", "all", "out"))
        tail_lanes = P - SELF_N // LANE
        T_LAST = 2 * (MERGES - 1)

        def tile_of(u):
            i = int(u >= HALF[1][0])
            return i, (u - HALF[i][0]) * P

        with nc.Block() as block:
            @block.sync
            def _(sp):
                sp.dma_start(wqkv[:], a["wqkv"].rearrange("(k p) n -> p k n", p=P)).then_inc(s_w, 16)
                sp.dma_start(srt.buf[0][:].bitcast(I32), a["gat_src"]).then_inc(s_edges, 16)
                sp.dma_start(dst, a["gat_dst"]).then_inc(s_edges, 16)
                sp.dma_start(valid[:], a["valid"]).then_inc(s_w, 16)
                for to, src in ((wproj, "wproj"), (wself, "wself"), (wg1, "wg1")):
                    sp.dma_start(to[:], a[src].rearrange("(k p) n -> p k n", p=P)).then_inc(s_w, 16)
                for to, src in ((bg1, "bg1"), (bproj, "bproj")):
                    sp.dma_start(to[:], a[src]).then_inc(s_w, 16)
                for to, src, st in ((wg2, "wg2", s_rst[0]), (bg2, "bg2", s_rst[1])):
                    sp.dma_start(to[:], a[src]).then_inc(st, 16)
                with sp.Fori(0, GROUPS) as g:
                    for i, (u0, n) in enumerate(HALF):
                        sp.wait_ge(s_kv, g * GT + u0 + n)
                        sp.dma_start(xT[i][:], c.xnT_d[:, :, ds(g * GN + u0 * P, n * P)]).then_inc(s_xT[i], 16)
                sp.wait_ge(s_kv, TILES + GT)
                with sp.Fori(0, GROUPS) as g:
                    for i, (u0, n) in enumerate(HALF):
                        sp.wait_ge(s_rows, g * GT + u0 + n)
                        at = ds(g * GN + u0 * P, n * P)
                        sp.dma_start(xT[i][:], c.xnT_d[:, :, at]).then_inc(s_in[i], 16)
                        sp.dma_start(x2T[i][:], c.xn2T_d[:, :, at]).then_inc(s_in[i], 16)
                        sp.dma_start(xr[:, u0:u0 + n, :], x_v[:, ds(g * GT + u0, n), :]).then_inc(s_in[i], 16)
                sp.wait_ge(s_sorted, 1)
                sp.dma_start(c.tail_d.rearrange("(p j) -> p j", j=LANE), srt.buf[1][tail_lanes:P, :]).then_inc(s_tail, 16)
                sp.wait_ge(s_tail, 16)
                sp.dma_start(tail[:], c.tail_d.rearrange("(p j) -> p j", p=P)).then_inc(s_tail_ld, 16)
                sp.wait_ge(s_low, 1)
                sp.dma_start(c.low_d.rearrange("(p j) -> p j", p=P), upper[1][:]).then_inc(s_tail, 16)
                sp.wait_ge(s_tail, 32)
                sp.dma_start(srt.buf[1][tail_lanes:P, :], c.low_d.rearrange("(p j) -> p j", j=LANE)).then_inc(s_low_ld, 16)
                sp.dma_start(c.skey_gat[0:P].rearrange("(p j) -> p j", p=1), first[:]).then_inc(s_out, 16)
                sp.wait_ge(s_all, 1)
                sp.dma_start(c.skey_gat[P:P + SORT_N].rearrange("(p j) -> p j", p=P), srt.buf[1][:]).then_inc(s_out, 16)
                sp.wait_ge(s_up, 1)
                sp.dma_start(c.skey_gat[P + SORT_N:P + GAT_N].rearrange("(p j) -> p j", p=P), upper[1][:]).then_inc(s_out, 16)
                sp.wait_ge(s_out, 48)

            @block.gpsimd
            def _(pool):
                nc.gpsimd.iota(selves[:], pattern=[[-1, NS]], base=SELF_N - 1, channel_multiplier=-NS).then_inc(s_ids, 1)
                with pool.Fori(0, PAIRS) as p:
                    for q in range(QUART):
                        pool.wait_ge(s_ix, QUART * p + q + 1)
                        nc.gpsimd.tensor_tensor(tick[:, q:q + 1], c.eps[:], c.eps[:], ALU.add).then_inc(s_tick, SHALF)
                        for u in range(SHALF):
                            pool.indirect_dma_start(msg[:, q, u, 0:D], None, c.xn_tab,
                                                    bass.IndirectOffsetOnAxis(ap=ixs[:, q, u:u + 1], axis=0)).then_inc(s_g[q], 16)

            @block.vector
            def _(v):
                V = nc.vector

                def tiles_of(at):
                    return nc.values_load_multi_w_load_instructions(
                        t.tile[0:1, ds(at, SBLK)], engines=[DVE_ENGINE], min_val=0, max_val=TILES - 1,
                        skip_runtime_bounds_check_because="at most the last tile by a min")[1]

                def sums(at, odd, tiles, u0, u1):
                    for u in range(u0, u1):
                        v.drain()
                        v.wait_ge(s_mm, at + u + 1 + 2 * SBLK)
                        own = acc[:, ds(tiles[u] * ROWW, ROWW)]
                        V.tensor_tensor(own, own, bank[u % BANKS][:, 0:ROWW], ALU.add).then_inc(s_acc, 1)
                        if u % SHALF == SHALF - 1:
                            v.wait_ge(s_tick, at + u + 1)
                            V.tensor_copy(ixs[:, 2 * odd + u // SHALF, :],
                                          t.idx[:, ds(at + u + 1 - SHALF + 2 * SBLK, SHALF)]).then_inc(s_ix, 1)

                def gated(g, i):
                    n = HALF[i][1] * P
                    v.wait_ge(s_gate, 4 * g + 2 * i + KC)
                    for h in range(KC):
                        v.wait_ge(s_at, 4 * g + 2 * i + h + 1)
                        last = V.tensor_tensor(prod[:, h, 0:n], mix[1 - h][:, 0:n], gate[:, h, 0:n], ALU.mult)
                    last.then_inc(s_prod, 1)

                for q in range(QUART):
                    V.tensor_copy(ixs[:, q, :], t.idx[:, q * SHALF:(q + 1) * SHALF]).then_inc(s_ix, 1)
                v.sem_inc(s_acc, BANKS)
                v.sem_inc(s_prod, 1)
                V.memset(msg[:, :, :, D:ROWW], 1.0)
                V.memset(zeros[:], 0.0)
                V.memset(first[:], SENTINEL)
                V.memset(acc[:], 0.0)
                V.tensor_copy(blk_i[:], c.iota_row[:])
                V.tensor_scalar(own_i[:], c.iota_col[:], HD.bit_length() - 1, None, ALU.arith_shift_right)
                v.drain()
                v.sem_inc(s_init, 1)
                V.tensor_scalar(blk_i[:], blk_i[:], HD.bit_length() - 1, None, ALU.arith_shift_right)
                V.tensor_copy(own_f[:], own_i[:])
                v.drain()
                V.tensor_copy(blk_f[:], blk_i[:])
                v.drain()
                V.tensor_scalar(bd[:], blk_f[:], own_f[:], None, ALU.is_equal)
                v.wait_ge(s_edges, 32)
                V.tensor_scalar(dst, dst, SRC_BITS, OFF, ALU.logical_shift_left, ALU.bitwise_or)
                v.drain()
                V.tensor_tensor(srt.buf[0][:].bitcast(I32), srt.buf[0][:].bitcast(I32), dst, ALU.bitwise_or)
                v.drain()
                srt.first_sign(v)

                stages = len(srt.STAGES)

                def lanes(at, i):
                    sums(at, i % 2, tiles_of(at), 0, SBLK)
                    for k in range(i * stages // 6, (i + 1) * stages // 6):
                        srt.lane_stage(v, k)

                for i in range(2 * LANE_PAIRS):
                    lanes(i * SBLK, i)
                with v.Fori(LANE_PAIRS, MID_PAIR) as p:
                    for odd in range(2):
                        at = p * (2 * SBLK) + odd * SBLK
                        sums(at, odd, tiles_of(at), 0, SBLK)
                v.drain()
                v.wait_ge(s_ctx, TILES + 2)
                for h in range(KC):
                    V.reciprocal(rz[:, h:h + 1], mix[1][:, h * CW + P:h * CW + CW])
                v.drain()
                for h in range(KC):
                    last = V.scalar_tensor_tensor(ctxbd[:, h, :], mix[1][:, h * CW:h * CW + P], rz[:, h:h + 1],
                                                  bd[:], ALU.mult, ALU.mult)
                last.then_inc(s_bd, 1)
                for i in range(2):
                    lanes((2 * MID_PAIR + i) * SBLK, 4 + i)
                v.wait_ge(s_m, 1)
                V.tensor_copy(m_sb[:], mix[0][:, :].rearrange("p (k d) -> p k d", k=KC)).then_inc(s_msb, 1)

                with v.Fori(0, GROUPS) as g:
                    m = g + 1
                    at = C_PAIR * 2 * SBLK + g * (4 * SBLK)
                    srt.ask(v, m)
                    tiles = tiles_of(at)
                    sums(at, 0, tiles, 0, 4)
                    v.drain()
                    v.wait_ge(srt.s_turned, 2 * m - 1)
                    srt.across_stage(v, m, 0)
                    for i in range(1, 4):
                        sums(at, 0, tiles, 4 * i, 4 * i + 4)
                        srt.across_stage(v, m, i)
                    gated(g, 0)
                    at = at + SBLK
                    tiles = tiles_of(at)
                    sums(at, 1, tiles, 0, 4)
                    srt.across_stage(v, m, 4)
                    srt.across_stage(v, m, 5)
                    sums(at, 1, tiles, 4, 8)
                    srt.across_stage(v, m, 6)
                    srt.ask_back(v)
                    sums(at, 1, tiles, 8, 16)
                    v.drain()
                    v.wait_ge(srt.s_turned, 2 * m)
                    srt.along_stage(v, 0)
                    at = at + SBLK
                    tiles = tiles_of(at)
                    for i in range(4):
                        sums(at, 0, tiles, 4 * i, 4 * i + 4)
                        srt.along_stage(v, 1 + i)
                    gated(g, 1)
                    at = at + SBLK
                    tiles = tiles_of(at)
                    for i in range(2):
                        sums(at, 1, tiles, 4 * i, 4 * i + 4)
                        srt.along_stage(v, 5 + 2 * i)
                        srt.along_stage(v, 6 + 2 * i)
                    sums(at, 1, tiles, 8, 12)
                    srt.along_stage(v, 9)
                    sums(at, 1, tiles, 12, 16)
                    v.drain()
                v.sem_inc(s_sorted, 1)

                v.wait_ge(s_ids, 1)
                V.tensor_scalar(pad[:], selves[:], N_NODES, PAD_DST, ALU.is_ge, ALU.mult)
                v.drain()
                V.tensor_tensor(selves[:], selves[:], pad[:], ALU.max)
                v.drain()
                V.tensor_scalar(selves[:], selves[:], SRC_BITS, OFF | SELF, ALU.logical_shift_left, ALU.bitwise_or)
                rest = R_PAIR * 2 * SBLK
                sums(rest, 0, tiles_of(rest), 0, SBLK)
                v.wait_ge(s_tail_ld, 16)
                V.tensor_tensor(upper[1][:], tail[:], selves[:].bitcast(F32), ALU.min)
                V.tensor_tensor(tail[:], tail[:], selves[:].bitcast(F32), ALU.max)
                v.drain()
                v.sem_inc(s_low, 1)
                sums(rest + SBLK, 1, tiles_of(rest + SBLK), 0, SBLK)
                v.drain()
                v.wait_ge(s_low_ld, 16)
                srt.ask(v, MERGES)
                v.wait_ge(srt.s_turned, T_LAST + 1)
                for i in range(LANE_BITS):
                    srt.across_stage(v, MERGES, i)
                srt.ask_back(v)
                sums(rest + 2 * SBLK, 0, tiles_of(rest + 2 * SBLK), 0, SBLK)
                v.drain()
                v.wait_ge(srt.s_turned, T_LAST + 2)
                for i in range(ALONG):
                    srt.along_stage(v, i)
                v.sem_inc(s_all, 1)
                v.sem_inc(srt.s_ready, 1)
                v.wait_ge(srt.s_turned, T_LAST + 3)
                srt.compare_psum(v, upper_t[0][:], psS[0:NS, 0:P], P >> 1)
                for i in range(1, LANE_BITS):
                    srt.compare(v, upper_t[i % 2][:], upper_t[1 - i % 2][:], P >> (i + 1))
                v.sem_inc(srt.s_ready, 1)
                v.wait_ge(srt.s_turned, T_LAST + 4)
                srt.compare_psum(v, upper[0][:], psS[:, 0:NS], NS >> 1)
                for i in range(1, NS.bit_length() - 1):
                    srt.compare(v, upper[i % 2][:], upper[1 - i % 2][:], NS >> (i + 1))
                v.sem_inc(s_up, 1)
                sums(rest + 3 * SBLK, 1, tiles_of(rest + 3 * SBLK), 0, SBLK)

            @block.tensor
            def _(pe):
                def steps(p, k, u0, u1):
                    half = QUART * p + k
                    if u0 == 0:
                        pe.wait_ge(s_hot, half + 1)
                        pe.wait_ge(s_g[k], 16 * SHALF * p + 16 * SHALF)
                    for u in range(u0, u1):
                        pe.wait_ge(s_acc, half * SHALF + u + 1)
                        nc.tensor.matmul(bank[u % BANKS][:, 0:ROWW], hot[:, k, u, :], msg[:, k, u, :],
                                         start=True, stop=True).then_inc(s_mm, 1)

                def pair(p):
                    for k in range(QUART):
                        steps(p, k, 0, SHALF)

                def kv(g, u):
                    i, at = tile_of(u)
                    if u in (0, HALF[1][0]):
                        pe.wait_ge(s_xT[i], 16 * g + 16)
                    pe.wait_ge(s_ev, g * GT + u + 1)
                    b = mix[0]
                    for k in range(KC):
                        nc.tensor.matmul(b[:, :], xT[i][:, k, at:at + P], wqkv[:, k, D:3 * D], start=(k == 0), stop=False,
                                         skip_group_check=True)
                    nc.tensor.matmul(b[:, 0:D], c.ones[0:1, :], ncm[:], start=False, stop=True,
                                     skip_group_check=True).then_inc(s_kv, 1)

                def context(g, u):
                    pe.wait_ge(s_ev, g * GT + u + 2)
                    for h in range(KC):
                        last = nc.tensor.matmul(mix[1][:, h * CW:(h + 1) * CW], ke[:, u % 2, h * P:(h + 1) * P], vm[:, u % 2, h, :],
                                                start=False, stop=False, skip_group_check=True)
                    last.then_inc(s_ctx, 1)

                def hidden(g, i):
                    n = HALF[i][1] * P
                    pe.wait_ge(s_in[i], 48 * g + 48)
                    pe.wait_ge(s_copied, g * GT + HALF[i][0] + GT)
                    for k in range(KC):
                        last = nc.tensor.matmul(mix[0][0:GATE_H, 0:n], wg1[:, k, :], x2T[i][:, k, :], start=(k == 0),
                                                stop=(k == KC - 1))
                    last.then_inc(s_hgp, 1)

                def gates(g, i, h):
                    n = HALF[i][1] * P
                    pe.wait_ge(s_hg, 2 * g + i + 1)
                    nc.tensor.matmul(mix[1 - h][:, 0:n], wg2[:, h * P:(h + 1) * P], hg[:, 0:n], start=True,
                                     stop=True).then_inc(s_gp, 1)

                def attention(g, i):
                    n = HALF[i][1] * P
                    for h in range(KC):
                        pe.wait_ge(s_gate, 4 * g + 2 * i + h + 1)
                        for k in range(KC):
                            last = nc.tensor.matmul(mix[1 - h][:, 0:n], m_sb[:, k, h * P:(h + 1) * P], xT[i][:, k, :],
                                                    start=(k == 0), stop=(k == KC - 1))
                        last.then_inc(s_at, 1)

                def output(g, i, j):
                    u = HALF[i][0] + j
                    at = j * P
                    b = mix[j % 2]
                    if j == 0:
                        pe.wait_ge(s_prod, 2 * g + i + 2)
                    elif j >= 2:
                        pe.wait_ge(s_copied, g * GT + u - 1 + GT)
                    for k in range(KC):
                        nc.tensor.matmul(b[:, D:2 * D], xT[i][:, k, at:at + P], wself[:, k, :], start=(k == 0), stop=(k == KC - 1))
                    nc.tensor.matmul(b[:, 0:D], c.ident[:], xr[:, u, :], start=True, stop=False)
                    nc.tensor.matmul(b[:, 0:D], c.ones[0:1, :], bproj[:], start=False, stop=False)
                    for k in range(KC):
                        last = nc.tensor.matmul(b[:, 0:D], prod[:, k, at:at + P], wproj[:, k, :], start=False, stop=(k == KC - 1))
                    last.then_inc(s_rows, 1)

                pe.sem_inc(s_mm, 2 * SBLK)
                pe.sem_inc(s_kv, GT)
                pe.sem_inc(s_ctx, 2)
                pe.sem_inc(s_rows, GT)
                pe.wait_ge(s_init, 1)
                nc.tensor.matmul(mix[1][:, 0:KC * CW], zeros[:, 0:P], zeros[:], start=True, stop=False,
                                 skip_group_check=True)
                pe.wait_ge(s_w, 112)
                for k in range(KC):
                    for h in range(KC):
                        last = nc.tensor.transpose(mix[0][:, h * D + k * P:h * D + (k + 1) * P], wqkv[:, k, h * P:(h + 1) * P], c.ident[:])
                last.then_inc(s_wq, 1)
                pe.wait_ge(s_wqc, 1)
                with pe.Fori(0, LANE_PAIRS) as p:
                    pair(p)
                with pe.Fori(0, GROUPS) as g:
                    for u in range(GT + 1):
                        steps(LANE_PAIRS + g, u // 2, u % 2 * 4, u % 2 * 4 + 4)
                        if u < GT:
                            kv(g, u)
                        if u:
                            context(g, u - 1)
                pair(MID_PAIR)
                pe.wait_ge(s_bd, 1)
                for k in range(KC):
                    for h in range(KC):
                        last = nc.tensor.matmul(mix[0][:, k * D + h * P:k * D + (h + 1) * P], wqT[:, h, k * P:(k + 1) * P], ctxbd[:, h, :],
                                                start=True, stop=True)
                last.then_inc(s_m, 1)
                pe.wait_ge(s_msb, 1)
                pe.wait_ge(s_rst[0], 16)
                with pe.Fori(0, GROUPS) as g:
                    srt.turn_from(pe, 0, 2 * g + 1)
                    for i in range(2):
                        p = C_PAIR + 2 * g + i
                        steps(p, 0, 0, 4)
                        hidden(g, i)
                        steps(p, 0, 4, 8)
                        gates(g, i, 0)
                        steps(p, 1, 0, 4)
                        gates(g, i, 1)
                        steps(p, 1, 4, 8)
                        attention(g, i)
                        for j in range(4):
                            steps(p, 2 + j // 2, j % 2 * 4, j % 2 * 4 + 4)
                            if j < HALF[i][1]:
                                output(g, i, j)
                            if i == 0 and j == 2:
                                srt.turn_from(pe, 1, 2 * g + 2)
                pair(R_PAIR)
                srt.turn_from(pe, 0, T_LAST + 1)
                srt.turn_from(pe, 1, T_LAST + 2)
                for k in range(2):
                    steps(R_PAIR + 1, k, 0, SHALF)
                pe.wait_ge(srt.s_ready, T_LAST + 3)
                nc.tensor.transpose(psS[0:NS, 0:P], tail[:], c.ident[:]).then_inc(srt.s_turned, 1)
                pe.wait_ge(srt.s_ready, T_LAST + 4)
                nc.tensor.transpose(psS[:, 0:NS], upper_t[0][:], c.ident[0:NS, 0:NS]).then_inc(srt.s_turned, 1)
                for k in range(2, QUART):
                    steps(R_PAIR + 1, k, 0, SHALF)

            @block.scalar
            def _(act):
                A = nc.scalar

                def prep(p, k):
                    half = QUART * p + k
                    act.drain()
                    act.wait_ge(s_mm, half * SHALF + SHALF)
                    for u in range(SHALF):
                        A.activation(dif[:, u, :], c.iota_row[:], ACT.Abs, bias=t.nloc[:, ds(half * SHALF + u, 1)])
                    act.drain()
                    A.activation(hot[:, k], dif[:], ACT.Relu, bias=c.ones[:, 0:1], scale=-1.0).then_inc(s_hot, 1)

                def taken(g, u):
                    b = u % 2
                    one = valid[:, ds(g * GT + u, 1)]
                    act.wait_ge(s_kv, g * GT + u + 1 + GT)
                    act.wait_ge(s_ctx, g * GT + u + (2 if u == 0 else 1))
                    A.activation(ke[:, b, :], mix[0][:, 0:D], ACT.Exp)
                    A.copy(vm[:, b, :, P:CW], bcast(one, 1, KC))
                    A.activation(vm[:, b, :, 0:P], mix[0][:, D:2 * D].rearrange("p (h d) -> p h d", h=KC), ACT.Copy,
                                 scale=one).then_inc(s_ev, 1)

                def gates(g, i):
                    n = HALF[i][1] * P
                    act.wait_ge(s_hgp, 2 * g + i + 1)
                    A.activation(hg[:, 0:n], mix[0][0:GATE_H, 0:n], ACT.Gelu, bias=bg1[:]).then_inc(s_hg, 1)
                    act.wait_ge(s_prod, 2 * g + i + 1)
                    for h in range(KC):
                        act.wait_ge(s_gp, 4 * g + 2 * i + h + 1)
                        A.activation(gate[:, h, 0:n], mix[1 - h][:, 0:n], ACT.Sigmoid, bias=bg2[:, h:h + 1]).then_inc(s_gate, 1)

                def copied(g, i, j):
                    u = HALF[i][0] + j
                    act.wait_ge(s_rows, g * GT + u + 1 + GT)
                    if j == 0:
                        act.wait_ge(s_rst[i], 16 * g + 16)
                    A.copy(rows[:, u, :], mix[j % 2][:, :]).then_inc(s_copied, 1)

                act.sem_inc(s_ev, 1)
                act.sem_inc(s_copied, GT)
                for k in range(2):
                    prep(0, k)
                act.wait_ge(s_wq, 1)
                A.copy(wqT[:], mix[0][:, :].rearrange("p (h d) -> p h d", h=KC)).then_inc(s_wqc, 1)
                act.wait_ge(s_w, 112)
                def pair(p):
                    for k in range(QUART):
                        prep(p + (k + 2) // QUART, (k + 2) % QUART)

                with act.Fori(0, LANE_PAIRS) as p:
                    pair(p)
                with act.Fori(0, GROUPS) as g:
                    for k in range(QUART):
                        prep(LANE_PAIRS + g + (k + 2) // QUART, (k + 2) % QUART)
                        for u in range(2 * k, min(2 * k + 2, GT)):
                            taken(g, u)
                pair(MID_PAIR)
                act.wait_ge(s_rst[0], 16)
                act.wait_ge(s_rst[1], 16)
                with act.Fori(0, GROUPS) as g:
                    for i, (u0, n) in enumerate(HALF):
                        p = C_PAIR + 2 * g + i
                        prep(p, 2)
                        gates(g, i)
                        prep(p, 3)
                        prep(p + 1, 0)
                        copied(g, i, 0)
                        copied(g, i, 1)
                        prep(p + 1, 1)
                        for j in range(2, n):
                            copied(g, i, j)
                        act.wait_ge(s_copied, g * GT + u0 + n + GT)
                        act.dma_start(rows_v[:, ds(g * GT + u0, n), :], rows[:, u0:u0 + n, :]).then_inc(s_rst[i], 16)
                with act.Fori(R_PAIR, PAIRS - 1) as p:
                    pair(p)
                for k in range(2, QUART):
                    prep(PAIRS - 1, k)
                for i in range(2):
                    act.wait_ge(s_rst[i], 16 * GROUPS + 16)


def gnn_out(c, a, acc, firsts):
    nc = c.nc
    ROWW = D + 1
    ctx, sb, ps = c.open()
    with ctx:
        wneigh = sb("go_wneigh", [P, KC, D])
        wg = sb("go_wg", [P, KC, ROW])
        b_gnn = sb("go_b", [1, D])
        att = sb("go_att", [P, 2, HE])
        prod = sb("go_att_prod", [P, HE])
        rdeg = sb("go_rdeg", [P, TILES])
        hn = sb("go_hn", [P, GT, D])
        hnT = sb("go_hnT", [P, GT, KC, P])
        base = sb("go_base", [P, GT, 2 * D])
        z = sb("go_z", [P, 2, D])
        x2 = sb("go_x2", [P, GT, D])
        y = sb("go_y", [P, GT, D])
        yT = sb("go_yT", [P, KC, GN])
        hx = sb("go_hx", [P, GT, ROW])
        stats = sb("go_stats", [P, GT, 6])
        mv = sb("go_mv", [P, GT, 2])
        std = sb("go_std", [P, GT])
        rstd = sb("go_rstd", [P, GT])
        chunks = sb("go_chunks", [FENCE_P, FENCES // FENCE_P, P], I32)
        first_i = sb("go_first_i", [FENCE_P, FENCES // FENCE_P], I32)
        first_f = sb("go_first_f", [FENCE_P, FENCES // FENCE_P])
        s_chunks, s_first, s_first_st, s_firsts = (c.sem("go_" + n) for n in ("chunks", "first", "first_st", "firsts"))
        first_d = c.dram("go_first_d", [FENCES])
        psT = [ps(f"go_psT{i}", [P, 512]) for i in range(2)]
        psZ = [ps(f"go_psZ{i}", [P, 512]) for i in range(2)]
        psY = [ps(f"go_psY{i}", [P, 512]) for i in range(2)]
        psH = [ps(f"go_psH{i}", [P, 512]) for i in range(2)]
        s_base = [c.sem(f"go_base_in{i}") for i in range(2)]
        s_w, s_wg, s_hn, s_hnT, s_hnc, s_z, s_x2 = (c.sem("go_" + n) for n in (
            "w", "wg", "hn", "hnT", "hnc", "z", "x2"))
        s_mv, s_std, s_y, s_yT, s_yc, s_hx, s_hxc = (c.sem("go_" + n) for n in (
            "mv", "std", "y", "yT", "yc", "hx", "hxc"))
        s_x2st, s_x2free, s_yst, s_yfree, s_hxst, s_hxfree = (c.sem("go_" + n) for n in (
            "x2st", "x2free", "yst", "yfree", "hxst", "hxfree"))
        base_v = c.base_d.rearrange("(t p) d -> p t d", p=P)
        x2_v = c.x2_d.rearrange("(t p) d -> p t d", p=P)
        hx_v = c.hx_d.rearrange("(t p) d -> p t d", p=P)
        acc_v = acc[:].rearrange("p (t d) -> p t d", t=TILES)

        def slot(g, u):
            return g * GT + u + (2 if u == 0 else 1)

        with nc.Block() as block:
            @block.sync
            def _(sp):
                sp.dma_start(chunks[:], c.skey_gat[P:P + GAT_N].rearrange("(p w e) -> p w e", p=FENCE_P, e=P).bitcast(I32)).then_inc(s_chunks, 16)
                sp.dma_start(wneigh[:], a["wneigh"].rearrange("(k p) n -> p k n", p=P)).then_inc(s_w, 16)
                sp.dma_start(wg[:, :, 0:HE], a["w_gat"].rearrange("(k p) n -> p k n", p=P)).then_inc(s_w, 16)
                sp.dma_start(b_gnn[:], a["b_gnn"]).then_inc(s_w, 16)
                sp.dma_start(att[:, 0, :], a["att_src"].to_broadcast([P, HE])).then_inc(s_w, 16)
                sp.dma_start(att[:, 1, :], a["att_dst"].to_broadcast([P, HE])).then_inc(s_w, 16)
                with sp.Fori(0, GROUPS) as g:
                    for i, (u0, n) in enumerate(HALF):
                        sp.wait_ge(s_x2, g * GT + u0 + n)
                        sp.dma_start(base[:, u0:u0 + n, :], base_v[:, ds(g * GT + u0, n), :]).then_inc(s_base[i], 16)

            @block.gpsimd
            def _(pool):
                pool.sem_inc(s_x2free, 2)
                pool.sem_inc(s_yfree, 1)
                pool.sem_inc(s_hxfree, 1)
                pool.wait_ge(s_first, 1)
                pool.dma_start(first_d.rearrange("(p w) -> p w", p=FENCE_P), first_f[:]).then_inc(s_first_st, 16)
                pool.wait_ge(s_first_st, 16)
                pool.dma_start(firsts[:], first_d.rearrange("(o n) -> o n", o=1).to_broadcast([P, FENCES])).then_inc(s_firsts, 16)
                with pool.Fori(0, GROUPS) as g:
                    for i, (u0, n) in enumerate(HALF):
                        pool.wait_ge(s_x2, g * GT + u0 + n + GT)
                        pool.dma_start(x2_v[:, ds(g * GT + u0, n), :], x2[:, u0:u0 + n, :]).then_inc(s_x2st, 16)
                        pool.wait_ge(s_x2st, 32 * g + 16 * i + 16)
                        pool.sem_inc(s_x2free, 1)
                    pool.wait_ge(s_yc, g * GT + GT + 2)
                    pool.dma_start(c.x2nT_d[:, :, ds(g * GN, GN)], yT[:]).then_inc(s_yst, 16)
                    pool.wait_ge(s_hxc, g * GT + GT + 2)
                    pool.dma_start(hx_v[:, ds(g * GT, GT), :], hx[:]).then_inc(s_hxst, 16)
                    pool.wait_ge(s_yst, 16 * g + 16)
                    pool.sem_inc(s_yfree, 1)
                    pool.wait_ge(s_hxst, 16 * g + 16)
                    pool.sem_inc(s_hxfree, 1)
                pool.wait_ge(s_firsts, 16)

            @block.vector
            def _(v):
                v.sem_inc(s_x2, GT)
                nc.vector.tensor_scalar(rdeg[:], acc_v[:, :, D], 1.0, None, ALU.max)
                v.drain()
                nc.vector.reciprocal(rdeg[:], rdeg[:])
                v.wait_ge(s_w, 80)
                for i in range(2):
                    for k in range(KC):
                        nc.vector.tensor_tensor(prod[:], wg[:, k, 0:HE], att[:, i, :], ALU.mult)
                        v.drain()
                        last = nc.vector.tensor_reduce(wg[:, k, HE + i * HEADS:HE + (i + 1) * HEADS],
                                                       prod[:].rearrange("p (h e) -> p h e", h=HEADS), AX_X, ALU.add)
                        v.drain()
                v.sem_inc(s_wg, 1)
                v.wait_ge(s_chunks, 16)
                nc.vector.tensor_scalar(first_i[:], chunks[:, :, 0], SRC_BITS, DST_MASK, ALU.logical_shift_right, ALU.bitwise_and)
                v.drain()
                nc.vector.tensor_copy(first_f[:], first_i[:]).then_inc(s_first, 1)

                def means(g):
                    v.wait_ge(s_hnT, g * GT + 2)
                    for u in range(GT):
                        at = g * GT + u
                        nc.vector.tensor_scalar(hn[:, u, :], acc[:, ds(at * ROWW, D)], rdeg[:, ds(at, 1)], None,
                                                ALU.mult).then_inc(s_hn, 1)

                def group(g, last):
                    for u in range(GT):
                        for i, (u0, n) in enumerate(HALF):
                            if u == u0:
                                v.wait_ge(s_base[i], 16 * g + 16)
                                v.wait_ge(s_x2free, 2 * g + i + 1)
                        v.wait_ge(s_z, g * GT + u + 1 + GT)
                        nc.vector.tensor_tensor(z[:, u % 2, :], psZ[u % 2][:, 0:D], base[:, u, D:2 * D], ALU.add)
                        v.drain()
                        nc.vector.scalar_tensor_tensor(x2[:, u, :], z[:, u % 2, :], 0.0, base[:, u, 0:D], ALU.max,
                                                       ALU.add).then_inc(s_x2, 1)
                        v.drain()
                        nc.vector.bn_stats(stats[:, u, :], x2[:, u, :])
                    v.drain()
                    for u in range(GT):
                        agg = nc.vector.bn_aggr(mv[:, u, :], stats[:, u, :])
                    agg.then_inc(s_mv, 1)
                    if not last:
                        means(g + 1)
                    v.wait_ge(s_std, g + 1)
                    nc.vector.reciprocal(rstd[:], std[:])
                    v.drain()
                    v.wait_ge(s_yT, g * GT + 2)
                    for u in range(GT):
                        nc.vector.tensor_scalar(y[:, u, :], x2[:, u, :], mv[:, u, 0:1], rstd[:, u:u + 1],
                                                ALU.subtract, ALU.mult).then_inc(s_y, 1)
                    v.drain()

                means(0)
                with v.Fori(0, GROUPS - 1) as g:
                    group(g, False)
                group(GROUPS - 1, True)

            @block.scalar
            def _(act):
                act.sem_inc(s_hnc, 2)
                act.sem_inc(s_yc, 2)
                act.sem_inc(s_hxc, 2)
                def mean_out(g, u):
                    act.wait_ge(s_hnT, g * GT + u + 3)
                    act.wait_ge(s_z, g * GT + u + 1)
                    nc.scalar.copy(hnT[:, u], psT[u % 2][:, 0:D].rearrange("p (k n) -> p k n", k=KC)).then_inc(s_hnc, 1)

                def y_out(g, u):
                    if u == 0:
                        act.wait_ge(s_yfree, g + 1)
                        act.wait_ge(s_hxfree, g + 1)
                    act.wait_ge(s_yT, g * GT + u + 3)
                    nc.scalar.copy(yT[:, :, u * P:(u + 1) * P],
                                   psY[u % 2][:, 0:D].rearrange("p (k n) -> p k n", k=KC)).then_inc(s_yc, 1)

                def hx_out(g, u):
                    act.wait_ge(s_hx, g * GT + u + 1)
                    nc.scalar.copy(hx[:, u, :], psH[u % 2][:, 0:ROW]).then_inc(s_hxc, 1)

                def root(g):
                    act.wait_ge(s_mv, g + 1)
                    nc.scalar.activation(std[:], mv[:, :, 1], ACT.Sqrt, bias=c.eps[:]).then_inc(s_std, 1)

                for u in range(GT):
                    mean_out(0, u)
                root(0)
                with act.Fori(1, GROUPS) as g:
                    for u in range(GT):
                        mean_out(g, u)
                        y_out(g - 1, u)
                        if u:
                            hx_out(g - 1, u - 1)
                    hx_out(g - 1, GT - 1)
                    root(g)
                for u in range(GT):
                    y_out(GROUPS - 1, u)
                    if u:
                        hx_out(GROUPS - 1, u - 1)
                hx_out(GROUPS - 1, GT - 1)

            @block.tensor
            def _(pe):
                pe.sem_inc(s_hnT, 2)
                pe.sem_inc(s_z, GT)
                pe.sem_inc(s_yT, 2)
                pe.wait_ge(s_wg, 1)

                def turn_mean(g, u):
                    pe.wait_ge(s_hn, g * GT + u + 1)
                    pe.wait_ge(s_hnc, slot(g, u))
                    for k in range(KC):
                        last = nc.tensor.transpose(psT[u % 2][:, k * P:(k + 1) * P], hn[:, u, k * P:(k + 1) * P], c.ident[:])
                    last.then_inc(s_hnT, 1)

                def rows_of(g, u):
                    pe.wait_ge(s_yc, g * GT + u + 3)
                    pe.wait_ge(s_hxc, slot(g, u))
                    for k in range(KC):
                        last = nc.tensor.matmul(psH[u % 2][:, 0:ROW], yT[:, k, u * P:(u + 1) * P], wg[:, k, :],
                                                start=(k == 0), stop=(k == KC - 1))
                    last.then_inc(s_hx, 1)

                def neighbours(g, u):
                    pe.wait_ge(s_hnc, g * GT + u + 3)
                    pe.wait_ge(s_x2, slot(g, u) + GT - 2)
                    nc.tensor.matmul(psZ[u % 2][:, 0:D], c.ones[0:1, :], b_gnn[:], start=True, stop=False)
                    for k in range(KC):
                        last = nc.tensor.matmul(psZ[u % 2][:, 0:D], hnT[:, u, k, :], wneigh[:, k, :],
                                                start=False, stop=(k == KC - 1))
                    last.then_inc(s_z, 1)

                def turn_y(g, u):
                    pe.wait_ge(s_y, g * GT + u + 1)
                    pe.wait_ge(s_yc, slot(g, u))
                    for k in range(KC):
                        last = nc.tensor.transpose(psY[u % 2][:, k * P:(k + 1) * P], y[:, u, k * P:(k + 1) * P], c.ident[:])
                    last.then_inc(s_yT, 1)

                def both(first, second):
                    if first is not None:
                        turn_mean(first, 0)
                        turn_mean(first, 1)
                    for u in range(GT):
                        if first is not None and u + 2 < GT:
                            turn_mean(first, u + 2)
                        if second is not None:
                            turn_y(second, u)
                        if first is not None:
                            neighbours(first, u)
                        if second is not None and u:
                            rows_of(second, u - 1)
                    if second is not None:
                        rows_of(second, GT - 1)

                both(0, None)
                with pe.Fori(1, GROUPS) as g:
                    both(g, g - 1)
                both(None, GROUPS - 1)


def load_lanes(eng, wide, to, keys, sem):
    with eng.If(wide > 0):
        eng.dma_start(to, keys.rearrange("(p w) -> p w", p=P).bitcast(I32)).then_inc(sem, 16)
    with eng.If(wide < 1):
        eng.dma_start(to[:, 0:W_LOW], keys[0:P * W_LOW].rearrange("(p w) -> p w", p=P).bitcast(I32)).then_inc(sem, 16)


def gat_gather_experts(c, a, G, firsts, reach, width, gap):
    nc = c.nc
    FB, YB = 4, 4
    ctx, sb, ps = c.open()
    with ctx:
        keys = sb("gg_keys", [P, W], I32)
        num_i = sb("gg_num_i", [P, W], I32)
        src_f = sb("gg_src_f", [P, W])
        dst_f = sb("gg_dst_f", [P, W])
        self_f = sb("gg_self_f", [P, W])
        idx = sb("gg_idx", [P, W + SBLK], I32)
        ring = sb("gg_ring", [P, 2, SHALF, ROW])
        ixs = sb("gg_ixs", [P, 2, SHALF], I32)
        tick = sb("gg_tick", [P, 2])
        probe = sb("gg_probe", [P, 1], I32)
        wide_f = sb("gg_wide_f", [P, 1])
        s_probe, s_wide, s_blank = c.sem("gg_probe"), c.sem("gg_wide"), c.sem("gg_blank")
        s_keys, s_ix, s_tick = c.sem("gg_keys_in"), c.sem("gg_ix"), c.sem("gg_tick_done")
        s_g = [c.sem(f"gg_rows{h}") for h in range(2)]
        node_i = num_i[:, 0:G_ITERS]
        node_f = self_f[:, 0:G_ITERS]
        reached = dst_f
        s_free, s_node = c.sem("gg_free"), c.sem("gg_node")

        w1 = sb("ex_w1", [P, EXPERTS, KC, HID])
        w2 = sb("ex_w2", [P, EXPERTS, HC, D])
        b1 = sb("ex_b1", [P, EXPERTS * HC])
        yT = sb("ex_yT", [P, KC, GN])
        hh = sb("ex_hh", [P, HC, 2, GN // 2])
        yo = sb("ex_yo", [P, GT, D])
        psF = [ps(f"ex_psF{i}", [P, 512]) for i in range(FB)]
        psY = [ps(f"ex_psY{i}", [P, 512]) for i in range(YB)]
        s_w, s_yT, s_f, s_ge, s_s, s_yc, s_yst, s_yfree = (c.sem("ex_" + n) for n in (
            "w", "yT", "f", "ge", "s", "yc", "yst", "yfree"))
        NF, NS = 2 * HC, GT
        with nc.Block() as block:
            @block.sync
            def _(sp):
                at = P + P * W_LOW
                sp.dma_start(probe[:], c.skey_gat[at:at + 1].rearrange("(o n) -> o n", o=1).to_broadcast([P, 1]).bitcast(I32)).then_inc(s_probe, 16)
                sp.wait_ge(s_wide, 1)
                wide = sp.value_load(width[0:1, 0:1], min_val=0, max_val=1)
                load_lanes(sp, wide, keys[:], c.skey_gat[P:P + GAT_N], s_keys)
                for e in range(EXPERTS):
                    sp.dma_start(w1[:, e], a["w1"][e].rearrange("(k p) n -> p k n", p=P)).then_inc(s_w, 16)
                    sp.dma_start(w2[:, e], a["w2"][e].rearrange("(k p) n -> p k n", p=P)).then_inc(s_w, 16)
                sp.dma_start(b1[:], a["b1"]).then_inc(s_w, 16)
                sp.sem_inc(s_yfree, 1)
                with sp.Fori(0, GROUPS) as g:
                    sp.wait_ge(s_f, g * EXPERTS * NF + 1)
                    sp.dma_start(yT[:], c.x2nT_d[:, :, ds(g * GN, GN)]).then_inc(s_yT, 16)
                    for e in range(EXPERTS):
                        n = g * EXPERTS + e
                        sp.wait_ge(s_yc, n * NS + NS + YB)
                        sp.dma_start(c.y_d[e].rearrange("(t p) d -> p t d", p=P)[:, ds(g * GT, GT), :], yo[:]).then_inc(s_yst, 16)
                        sp.wait_ge(s_yst, 16 * n + 16)
                        sp.sem_inc(s_yfree, 1)

            @block.gpsimd
            def _(pool):
                pool.wait_ge(s_free, 1)
                nc.gpsimd.iota(node_i, pattern=[[P, G_ITERS]], base=0, channel_multiplier=1).then_inc(s_node, 1)

                def gathers(first, end):
                    with pool.Fori(first, end) as b:
                        for h in range(2):
                            pool.wait_ge(s_ix, 2 * b + h + 1)
                            nc.gpsimd.tensor_tensor(tick[:, h:h + 1], c.eps[:], c.eps[:], ALU.add).then_inc(s_tick, 1)
                            for u in range(SHALF):
                                pool.indirect_dma_start(ring[:, h, u, :], None, c.hx_d,
                                                        bass.IndirectOffsetOnAxis(ap=ixs[:, h, u:u + 1], axis=0)).then_inc(s_g[h], 16)

                gathers(0, LOW_ITERS)
                with pool.If(pool.value_load(width[0:1, 0:1], min_val=0, max_val=1) > 0):
                    gathers(LOW_ITERS, G_ITERS)

            @block.vector
            def _(v):
                v.wait_ge(s_probe, 16)
                nc.vector.tensor_scalar(probe[:], probe[:], SRC_BITS, DST_MASK, ALU.logical_shift_right, ALU.bitwise_and)
                nc.vector.memset(idx[:, W:W + SBLK], 0)
                nc.vector.memset(keys[:, W_LOW:W], 0)
                v.drain()
                nc.vector.tensor_scalar(wide_f[:], probe[:], float(N_NODES), None, ALU.is_lt)
                v.drain()
                nc.vector.tensor_copy(width[:, 0:1], wide_f[:])
                nc.vector.tensor_scalar(width[:, 1:2], wide_f[:], float(W - W_LOW), float(W_LOW - 1), ALU.mult, ALU.add)
                nc.vector.tensor_scalar(gap[:], wide_f[:], -float(W - W_LOW), float(W - W_LOW), ALU.mult, ALU.add)
                v.drain()
                v.sem_inc(s_wide, 1)
                v.wait_ge(s_wide, 1)
                wide = v.value_load(width[0:1, 0:1], min_val=0, max_val=1)
                v.wait_ge(s_keys, 16)
                nc.vector.tensor_scalar(num_i[:], keys[:], SELF, None, ALU.bitwise_and)
                nc.vector.tensor_scalar(keys[:], keys[:], SRC_BITS, DST_MASK, ALU.logical_shift_right, ALU.bitwise_and)
                v.drain()
                nc.vector.tensor_copy(src_f[:], num_i[:])
                nc.vector.tensor_copy(dst_f[:], keys[:])
                v.drain()
                nc.vector.tensor_scalar(self_f[:], src_f[:], float(SELF), None, ALU.is_equal)
                v.drain()
                nc.vector.tensor_tensor(dst_f[:], dst_f[:], src_f[:], ALU.subtract)
                v.drain()
                nc.vector.tensor_tensor(dst_f[:], dst_f[:], self_f[:], ALU.mult)
                v.drain()
                nc.vector.tensor_tensor(src_f[:], src_f[:], dst_f[:], ALU.add)
                v.drain()
                nc.vector.tensor_scalar(idx[:, 0:W], src_f[:], float(N_NODES - 1), None, ALU.min)
                v.drain()
                v.sem_inc(s_free, 1)
                for h in range(2):
                    nc.vector.tensor_copy(ixs[:, h, :], idx[:, h * SHALF:(h + 1) * SHALF]).then_inc(s_ix, 1)
                v.wait_ge(s_node, 1)
                nc.vector.tensor_copy(node_f, node_i)
                nc.vector.memset(G[:, W_LOW:W, :], 0.0)
                v.drain()
                nc.vector.memset(G[:, W_LOW:W, HE:HE + HEADS], -BIG)
                v.drain()

                def take(b, h):
                    v.wait_ge(s_tick, 2 * b + h + 1)
                    v.wait_ge(s_g[h], 16 * SHALF * b + 16 * SHALF)
                    nc.vector.tensor_copy(G[:, ds(b * SBLK + h * SHALF, SHALF), :], ring[:, h])
                    nc.vector.tensor_copy(ixs[:, h, :], idx[:, ds(b * SBLK + h * SHALF + SBLK, SHALF)]).then_inc(s_ix, 1)

                with v.Fori(0, LOW_ITERS) as b:
                    nc.vector.tensor_scalar(reached[:], firsts[:], node_f[:, ds(b, 1)], None, ALU.is_le, ALU.add,
                                            accum_out=reach[:, ds(b, 1)])
                    v.drain()
                    for h in range(2):
                        take(b, h)
                v.drain()
                with v.If(wide > 0):
                    with v.Fori(LOW_ITERS, G_ITERS) as b:
                        for h in range(2):
                            take(b, h)

            @block.tensor
            def _(pe):
                pe.sem_inc(s_s, 1)
                pe.sem_inc(s_f, 1)
                pe.wait_ge(s_w, 144)

                def first(g, e):
                    for i in range(NF):
                        n = (g * EXPERTS + e) * NF + i
                        pe.wait_ge(s_ge, n + 1)
                        for k in range(KC):
                            last = nc.tensor.matmul(psF[i % FB][:, 0:HB], w1[:, e, k, (i // 2) * P:(i // 2 + 1) * P],
                                                    yT[:, k, (i % 2) * HB:(i % 2 + 1) * HB], start=(k == 0), stop=(k == KC - 1))
                        last.then_inc(s_f, 1)

                def second(g, e):
                    pe.wait_ge(s_ge, (g * EXPERTS + e) * NF + NF + FB)
                    for u in range(NS):
                        n = (g * EXPERTS + e) * NS + u
                        bank = psY[(e * NS + u) % YB]
                        pe.wait_ge(s_yc, n + 1)
                        for k in range(HC):
                            last = nc.tensor.matmul(bank[:, 0:D], hh[:, k].rearrange("p a b -> p (a b)")[:, u * P:(u + 1) * P],
                                                    w2[:, e, k, :], start=(k == 0), stop=(k == HC - 1))
                        last.then_inc(s_s, 1)

                with pe.Fori(0, GROUPS) as g:
                    pe.wait_ge(s_yT, 16 * g + 16)
                    for e in range(EXPERTS):
                        first(g, e)
                        second(g, e)

            @block.scalar
            def _(act):
                act.sem_inc(s_ge, FB)
                act.sem_inc(s_yc, YB)
                act.wait_ge(s_w, 144)
                with act.Fori(0, GROUPS) as g:
                    for e in range(EXPERTS):
                        n = g * EXPERTS + e
                        act.wait_ge(s_s, n * NS + 1)
                        for i in range(NF):
                            act.wait_ge(s_f, n * NF + i + 2)
                            nc.scalar.activation(hh[:, i // 2, i % 2, :], psF[i % FB][:, 0:HB], ACT.Gelu,
                                                 bias=b1[:, e * HC + i // 2:e * HC + i // 2 + 1]).then_inc(s_ge, 1)
                        act.wait_ge(s_yfree, n + 1)
                        for u in range(NS):
                            act.wait_ge(s_s, n * NS + u + 2)
                            nc.scalar.copy(yo[:, u, :], psY[(e * NS + u) % YB][:, 0:D]).then_inc(s_yc, 1)


def gat_softmax(c, a, out, G, reach, width, gap):
    nc = c.nc
    NV = HE + HEADS
    ctx, sb, ps = c.open()
    with ctx:
        start = sb("gs2_start", [P, W])
        keep = sb("gs2_keep", [P, W])
        other = sb("gs2_other", [P, W])
        selfm = sb("gs2_self", [P, W])
        pen = sb("gs2_pen", [P, W])
        keys = pen[:].bitcast(I32)
        top = sb("gs2_top", [P, W, HEADS])
        dlog = sb("gs2_dlog", [P, W, HEADS])
        lanes = sb("gs2_lanes", [P, 2, NV])
        turned = sb("gs2_turned", [NV, 2, P])
        chain = sb("gs2_chain", [NV, P + 2])
        carry = sb("gs2_carry", [P, NV])
        node_i = sb("gs2_node_i", [P, TILES], I32)
        chunk_i = sb("gs2_chunk_i", [P, TILES], I32)
        ends = sb("gs2_ends", [P, TILES, P])
        place = sb("gs2_place", [P, TILES])
        endpos = sb("gs2_endpos", [P, TILES], I32)
        s_node, s_chunk, s_ends, s_endpos = (c.sem("gs2_" + n) for n in ("node", "chunk", "ends", "endpos"))
        num = sb("gs2_num", [P, TILES, ROW])
        den = sb("gs2_den", [P, TILES, HEADS])
        par = sb("gs2_par", [P, 3, HE])
        dev = sb("gs2_dev", [P, TILES, HE])
        sq = sb("gs2_sq", [P, TILES, HE])
        mu = sb("gs2_mu", [P, TILES])
        var = sb("gs2_var", [P, TILES])
        score = sb("gs2_score", [P, TILES, EXPERTS])
        wins = sb("gs2_wins", [P, TILES])
        rank = sb("gs2_rank", [P, TILES, EXPERTS])
        gates = sb("gs2_gates", [P, TILES, EXPERTS])
        lane = sb("gs2_lane", [P, TILES])
        wd = sb("gs2_wd", [P, 1])
        bound = sb("gs2_bound", [P, P])
        ps_in = ps("gs2_ps_in", [P, 512])
        ps_out = ps("gs2_ps_out", [P, 512])
        s_in, s_lanes, s_turned, s_chain, s_back, s_exp_in, s_exp, s_done, s_st, s_num, s_std, s_stored, s_blank, s_hotp, s_hotT, s_sel = (c.sem("gs2_" + n) for n in (
            "in", "lanes", "turned", "chain", "back", "exp_in", "exp", "done", "st", "num", "std", "stored", "blank",
            "hotp", "hotT", "sel"))
        prev = top[:].rearrange("p w h -> p (w h)")[:, 0:W].bitcast(I32)
        fix = top[:].rearrange("p w h -> p (w h)")[:, 0:TILES * NV].rearrange("p (t r) -> p t r", r=NV)
        zero = dlog[:].rearrange("p w h -> p (w h)")[:, 0:W]
        widths = (HEADS, 2 * HEADS, NV)
        parts = [W_LOW * i // 3 for i in range(4)] + [W]

        G_v = G[:].rearrange("p w r -> p (w r)")
        NB, SIZE = 2, (EXPERTS + 1) * GT * D
        buf = [G_v[:, i * SIZE:(i + 1) * SIZE].rearrange("p (e t d) -> p e t d", e=EXPERTS + 1, t=GT) for i in range(NB)]
        b2 = sb("co_b2", [EXPERTS, D])
        gT = dlog[:].rearrange("p w h -> p (w h)")[0:EXPERTS, 0:GN]
        ps_gT = ps("co_ps_gT", [P, 1024])
        ps_b = ps("co_ps_b", [P, 2048])
        s_gTp, s_gT, s_bias, s_sum, s_out = (c.sem("co_" + n) for n in ("gTp", "gT", "bias", "sum", "out"))
        s_load = [c.sem(f"co_in{i}") for i in range(NB)]
        x2_v = c.x2_d.rearrange("(t p) d -> p t d", p=P)
        y_v = [c.y_d[e].rearrange("(t p) d -> p t d", p=P) for e in range(EXPERTS)]
        out_v = out.rearrange("(t p) d -> p t d", p=P)

        BATCHES = -(-TILES // 4)
        PER = 512 // NV

        def sel(t):
            at = t // PER * 512 + t % PER * NV
            return ps_b[:, at:at + NV]

        with nc.Block() as block:
            @block.sync
            def _(sp):
                wide = sp.value_load(width[0:1, 0:1], min_val=0, max_val=1)
                sums_v = c.sums_d.rearrange("(p w) r -> p w r", p=P)
                sp.dma_start(sums_v[:, W_LOW:W, :], G[:, W_LOW:W, :]).then_inc(s_st, 16)
                sp.wait_ge(s_blank, 1)
                load_lanes(sp, wide, keys, c.skey_gat[P:P + GAT_N], s_in)
                load_lanes(sp, wide, prev, c.skey_gat[P - 1:P + GAT_N - 1], s_in)
                sp.dma_start(b2[:], a["b2"]).then_inc(s_in, 16)
                for i, name in enumerate(("b_gat", "gamma", "beta")):
                    sp.dma_start(par[:, i, :], a[name].to_broadcast([P, HE])).then_inc(s_in, 16)
                for i in range(3):
                    sp.wait_ge(s_done, i + 1)
                    sp.dma_start(sums_v[:, parts[i]:parts[i + 1], :], G[:, parts[i]:parts[i + 1], :]).then_inc(s_st, 16)
                with sp.If(wide > 0):
                    sp.wait_ge(s_done, 4)
                    sp.dma_start(sums_v[:, W_LOW:W, :], G[:, W_LOW:W, :]).then_inc(s_st, 16)
                    sp.wait_ge(s_st, 80)
                sp.wait_ge(s_st, 64)
                sp.wait_ge(s_lanes, 3)
                sp.sem_inc(s_stored, 1)
                for g in range(GROUPS):
                    if g >= NB:
                        sp.wait_ge(s_out, 16 * (g - NB + 1))
                    at = slice(g * GT, (g + 1) * GT)
                    sp.dma_start(buf[g % NB][:, EXPERTS], x2_v[:, at, :]).then_inc(s_load[g % NB], 16)
                    for e in range(EXPERTS):
                        sp.dma_start(buf[g % NB][:, e], y_v[e][:, at, :]).then_inc(s_load[g % NB], 16)

            @block.gpsimd
            def _(pool):
                nc.gpsimd.iota(node_i[:], pattern=[[P, TILES]], base=0, channel_multiplier=1).then_inc(s_node, 1)
                pool.wait_ge(s_chunk, 1)
                for t in range(TILES):
                    pool.indirect_dma_start(ends[:, t, :], None, c.skey_gat.rearrange("(c e) -> c e", e=P),
                                            bass.IndirectOffsetOnAxis(ap=chunk_i[:, t:t + 1], axis=0)).then_inc(s_ends, 16)
                pool.wait_ge(s_endpos, 1)
                pool.wait_ge(s_stored, 1)
                for t in range(TILES):
                    pool.indirect_dma_start(num[:, t, :], None, c.sums_d,
                                            bass.IndirectOffsetOnAxis(ap=endpos[:, t:t + 1], axis=0)).then_inc(s_num, 16)

            @block.tensor
            def _(pe):
                for r, n in enumerate(widths):
                    pe.wait_ge(s_lanes, r + 1)
                    for i in range(2):
                        last = nc.tensor.transpose(ps_in[0:n, i * P:(i + 1) * P], lanes[:, i, 0:n], c.ident[:])
                    last.then_inc(s_turned, 1)
                    pe.wait_ge(s_chain, r + 1)
                    nc.tensor.transpose(ps_out[:, 0:n], chain[0:n, 0:P] if r != 1 else chain[0:n, 2:P + 2],
                                        c.ident[0:n, 0:n]).then_inc(s_back, 1)
                pe.wait_ge(s_endpos, 2)
                for b in range(BATCHES):
                    if b >= 2:
                        pe.wait_ge(s_hotT, b - 1)
                    for t in range(4 * b, min(4 * b + 4, TILES)):
                        last = nc.tensor.transpose(ps_gT[:, b % 2 * 512 + t % 4 * P:b % 2 * 512 + (t % 4 + 1) * P], ends[:, t, :], c.ident[:])
                    last.then_inc(s_hotp, 1)
                pe.wait_ge(s_hotT, BATCHES)
                for t in range(TILES):
                    last = nc.tensor.matmul(sel(t), ends[:, t, :], carry[:], start=True, stop=True)
                last.then_inc(s_sel, 1)
                pe.wait_ge(s_in, 96)
                pe.wait_ge(s_exp_in, 3)
                for g in range(GROUPS):
                    if g:
                        pe.wait_ge(s_gT, g)
                    for u in range(GT):
                        last = nc.tensor.transpose(ps_gT[0:EXPERTS, u * P:(u + 1) * P], gates[:, g * GT + u, :], c.ident[:])
                    last.then_inc(s_gTp, 1)
                    pe.wait_ge(s_gT, g + 1)
                    if g:
                        pe.wait_ge(s_sum, g)
                    for u in range(GT):
                        last = nc.tensor.matmul(ps_b[:, u * D:(u + 1) * D], gT[:, u * P:(u + 1) * P], b2[:], start=True, stop=True)
                    last.then_inc(s_bias, 1)

            @block.scalar
            def _(act):
                act.wait_ge(s_exp_in, 1)
                nc.scalar.activation(top[:], top[:], ACT.Exp).then_inc(s_exp, 1)
                for b in range(BATCHES):
                    act.wait_ge(s_hotp, b + 1)
                    n = min(4, TILES - 4 * b)
                    nc.scalar.copy(ends[:, 4 * b:4 * b + n, :].rearrange("p t l -> p (t l)"),
                                   ps_gT[:, b % 2 * 512:b % 2 * 512 + n * P]).then_inc(s_hotT, 1)
                act.wait_ge(s_std, 1)
                nc.scalar.activation(var[:], var[:], ACT.Sqrt, bias=c.eps[:], scale=1.0 / HE).then_inc(s_std, 1)
                act.wait_ge(s_exp_in, 2)
                nc.scalar.activation(score[:], score[:], ACT.Exp).then_inc(s_exp, 1)
                for g in range(GROUPS):
                    act.wait_ge(s_gTp, g + 1)
                    nc.scalar.copy(gT, ps_gT[0:EXPERTS, 0:GN]).then_inc(s_gT, 1)
                    act.wait_ge(s_sum, g + 1)
                    act.dma_start(out_v[:, g * GT:(g + 1) * GT, :], buf[g % NB][:, EXPERTS]).then_inc(s_out, 16)
                    act.wait_ge(s_out, 16 * (g + 1))

            @block.vector
            def _(v):
                V = nc.vector

                def carries(r, op0, op1, first, backward=False):
                    n = widths[r]
                    v.drain()
                    v.sem_inc(s_lanes, 1)
                    v.wait_ge(s_turned, r + 1)
                    V.tensor_copy(turned[0:n].rearrange("p a b -> p (a b)"), ps_in[0:n, 0:2 * P])
                    V.memset(chain[:, 0:1] if not backward else chain[:, P + 1:P + 2], first)
                    v.drain()
                    flags, vals = turned[0:n, 0, :], turned[0:n, 1, :]
                    if backward:
                        V.tensor_tensor_scan(chain[0:n, 1:P + 1][:, ::-1], flags[:, ::-1], vals[:, ::-1], first, op0, op1)
                    else:
                        V.tensor_tensor_scan(chain[0:n, 1:P + 1], flags, vals, first, op0, op1)
                    v.drain()
                    v.sem_inc(s_chain, 1)
                    v.wait_ge(s_back, r + 1)
                    V.tensor_copy(carry[:, 0:n], ps_out[:, 0:n])
                    v.drain()

                V.memset(keys[:, W_LOW:W], 0)
                V.memset(prev[:, W_LOW:W], 0).then_inc(s_blank, 1)
                wide = v.value_load(width[0:1, 0:1], min_val=0, max_val=1)
                last = v.value_load(width[0:1, 1:2], min_val=W_LOW - 1, max_val=W - 1)
                V.tensor_scalar(wd[:], gap[:], -1.0, float(W), ALU.mult, ALU.add)
                v.drain()
                V.tensor_scalar(bound[:], c.iota_row[:], wd[:], None, ALU.mult)
                V.tensor_copy(chunk_i[:], reach[:, 0:TILES]).then_inc(s_chunk, 1)
                v.wait_ge(s_node, 1)
                V.tensor_scalar(node_i[:], node_i[:], SRC_BITS, OFF | SELF, ALU.logical_shift_left, ALU.bitwise_or)
                v.wait_ge(s_in, 96)
                V.tensor_scalar(selfm[:].bitcast(I32), keys, SELF, None, ALU.bitwise_and)
                V.tensor_scalar(keys, keys, SRC_BITS, None, ALU.logical_shift_right)
                V.tensor_scalar(prev, prev, SRC_BITS, None, ALU.logical_shift_right)
                v.drain()
                V.tensor_copy(start[:], keys)
                V.tensor_copy(keep[:], prev)
                V.tensor_copy(other[:], selfm[:].bitcast(I32))
                v.drain()
                V.tensor_tensor(keep[:], start[:], keep[:], ALU.is_equal)
                V.tensor_scalar(selfm[:], other[:], float(SELF), None, ALU.is_equal)
                v.drain()
                V.tensor_scalar(other[:], selfm[:], -1.0, 1.0, ALU.mult, ALU.add)
                V.tensor_scalar(start[:], keep[:], BIG, -BIG, ALU.mult, ALU.add)
                V.memset(zero, 0.0)
                v.drain()

                for h in range(HEADS):
                    V.tensor_tensor_scan(top[:, :, h], start[:], G[:, :, HE + h], -BIG, ALU.add, ALU.max)
                V.tensor_tensor_scan(pen[:], start[:], zero, 0.0, ALU.min, ALU.add)
                v.drain()
                V.tensor_copy(lanes[:, 0, 0:HEADS], pen[:, ds(last, 1)].to_broadcast([P, HEADS]))
                V.tensor_copy(lanes[:, 1, 0:HEADS], top[:, ds(last, 1), :].rearrange("p o h -> p (o h)"))
                carries(0, ALU.add, ALU.max, -BIG)
                for h in range(HEADS):
                    V.scalar_tensor_tensor(top[:, :, h], pen[:], carry[:, h:h + 1], top[:, :, h], ALU.add, ALU.max)
                v.drain()

                V.tensor_tensor(top[:], top[:], bcast(selfm[:], 2, HEADS), ALU.mult)
                V.tensor_tensor(dlog[:], G[:, :, HE + HEADS:ROW], bcast(selfm[:], 2, HEADS), ALU.mult)
                V.memset(pen[:], 0.0)
                v.drain()
                V.tensor_tensor_scan(start[:, ::-1], other[:, ::-1], pen[:, ::-1], 1.0, ALU.mult, ALU.add)
                for t in (top, dlog):
                    for h in range(HEADS):
                        V.tensor_tensor_scan(t[:, ::-1, h], other[:, ::-1], t[:, ::-1, h], 0.0, ALU.mult, ALU.add)
                v.drain()
                V.tensor_copy(lanes[:, 0, 0:2 * HEADS], bcast(start[:, 0], 1, 2 * HEADS))
                V.tensor_copy(lanes[:, 1, 0:HEADS], top[:, 0, :])
                V.tensor_copy(lanes[:, 1, HEADS:2 * HEADS], dlog[:, 0, :])
                carries(1, ALU.mult, ALU.add, 0.0, backward=True)
                for i, t in enumerate((top, dlog)):
                    for h in range(HEADS):
                        V.scalar_tensor_tensor(t[:, :, h], start[:], carry[:, i * HEADS + h:i * HEADS + h + 1], t[:, :, h],
                                               ALU.mult, ALU.add)
                v.drain()

                V.tensor_tensor(top[:], top[:], dlog[:], ALU.add)
                V.tensor_tensor(dlog[:], dlog[:], G[:, :, HE:HE + HEADS], ALU.add)
                v.drain()
                for t in (top, dlog):
                    V.scalar_tensor_tensor(t[:], t[:], 0.2, t[:], ALU.mult, ALU.max)
                v.drain()
                V.tensor_tensor(top[:], dlog[:], top[:], ALU.subtract).then_inc(s_exp_in, 1)
                V.tensor_tensor_scan(start[:], keep[:], pen[:], 1.0, ALU.mult, ALU.add)
                v.wait_ge(s_exp, 1)
                v.wait_ge(s_st, 16)
                V.tensor_tensor(G[:, :, 0:HE].rearrange("p w (h e) -> p w h e", h=HEADS),
                                G[:, :, 0:HE].rearrange("p w (h e) -> p w h e", h=HEADS), bcast(top[:], 3, EXPERTS), ALU.mult)
                V.tensor_copy(G[:, :, HE:NV], top[:])
                v.drain()

                V.tensor_copy(G[:, :, NV], start[:])

                def scan_part(i):
                    a, b = parts[i], parts[i + 1]
                    for k in range(NV):
                        V.tensor_tensor_scan(G[:, a:b, k], keep[:, a:b], G[:, a:b, k], G[:, a - 1, k:k + 1] if i else 0.0,
                                             ALU.mult, ALU.add)
                    v.drain()
                    v.sem_inc(s_done, 1)

                for i in range(3):
                    scan_part(i)
                with v.If(wide > 0):
                    scan_part(3)
                V.tensor_copy(lanes[:, 0, :], start[:, ds(last, 1)].to_broadcast([P, NV]))
                V.tensor_copy(lanes[:, 1, :], G[:, ds(last, 1), 0:NV].rearrange("p o r -> p (o r)"))
                carries(2, ALU.mult, ALU.add, 0.0)

                v.wait_ge(s_ends, 16 * TILES)
                V.tensor_tensor(ends[:], ends[:], bcast(node_i[:].bitcast(F32), 2, P), ALU.is_le)
                v.drain()
                V.tensor_reduce(place[:], ends[:], AX_X, ALU.add)
                v.drain()
                V.scalar_tensor_tensor(place[:], reach[:, 0:TILES], float(P), place[:], ALU.mult, ALU.add)
                v.drain()
                V.tensor_scalar(place[:], place[:], -float(P + 1), None, ALU.add)
                v.drain()
                V.tensor_tensor(ends[:], bcast(place[:], 2, P), bcast(bound[:], 1, TILES), ALU.is_ge)
                v.drain()
                V.tensor_reduce(lane[:], ends[:], AX_X, ALU.add)
                v.drain()
                V.tensor_scalar(lane[:], lane[:], -1.0, None, ALU.add)
                v.drain()
                V.scalar_tensor_tensor(place[:], lane[:], gap[:], place[:], ALU.mult, ALU.add)
                v.drain()
                V.tensor_copy(endpos[:], place[:]).then_inc(s_endpos, 1)
                V.tensor_tensor(ends[:], bcast(c.iota_row[:], 1, TILES), bcast(lane[:], 2, P), ALU.is_equal).then_inc(s_endpos, 1)

                v.wait_ge(s_sel, 1)
                v.wait_ge(s_num, 16 * TILES)
                for t in range(0, TILES, PER):
                    n = min(PER, TILES - t)
                    V.tensor_tensor(fix[:, t:t + n, :], ps_b[:, t // PER * 512:t // PER * 512 + n * NV].rearrange("p (t r) -> p t r", r=NV),
                                    num[:, t:t + n, NV:NV + 1].to_broadcast([P, n, NV]), ALU.mult)
                v.drain()
                V.tensor_tensor(num[:, :, 0:NV], num[:, :, 0:NV], fix, ALU.add)
                v.drain()
                V.tensor_scalar(den[:], num[:, :, HE:NV], 1e-16, None, ALU.add)
                v.drain()
                V.reciprocal(den[:], den[:])
                v.drain()
                V.tensor_tensor(dev[:].rearrange("p t (h e) -> p t h e", h=HEADS),
                                num[:, :, 0:HE].rearrange("p t (h e) -> p t h e", h=HEADS), bcast(den[:], 3, EXPERTS), ALU.mult)
                v.drain()
                V.tensor_tensor(dev[:], dev[:], bcast(par[:, 0, :], 1, TILES), ALU.add)
                v.drain()
                V.tensor_reduce(mu[:], dev[:], AX_X, ALU.add)
                v.drain()
                V.scalar_tensor_tensor(dev[:], bcast(mu[:], 2, HE), -1.0 / HE, dev[:], ALU.mult, ALU.add)
                v.drain()
                V.tensor_tensor(sq[:], dev[:], dev[:], ALU.mult)
                v.drain()
                V.tensor_reduce(var[:], sq[:], AX_X, ALU.add).then_inc(s_std, 1)
                v.wait_ge(s_std, 2)
                V.reciprocal(var[:], var[:])
                v.drain()
                V.tensor_tensor(dev[:], dev[:], bcast(var[:], 2, HE), ALU.mult)
                v.drain()
                V.tensor_tensor(dev[:], dev[:], bcast(par[:, 1, :], 1, TILES), ALU.mult)
                v.drain()
                V.tensor_tensor(dev[:], dev[:], bcast(par[:, 2, :], 1, TILES), ALU.add)
                v.drain()
                V.tensor_reduce(score[:], dev[:].rearrange("p t (h e) -> p t e h", h=HEADS), AX_X, ALU.add)
                v.drain()
                V.tensor_scalar(score[:], score[:], 1.0 / HEADS, None, ALU.mult)
                for e in range(EXPERTS):
                    V.memset(rank[:, :, e], float(e))
                v.drain()
                for e in range(EXPERTS):
                    for f in range(e + 1, EXPERTS):
                        V.tensor_tensor(wins[:], score[:, :, f], score[:, :, e], ALU.is_gt)
                        v.drain()
                        V.tensor_tensor(rank[:, :, e], rank[:, :, e], wins[:], ALU.add)
                        V.tensor_tensor(rank[:, :, f], rank[:, :, f], wins[:], ALU.subtract)
                        v.drain()
                V.tensor_reduce(mu[:], score[:], AX_X, ALU.max)
                V.tensor_scalar(rank[:], rank[:], 2.0, None, ALU.is_lt)
                v.drain()
                V.tensor_tensor(score[:], score[:], bcast(mu[:], 2, EXPERTS), ALU.subtract).then_inc(s_exp_in, 1)
                v.wait_ge(s_exp, 2)
                V.tensor_tensor(score[:], score[:], rank[:], ALU.mult)
                v.drain()
                V.tensor_reduce(mu[:], score[:], AX_X, ALU.add)
                v.drain()
                V.reciprocal(mu[:], mu[:])
                v.drain()
                V.tensor_tensor(gates[:], score[:], bcast(mu[:], 2, EXPERTS), ALU.mult)
                v.drain()
                v.sem_inc(s_exp_in, 1)

                for g in range(GROUPS):
                    b = buf[g % NB]
                    v.wait_ge(s_load[g % NB], 16 * (EXPERTS + 1) * (g // NB + 1))
                    for e in range(EXPERTS):
                        for u in range(GT):
                            V.scalar_tensor_tensor(b[:, EXPERTS, u, :], b[:, e, u, :], gates[:, g * GT + u, e:e + 1],
                                                   b[:, EXPERTS, u, :], ALU.mult, ALU.add)
                        v.drain()
                    v.wait_ge(s_bias, g + 1)
                    V.tensor_tensor(b[:, EXPERTS].rearrange("p t d -> p (t d)"), b[:, EXPERTS].rearrange("p t d -> p (t d)"),
                                    ps_b[:, 0:GT * D], ALU.add).then_inc(s_sum, 1)


def lay_out(inputs):
    col = lambda v: np.ascontiguousarray(v.reshape(-1, P).T)
    valid = np.zeros((N_PAD,), np.float32)
    valid[:N_NODES] = 1.0
    i = {k: np.asarray(v) for k, v in inputs.items()}
    pad = SORT_N - E_GNN
    edges = i["L0_ffn_edge_index"]
    return {
        "x": np.pad(i["x"], ((0, N_PAD - N_NODES), (0, 0)), mode="edge"),
        "src": np.pad(i["src"], (0, pad)).reshape(P, LANE),
        "dst": np.pad(i["dst"], (0, pad), constant_values=PAD_DST).reshape(P, LANE),
        "gat_src": edges[0].reshape(P, LANE), "gat_dst": edges[1].reshape(P, LANE),
        "ln_g": col(i["L0_mix_ln_g"]), "ln_b": col(i["L0_mix_ln_b"]),
        "wqkv": i["L0_mix_Wqkv"], "wproj": i["L0_mix_Wproj"], "wself": i["L0_gnn_W_self"],
        "wneigh": i["L0_gnn_W_neigh"], "wg1": i["L0_mix_Wg1"], "wg2": i["L0_mix_Wg2"],
        "bg1": i["L0_mix_bg1"].reshape(GATE_H, 1), "bg2": col(i["L0_mix_bg2"]),
        "bproj": i["L0_mix_bproj"].reshape(1, D), "b_gnn": i["L0_gnn_b"].reshape(1, D),
        "valid": col(valid),
        "w_gat": i["L0_ffn_W_gat"], "att_src": i["L0_ffn_att_src"].reshape(1, HE), "att_dst": i["L0_ffn_att_dst"].reshape(1, HE),
        "b_gat": i["L0_ffn_b_gat"].reshape(1, HE), "gamma": i["L0_ffn_ln_gamma"].reshape(1, HE),
        "beta": i["L0_ffn_ln_beta"].reshape(1, HE),
        "w1": i["L0_ffn_W1"], "w2": i["L0_ffn_W2"],
        "b1": col(i["L0_ffn_b1"]), "b2": i["L0_ffn_b2"],
    }




def program(nc, a, out):
    c = Core(nc)
    c.skey_gnn = c.dram("skey_gnn", [SORT_N])
    c.skey_gat = c.dram("skey_gat", [P + GAT_N])
    c.tail_d = c.dram("tail_d", [SELF_N])
    c.low_d = c.dram("low_d", [SELF_N])
    c.xn_tab = c.dram("xn_tab", [N_PAD, D])
    c.xnT_d = c.dram("xnT_d", [P, KC, N_PAD])
    c.xn2T_d = c.dram("xn2T_d", [P, KC, N_PAD])
    c.base_d = c.dram("base_d", [N_PAD, 2 * D])
    c.x2_d = c.dram("x2_d", [N_PAD, D])
    c.x2nT_d = c.dram("x2nT_d", [P, KC, N_PAD])
    c.hx_d = c.dram("hx_d", [N_PAD, ROW])
    c.y_d = c.dram("y_d", [EXPERTS, N_PAD, D])
    c.sums_d = c.dram("sums_d", [GAT_N, ROW])
    constants(c)
    key_tables(c)
    firsts = nc.alloc_sbuf_tensor("chunk_firsts", [P, FENCES], F32)
    reach = nc.alloc_sbuf_tensor("reach", [P, G_ITERS], F32)
    width = nc.alloc_sbuf_tensor("lane_width", [P, 2], I32)
    gap = nc.alloc_sbuf_tensor("lane_gap", [P, 1], F32)
    ctx, sb, ps = c.open()
    with ctx:
        t = StepTables(sb)
        ncm = sb("ncm", [1, D])
        prepare(c, a, t, ncm)
        acc = sb("acc", [P, TILES * (D + 1)])
        aggregate(c, a, t, ncm, acc)
        gnn_out(c, a, acc, firsts)
    ctx, sb, ps = c.open()
    with ctx:
        G = sb("edge_rows", [P, W, ROW])
        gat_gather_experts(c, a, G, firsts, reach, width, gap)
        gat_softmax(c, a, out, G, reach, width, gap)


def kernel(**inputs):
    import concourse.bacc as _bacc
    from concourse.bass_utils import run_bass_kernel_spmd as _run

    nc = _bacc.Bacc("TRN2", target_bir_lowering=False, num_devices=1)
    arrays, aps = {}, {}
    for name, array in lay_out(inputs).items():
        array = np.ascontiguousarray(array)
        arrays[f"in_{name}_dram"] = array
        aps[name] = nc.dram_tensor(f"in_{name}_dram", array.shape, mybir.dt.from_np(array.dtype), kind="ExternalInput").ap()
    out = nc.dram_tensor("out_0_dram", (N_PAD, D), F32, kind="ExternalOutput").ap()
    program(nc, aps, out)
    r = _run(nc, [arrays], core_ids=[0])
    return r.results[0]["out_0_dram"][:N_NODES]
```

```python
from contextlib import ExitStack

import numpy as np
import concourse.bass as bass
from concourse import mybir

F32 = mybir.dt.float32
I32 = mybir.dt.int32
ALU = mybir.AluOpType
ACT = mybir.ActivationFunctionType
AX_X = mybir.AxisListType.X
DVE_ENGINE = mybir.EngineType.DVE
ds = bass.ds

P = 128
N_NODES = 6250
D = 256
KC = D // P
TILES = -(-N_NODES // P)
N_PAD = TILES * P
GROUPS = 7
GT = TILES // GROUPS
GN = GT * P
HALF = [(0, 4), (4, 3)]
HB = GN // 2
LN_EPS = 1e-5
HEADS_MIX = 8
HD = D // HEADS_MIX
GATE_H = 64

EXPERTS = 4
HEADS = 4
HE = HEADS * EXPERTS
HID = 512
HC = HID // P

E_GNN = 100000
E_GAT = 131072
LANE = 1024
SORT_N = P * LANE
OFF = 1 << 30
SRC_BITS = 14
SRC_MASK = (1 << SRC_BITS) - 1
EDGE = 1 << SRC_BITS - 1
DST_MASK = 8191
PAD_DST = 8191

CH_GNN = -(-E_GNN // P)
STEPS = CH_GNN + TILES - 1
SBLK = 16
SHALF = SBLK // 2
S_ITERS = -(-STEPS // SBLK)
STEP_COLS = -(-(S_ITERS * SBLK + SHALF) // P) * P
STEP_G = STEP_COLS // P

SELF_N = 8192
GAT_N = SORT_N + SELF_N
W = GAT_N // P
G_ITERS = W // SBLK
LOW_ITERS = 53
W_LOW = LOW_ITERS * SBLK
FENCES = GAT_N // P
FENCE_P = 64
ROW = HE + 2 * HEADS
NV = HE + HEADS
BLOCK = 7 * SBLK
LAST = W_LOW % BLOCK
BLOCK_MAX = W - W_LOW - BLOCK
BIG = 1e30
SENTINEL = float(np.array(OFF | PAD_DST << SRC_BITS, np.int32).view(np.float32))

LANE_BITS = P.bit_length() - 1
ALONG = LANE.bit_length() - 1
MERGES = LANE_BITS + 1

assert TILES == GROUPS * GT and E_GAT == SORT_N and W % SBLK == 0 and FENCES % FENCE_P == 0


def bcast(ap, axis, n):
    v = ap.unsqueeze(axis)
    return v.to_broadcast([*v.shape[:axis], n, *v.shape[axis + 1:]])


class Core:

    def __init__(self, nc):
        self.nc = nc

    def sem(self, name):
        return self.nc.alloc_semaphore(name)

    def dram(self, name, shape, dt=F32):
        return self.nc.dram_tensor(name, shape, dt, kind="Internal").ap()

    def open(self):
        ctx = ExitStack()
        sb = lambda name, shape, dt=F32: ctx.enter_context(self.nc.sbuf_tensor(name, shape, dt))
        ps = lambda name, shape, dt=F32: ctx.enter_context(self.nc.psum_tensor(name, shape, dt))
        return ctx, sb, ps


def constants(c):
    nc = c.nc
    c.ident = nc.alloc_sbuf_tensor("ident", [P, P], F32)
    c.ones = nc.alloc_sbuf_tensor("ones", [P, P], F32)
    c.iota_row = nc.alloc_sbuf_tensor("iota_row", [P, P], F32)
    c.iota_col = nc.alloc_sbuf_tensor("iota_col", [P, 1], I32)
    c.eps = nc.alloc_sbuf_tensor("eps", [P, 1], F32)
    iota_colf = nc.alloc_sbuf_tensor("iota_colf", [P, 1], F32)
    s_iota = c.sem("const_iota")
    with nc.Block() as block:
        @block.gpsimd
        def _(pool):
            nc.gpsimd.iota(c.iota_row[:], pattern=[[1, P]], base=0, channel_multiplier=0,
                           allow_small_or_imprecise_dtypes=True)
            nc.gpsimd.iota(c.iota_col[:], pattern=[[0, 1]], base=0, channel_multiplier=1).then_inc(s_iota, 1)

        @block.vector
        def _(v):
            nc.vector.memset(c.ones[:], 1.0)
            nc.vector.memset(c.eps[:], LN_EPS)
            v.wait_ge(s_iota, 1)
            nc.vector.tensor_copy(iota_colf[:], c.iota_col[:])
            v.drain()
            nc.vector.tensor_scalar(c.ident[:], c.iota_row[:], iota_colf[:], None, ALU.is_equal)


def key_tables(c):
    nc = c.nc
    c.signs = nc.alloc_sbuf_tensor("signs", [P, MERGES + 1], F32)
    c.off = nc.alloc_sbuf_tensor("merge_off", [P, MERGES + 1, LANE_BITS], F32)
    c.noff = nc.alloc_sbuf_tensor("merge_noff", [P, MERGES + 1, LANE_BITS], F32)
    bits = nc.alloc_sbuf_tensor("sign_bits", [P, LANE_BITS + 1], I32)
    per = nc.alloc_sbuf_tensor("sign_block", [P, LANE_BITS + 1], F32)
    with nc.Block() as block:
        @block.vector
        def _(v):
            for b in range(LANE_BITS + 1):
                nc.vector.tensor_scalar(bits[:, b:b + 1], c.iota_col[:], b, 1, ALU.logical_shift_right, ALU.bitwise_and)
            nc.vector.memset(c.signs[:], 1.0)
            nc.vector.memset(c.off[:], 0.0)
            nc.vector.memset(c.noff[:], 0.0)
            v.drain()
            nc.vector.tensor_scalar(per[:], bits[:], -2.0, 1.0, ALU.mult, ALU.add)
            for m in range(1, LANE_BITS):
                nc.vector.memset(c.off[:, m, 0:LANE_BITS - m], BIG)
                nc.vector.memset(c.noff[:, m, 0:LANE_BITS - m], -BIG)
            v.drain()
            nc.vector.tensor_copy(c.signs[:, 0:1], per[:, 0:1])
            nc.vector.tensor_tensor(c.signs[:, 1:LANE_BITS + 1], per[:, 0:LANE_BITS], per[:, 1:LANE_BITS + 1], ALU.mult)


def pairs(ap, dist):
    v = ap.rearrange("p (n two d) -> p n two d", two=2, d=dist)
    return v[:, :, 0, :], v[:, :, 1, :]


def lane_stages():
    stages, size = [], 2
    while size <= LANE:
        stages.append((size, None))
        dist = size // 4
        while dist:
            stages.append((size, dist))
            dist //= 2
        size *= 2
    return stages


class Sorter:

    STAGES = lane_stages()

    def __init__(self, c, name, sb, turned):
        self.c = c
        self.buf = [sb(f"{name}_keys{i}", [P, LANE]) for i in range(2)]
        self.turned = turned
        self.s_ready, self.s_turned = c.sem(f"{name}_ready"), c.sem(f"{name}_turned")

    def compare(self, v, dst, src, dist):
        nc = self.c.nc
        s, t = pairs(src, dist), pairs(dst, dist)
        nc.vector.tensor_tensor(t[0], s[0], s[1], ALU.min)
        nc.vector.tensor_tensor(t[1], s[0], s[1], ALU.max)
        v.drain()

    def compare_psum(self, v, dst, src, dist):
        nc = self.c.nc
        s, t = pairs(src, dist), pairs(dst, dist)
        nc.vector.tensor_copy(t[1], s[1])
        v.drain()
        nc.vector.tensor_tensor(t[0], s[0], t[1], ALU.min)
        nc.vector.tensor_tensor(t[1], s[0], t[1], ALU.max)
        v.drain()

    def first_sign(self, v):
        self.c.nc.vector.tensor_scalar(self.buf[0][:], self.buf[0][:], self.c.signs[:, 0:1], None, ALU.mult)
        v.drain()

    def lane_stage(self, v, i):
        nc = self.c.nc
        size, dist = self.STAGES[i]
        src, dst = self.buf[i % 2][:], self.buf[1 - i % 2][:]
        if dist:
            self.compare(v, dst, src, dist)
        else:
            half = size // 2
            s, t = (x.rearrange("p (n z) -> p n z", z=size) for x in (src, dst))
            nc.vector.tensor_tensor(t[:, :, 0:half], s[:, :, 0:half], s[:, :, half:size][:, :, ::-1], ALU.min)
            nc.vector.tensor_tensor(t[:, :, half:size], s[:, :, half:size], s[:, :, 0:half][:, :, ::-1], ALU.max)
            v.drain()

    def ask(self, v, m):
        self.c.nc.vector.tensor_scalar(self.buf[0][:], self.buf[1][:], self.c.signs[:, ds(m, 1)], None, ALU.mult)
        v.drain()
        v.sem_inc(self.s_ready, 1)

    def across_stage(self, v, m, i):
        nc, c = self.c.nc, self.c
        off, noff = c.off[:, ds(m, 1), i], c.noff[:, ds(m, 1), i]
        dst = pairs(self.buf[1 - i % 2][:], P >> (i + 1))
        if i == 0:
            src = pairs(self.turned, P >> 1)
            nc.vector.tensor_copy(dst[1], src[1])
            v.drain()
            nc.vector.scalar_tensor_tensor(dst[0], dst[1], off, src[0], ALU.add, ALU.min)
            nc.vector.scalar_tensor_tensor(dst[1], src[0], noff, dst[1], ALU.add, ALU.max)
        else:
            src = pairs(self.buf[i % 2][:], P >> (i + 1))
            nc.vector.scalar_tensor_tensor(dst[0], src[1], off, src[0], ALU.add, ALU.min)
            nc.vector.scalar_tensor_tensor(dst[1], src[0], noff, src[1], ALU.add, ALU.max)
        v.drain()

    def ask_back(self, v):
        v.sem_inc(self.s_ready, 1)

    def along_stage(self, v, i):
        if i == 0:
            self.compare_psum(v, self.buf[0][:], self.turned, LANE >> 1)
        else:
            self.compare(v, self.buf[i % 2][:], self.buf[1 - i % 2][:], LANE >> (i + 1))

    def merge(self, v, m):
        self.ask(v, m)
        v.wait_ge(self.s_turned, 2 * m - 1)
        for i in range(LANE_BITS):
            self.across_stage(v, m, i)
        self.ask_back(v)
        v.wait_ge(self.s_turned, 2 * m)
        for i in range(ALONG):
            self.along_stage(v, i)

    def turn_from(self, pe, b, count):
        nc = self.c.nc
        pe.wait_ge(self.s_ready, count)
        for k in range(LANE // P):
            last = nc.tensor.transpose(self.turned[:, k * P:(k + 1) * P], self.buf[b][:, k * P:(k + 1) * P], self.c.ident[:])
        last.then_inc(self.s_turned, 1)


class StepTables:
    def __init__(self, sb):
        self.idx = sb("step_src", [P, STEP_COLS], I32)
        self.nloc = sb("step_nloc", [P, STEP_COLS])
        self.tile = sb("step_tile", [1, STEP_COLS], I32)


def prepare(c, a, t, ncm, acc):
    nc = c.nc
    Q = LANE // P
    TURNS = 2 * KC
    ctx, sb, ps = c.open()
    with ctx:
        xg = sb("xg", [P, GT, D])
        xn = sb("xn", [P, GT, D])
        diag = sb("ln_diag", [P, GT, P])
        eps_sq = sb("ln_eps_sq", [P, 1])
        stats = sb("stats", [P, GT, 6])
        mv = sb("mv", [P, GT, 2])
        std = sb("std", [P, 2, GT])
        rstd = sb("rstd", [P, 2, GT])
        xnT = sb("xnT", [P, KC, GN])
        xn2T = sb("xn2T", [P, KC, GN])
        ln_g = sb("ln_g", [P, KC])
        ln_b = sb("ln_b", [P, KC])
        wk = sb("ln_wk", [P, KC, 3 * D])
        bmax = sb("bmax", [P, KC, 2 * GROUPS])
        cmax = sb("cmax", [P, KC])
        psA = [ps(f"psA{i}", [P, 512]) for i in range(2)]
        psB = [ps(f"psB{i}", [P, 512]) for i in range(2)]
        psK = ps("psK", [P, 4 * 512])
        bankK = [psK[:, i * 512:(i + 1) * 512] for i in range(4)]
        s_x, s_mv, s_std, s_xn, s_diag = c.sem("ln_x"), c.sem("ln_mv"), c.sem("ln_std"), c.sem("ln_xn"), c.sem("ln_diag")
        s_tA, s_evA, s_tB, s_evB = c.sem("ln_tA"), c.sem("ln_evA"), c.sem("ln_tB"), c.sem("ln_evB")
        s_row, s_outA, s_outB, s_k, s_kmax, s_cm, s_cmT = (c.sem("ln_" + n) for n in (
            "row", "outA", "outB", "k", "kmax", "cm", "cmT"))
        x_v = a["x"].rearrange("(t p) d -> p t d", p=P)
        xn_v = c.xn_tab.rearrange("(t p) d -> p t d", p=P)

        src = sb("edge_src", [P, LANE], I32)
        dst = sb("edge_dst", [P, LANE], I32)
        nxt = sb("edge_next", [P, LANE], I32)
        less = sb("edge_less", [P, LANE])
        drops = sb("edge_drops", [P, 1])
        unsorted = sb("edge_unsorted", [1, 1], I32)
        srt = Sorter(c, "gnnsort", sb, psK[:, 0:LANE])
        s_edges, s_drops, s_bad, s_keys, s_flag, s_sorted, s_st = (c.sem("eg_" + n) for n in (
            "in", "drops", "bad", "keys", "flag", "sorted", "st"))

        keys = sb("st_keys", [P, LANE], I32)
        last_i = sb("st_last_i", [P, Q], I32)
        ends = sb("st_ends", [P, Q])
        ch_i = sb("st_ch_i", [P, Q], I32)
        ch_f = sb("st_ch_f", [P, Q])
        all_ends = sb("st_all_ends", [P, CH_GNN])
        before = sb("st_before", [P, CH_GNN])
        step_i = sb("st_step_i", [P, STEP_G], I32)
        step_f = sb("st_step_f", [P, STEP_G])
        chunk = sb("st_chunk", [P, STEP_G])
        chunk_i = sb("st_chunk_i", [P, STEP_G], I32)
        tile = sb("st_tile", [P, STEP_G])
        t_rows = sb("st_t_rows", [STEP_G, P], I32)
        row = sb("st_row", [P, STEP_G, P], I32)
        src_i = sb("st_src_i", [P, STEP_G, P], I32)
        src_f = sb("st_src_f", [P, STEP_G, P])
        dst_f = sb("st_dst_f", [P, STEP_G, P])
        s_keysin, s_num, s_ends, s_endst, s_all, s_chunk, s_rows, s_dec, s_turn, s_t, s_tst = (c.sem("st_" + n) for n in (
            "keys_in", "num", "ends", "end_st", "all", "chunk", "rows", "dec", "turn", "t", "t_st"))
        ends_d = c.dram("step_ends_d", [LANE])
        tile_d = c.dram("step_tile_d", [STEP_COLS])
        sorted_v = c.skey_gnn.rearrange("(p j) -> p j", p=P)
        dst_flat = a["dst"].rearrange("p j -> (p j)")

        with nc.Block() as block:
            @block.sync
            def _(sp):
                sp.dma_start(xg[:], x_v[:, 0:GT, :]).then_inc(s_x, 16)
                sp.dma_start(wk[:], a["wqkv"].rearrange("(k p) n -> p k n", p=P)).then_inc(s_row, 16)
                with sp.Fori(1, GROUPS) as g:
                    sp.wait_ge(s_xn, g * GT)
                    sp.dma_start(xg[:], x_v[:, ds(g * GT, GT), :]).then_inc(s_x, 16)
                    sp.dma_start(xn_v[:, ds(g * GT - GT, GT), :], xn[:]).then_inc(s_row, 16)
                sp.wait_ge(s_xn, TILES)
                sp.dma_start(xn_v[:, TILES - GT:TILES, :], xn[:]).then_inc(s_row, 16)
                sp.wait_ge(s_row, 16 * GROUPS + 16)

            @block.gpsimd
            def _(pool):
                pool.dma_start(dst[:], a["dst"]).then_inc(s_edges, 16)
                pool.dma_start(nxt[0:P - 1, :], dst_flat[1:SORT_N - LANE + 1].rearrange("(p j) -> p j", p=P - 1)).then_inc(s_edges, 16)
                pool.dma_start(nxt[P - 1:P, 0:LANE - 1], dst_flat[SORT_N - LANE + 1:SORT_N].rearrange("(p j) -> p j", p=1)).then_inc(s_edges, 16)
                pool.dma_start(src[:], a["src"]).then_inc(s_edges, 16)
                nc.gpsimd.iota(ch_i[:], pattern=[[1, Q]], base=0, channel_multiplier=Q)
                nc.gpsimd.iota(step_i[:], pattern=[[P, STEP_G]], base=0, channel_multiplier=1).then_inc(s_num, 1)
                nc.gpsimd.memset(acc[:], 0.0)
                pool.wait_ge(s_keys, 1)
                pool.dma_start(sorted_v, srt.buf[0][:]).then_inc(s_st, 16)
                pool.wait_ge(s_st, 16)
                pool.wait_ge(s_flag, 1)
                with pool.If(pool.value_load(unsorted[0:1, 0:1], min_val=0, max_val=P) > 0):
                    pool.wait_ge(s_sorted, 1)
                    pool.dma_start(sorted_v, srt.buf[1][:]).then_inc(s_st, 16)
                    pool.wait_ge(s_st, 32)
                pool.dma_start(keys[:], sorted_v.bitcast(I32)).then_inc(s_keysin, 16)
                pool.wait_ge(s_ends, 1)
                pool.dma_start(ends_d.rearrange("(p q) -> p q", p=P), ends[:]).then_inc(s_endst, 16)
                pool.wait_ge(s_endst, 16)
                pool.dma_start(all_ends[:], ends_d[0:CH_GNN].rearrange("(o n) -> o n", o=1).to_broadcast([P, CH_GNN])).then_inc(s_all, 16)
                pool.wait_ge(s_chunk, 1)
                for g in range(STEP_G):
                    pool.indirect_dma_start(row[:, g, :], None, c.skey_gnn.rearrange("(c e) -> c e", e=P).bitcast(I32),
                                            bass.IndirectOffsetOnAxis(ap=chunk_i[:, g:g + 1], axis=0)).then_inc(s_rows, 16)
                pool.wait_ge(s_t, 1)
                pool.dma_start(tile_d.rearrange("(g p) -> g p", p=P).bitcast(I32), t_rows[:]).then_inc(s_tst, 16)
                pool.wait_ge(s_tst, 16)
                pool.dma_start(t.tile[:], tile_d.rearrange("(o n) -> o n", o=1).bitcast(I32)).then_inc(s_tst, 16)
                pool.wait_ge(s_tst, 32)

            @block.vector
            def _(v):
                V = nc.vector

                def moments(rows):
                    for u in range(GT):
                        V.bn_stats(stats[:, u, :], rows[:, u, :])
                    v.drain()
                    for u in range(GT):
                        last = V.bn_aggr(mv[:, u, :], stats[:, u, :])
                    return last

                def maxima(g, count):
                    v.wait_ge(s_k, count)
                    for i in range(2):
                        for h in range(KC):
                            last = V.tensor_reduce(bmax[:, h, ds(2 * g + i, 1)], bankK[2 * i + h][:, 0:HB], AX_X, ALU.max)
                    last.then_inc(s_kmax, 1)
                    v.drain()

                def group(g, behind):
                    v.wait_ge(s_x, 16 * g + 16)
                    moments(xg).then_inc(s_mv, 1)
                    v.wait_ge(s_std, g + 2)
                    V.reciprocal(rstd[:], std[:])
                    v.drain()
                    V.tensor_tensor(rstd[:, 1, :], rstd[:, 1, :], std[:, 0, :], ALU.mult)
                    v.drain()
                    v.wait_ge(s_tA, g * TURNS + TURNS)
                    v.wait_ge(s_tB, g * TURNS + TURNS)
                    v.wait_ge(s_row, 16 * g + 16)
                    for u in range(GT):
                        V.tensor_scalar(xn[:, u, :], xg[:, u, :], mv[:, u, 0:1], rstd[:, 0, u:u + 1],
                                        ALU.subtract, ALU.mult).then_inc(s_xn, 1)
                    for u in range(GT):
                        V.tensor_scalar(diag[:, u, :], c.ident[:], rstd[:, 1, u:u + 1], None, ALU.mult).then_inc(s_diag, 1)
                    if behind:
                        maxima(g - 1, g)
                    v.drain()

                V.memset(eps_sq[:], LN_EPS * LN_EPS).then_inc(s_std, 1)
                group(0, False)
                V.memset(less[:, LANE - 1:LANE], 0.0)
                v.drain()
                v.wait_ge(s_edges, 64)
                V.tensor_tensor(less[:, 0:LANE - 1], dst[:, 0:LANE - 1], nxt[:, 0:LANE - 1], ALU.is_gt)
                V.tensor_tensor(less[0:P - 1, LANE - 1:LANE], dst[0:P - 1, LANE - 1:LANE], nxt[0:P - 1, LANE - 1:LANE], ALU.is_gt)
                v.drain()
                V.tensor_scalar(dst[:], dst[:], SRC_BITS, OFF, ALU.logical_shift_left, ALU.bitwise_or)
                V.tensor_reduce(drops[:], less[:], AX_X, ALU.max).then_inc(s_drops, 1)
                v.drain()
                V.tensor_tensor(srt.buf[0][:].bitcast(I32), src[:], dst[:], ALU.bitwise_or).then_inc(s_keys, 1)
                maxima(0, 1)
                v.wait_ge(s_bad, 1)
                V.tensor_copy(unsorted[:], psA[0][0:1, 0:1])
                v.drain()
                v.sem_inc(s_flag, 1)
                v.wait_ge(s_flag, 1)
                with v.If(v.value_load(unsorted[0:1, 0:1], min_val=0, max_val=P) > 0):
                    v.wait_ge(s_st, 16)
                    srt.first_sign(v)
                    for i in range(len(srt.STAGES)):
                        srt.lane_stage(v, i)
                    with v.Fori(1, MERGES) as m:
                        srt.merge(v, m)
                    v.sem_inc(s_sorted, 1)

                group(1, False)
                v.wait_ge(s_num, 1)
                V.tensor_copy(ch_f[:], ch_i[:])
                V.tensor_copy(step_f[:], step_i[:])
                v.wait_ge(s_keysin, 16)
                V.tensor_scalar(last_i[:], keys[:].rearrange("p (q e) -> p q e", e=P)[:, :, P - 1], SRC_BITS + LANE_BITS,
                                DST_MASK >> LANE_BITS, ALU.logical_shift_right, ALU.bitwise_and)
                v.drain()
                V.tensor_copy(ends[:], last_i[:])
                v.drain()
                V.scalar_tensor_tensor(ends[:], ends[:], float(TILES - 1), ch_f[:], ALU.min, ALU.add).then_inc(s_ends, 1)
                group(2, True)
                v.wait_ge(s_all, 16)
                for g in range(STEP_G):
                    V.tensor_scalar(before[:], all_ends[:], step_f[:, g:g + 1], None, ALU.is_lt, ALU.add,
                                    accum_out=chunk[:, g:g + 1])
                    v.drain()
                V.tensor_copy(chunk_i[:], chunk[:]).then_inc(s_chunk, 1)
                V.tensor_tensor(tile[:], step_f[:], chunk[:], ALU.subtract)
                v.drain()
                V.tensor_scalar(tile[:], tile[:], float(TILES - 1), None, ALU.min)
                v.drain()
                with v.Fori(3, 5) as g:
                    group(g, True)
                group(5, False)
                v.wait_ge(s_rows, 16 * STEP_G)
                V.tensor_scalar(src_i[:], row[:], SRC_MASK, None, ALU.bitwise_and)
                V.tensor_scalar(row[:], row[:], SRC_BITS, DST_MASK, ALU.logical_shift_right, ALU.bitwise_and)
                v.drain()
                V.tensor_scalar(src_f[:], src_i[:], float(N_NODES - 1), None, ALU.min)
                V.tensor_copy(dst_f[:], row[:])
                v.drain()
                V.scalar_tensor_tensor(dst_f[:], bcast(tile[:], 2, P), float(P), dst_f[:], ALU.mult, ALU.subtract)
                maxima(4, 5)
                v.sem_inc(s_dec, 1)
                v.wait_ge(s_turn, 1)
                V.tensor_copy(t.idx[:], psK[:, 0:STEP_COLS])
                V.tensor_copy(t.nloc[:], psK[:, 1024:1024 + STEP_COLS])
                V.tensor_copy(t_rows[:], psK[0:STEP_G, 2048 - P:2048])
                v.drain()
                v.sem_inc(s_t, 1)
                group(6, True)
                maxima(6, GROUPS)

                V.tensor_reduce(cmax[:], bmax[:], AX_X, ALU.max)
                v.drain()
                v.sem_inc(s_cm, 1)
                v.wait_ge(s_cmT, 1)
                V.tensor_scalar(ncm[:], psA[0][0:1, 0:D], -1.0, None, ALU.mult)

            @block.tensor
            def _(pe):
                pe.wait_ge(s_row, 16)

                def turns(g):
                    for bank, by, s_in, s_t, s_ev in ((psA, None, s_xn, s_tA, s_evA), (psB, diag, s_diag, s_tB, s_evB)):
                        for j in range(TURNS):
                            (u0, n), k = HALF[j // KC], j % KC
                            pe.wait_ge(s_in, g * GT + u0 + n)
                            pe.wait_ge(s_ev, g * TURNS + j + 1)
                            for u in range(n):
                                to, rows = bank[k][:, u * P:(u + 1) * P], xn[:, u0 + u, k * P:(k + 1) * P]
                                if by is None:
                                    last = nc.tensor.transpose(to, rows, c.ident[:])
                                else:
                                    last = nc.tensor.matmul(to, rows, by[:, u0 + u, :], start=True, stop=True)
                            last.then_inc(s_t, 1)

                def k_of(g):
                    pe.wait_ge(s_evA, g * TURNS + TURNS + KC)
                    pe.wait_ge(s_kmax, g + 1)
                    for i in range(2):
                        for h in range(KC):
                            for k in range(KC):
                                last = nc.tensor.matmul(bankK[2 * i + h][:, 0:HB], wk[:, k, D + h * P:D + (h + 1) * P],
                                                        xnT[:, k, i * HB:(i + 1) * HB], start=(k == 0), stop=(k == KC - 1))
                    last.then_inc(s_k, 1)

                turns(0)
                k_of(0)
                pe.wait_ge(s_drops, 1)
                nc.tensor.matmul(psA[0][0:1, 0:1], drops[:], c.ones[:, 0:1], start=True, stop=True).then_inc(s_bad, 1)
                pe.wait_ge(s_flag, 1)
                with pe.If(pe.value_load(unsorted[0:1, 0:1], min_val=0, max_val=P) > 0):
                    with pe.Fori(1, MERGES) as m:
                        srt.turn_from(pe, 0, 2 * m - 1)
                        srt.turn_from(pe, 1, 2 * m)
                with pe.Fori(1, 5) as g:
                    turns(g)
                    k_of(g)
                turns(5)
                pe.wait_ge(s_dec, 1)
                for g in range(STEP_G):
                    nc.tensor.transpose(psK[:, g * P:(g + 1) * P], src_f[:, g, :], c.ident[:])
                    nc.tensor.transpose(psK[:, 1024 + g * P:1024 + (g + 1) * P], dst_f[:, g, :], c.ident[:])
                nc.tensor.transpose(psK[0:STEP_G, 2048 - P:2048], tile[:], c.ident[:]).then_inc(s_turn, 1)
                pe.wait_ge(s_t, 1)
                k_of(5)
                turns(6)
                k_of(6)
                pe.wait_ge(s_cm, 1)
                for h in range(KC):
                    last = nc.tensor.transpose(psA[0][0:1, h * P:(h + 1) * P], cmax[:, h:h + 1], c.ident[:])
                last.then_inc(s_cmT, 1)

            @block.scalar
            def _(act):
                act.sem_inc(s_tA, TURNS)
                act.sem_inc(s_tB, TURNS)
                act.sem_inc(s_evA, KC)
                act.sem_inc(s_evB, KC)
                act.sem_inc(s_kmax, 1)
                act.dma_start(ln_g[:], a["ln_g"]).then_inc(s_outA, 16)
                act.dma_start(ln_b[:], a["ln_b"]).then_inc(s_outB, 16)

                def roots(g):
                    act.wait_ge(s_mv, g + 1)
                    nc.scalar.activation(std[:, 0, :], mv[:, :, 1], ACT.Sqrt, bias=c.eps[:])
                    nc.scalar.activation(std[:, 1, :], mv[:, :, 1], ACT.Sqrt, bias=eps_sq[:], scale=1.0 + LN_EPS).then_inc(s_std, 1)

                def rows(g):
                    act.wait_ge(s_outA, 16 * g + 16)
                    for j in range(TURNS):
                        (u0, n), k = HALF[j // KC], j % KC
                        act.wait_ge(s_tA, g * TURNS + j + 1 + TURNS)
                        nc.scalar.copy(xnT[:, k, u0 * P:(u0 + n) * P], psA[k][:, 0:n * P]).then_inc(s_evA, 1)
                    act.wait_ge(s_evA, g * TURNS + TURNS + KC)
                    act.dma_start(c.xnT_d[:, :, ds(g * GN, GN)], xnT[:]).then_inc(s_outA, 16)

                def mixer_rows(g):
                    act.wait_ge(s_outB, 16 * g + 16)
                    for j in range(TURNS):
                        (u0, n), k = HALF[j // KC], j % KC
                        act.wait_ge(s_tB, g * TURNS + j + 1 + TURNS)
                        nc.scalar.activation(xn2T[:, k, u0 * P:(u0 + n) * P], psB[k][:, 0:n * P], ACT.Identity,
                                             bias=ln_b[:, k:k + 1], scale=ln_g[:, k:k + 1]).then_inc(s_evB, 1)
                    act.wait_ge(s_evB, g * TURNS + TURNS + KC)
                    act.dma_start(c.xn2T_d[:, :, ds(g * GN, GN)], xn2T[:]).then_inc(s_outB, 16)

                act.wait_ge(s_std, 1)
                roots(0)
                with act.Fori(0, GROUPS - 1) as g:
                    rows(g)
                    mixer_rows(g)
                    roots(g + 1)
                rows(GROUPS - 1)
                mixer_rows(GROUPS - 1)
                act.wait_ge(s_outA, 16 * GROUPS + 16)
                act.wait_ge(s_outB, 16 * GROUPS + 16)


LANE_PAIRS = 2
MID_PAIR = LANE_PAIRS + GROUPS
SHARES = 10
C_PAIR = MID_PAIR + 1
R_PAIR = C_PAIR + 2 * GROUPS
PAIRS = S_ITERS // 2
QUART = 4
assert S_ITERS % 2 == 0 and PAIRS - R_PAIR == 2


def aggregate(c, a, t, ncm, acc, plan):
    nc = c.nc
    ROWW = D + 1
    BANKS = 4
    CW = P + 1
    NS = SELF_N // P
    ctx, sb, ps = c.open()
    with ctx:
        msg = sb("ag_msg", [P, QUART, SHALF, ROWW])
        hot = sb("ag_hot", [P, QUART, SHALF, P])
        lent = [plan.selfm[:], plan.dst[:], plan.idx[:].bitcast(F32)]
        dif = lent[0][:, 0:SHALF * P].rearrange("p (u n) -> p u n", u=SHALF)
        ixs = sb("ag_ixs", [P, QUART, SHALF], I32)
        tick = sb("ag_tick", [P, QUART])
        bank = [ps(f"ag_ps{i}", [P, 512]) for i in range(BANKS)]
        s_ix, s_tick, s_hot, s_mm, s_acc, s_init = (c.sem("ag_" + n) for n in ("ix", "tick", "hot", "mm", "acc", "init"))
        s_g = [c.sem(f"ag_rows{q}") for q in range(QUART)]

        wqkv = sb("wqkv", [P, KC, 3 * D])
        wproj = sb("wproj", [P, KC, D])
        wself = sb("wself", [P, KC, D])
        wg1 = sb("wg1", [P, KC, GATE_H])
        wg2 = sb("wg2", [GATE_H, D])
        bg1 = sb("bg1", [GATE_H, 1])
        bg2 = sb("bg2", [P, KC])
        bproj = sb("bproj", [1, D])
        valid = sb("valid", [P, TILES])
        bd = sb("bd", [P, P])
        blk_i = sb("blk_i", [P, P], I32)
        blk_f = sb("blk_f", [P, P])
        own_i = sb("own_i", [P, 1], I32)
        own_f = sb("own_f", [P, 1])
        zeros = sb("zeros", [P, KC * CW])
        xT = [sb(f"xT{i}", [P, KC, n * P]) for i, (_, n) in enumerate(HALF)]
        x2T = [sb(f"x2T{i}", [P, KC, n * P]) for i, (_, n) in enumerate(HALF)]
        xr = sb("xr", [P, GT, D])
        ke = lent[1][:, 0:2 * D].rearrange("p (b d) -> p b d", b=2)
        vm = lent[1][:, 2 * D:2 * D + 2 * KC * CW].rearrange("p (b k n) -> p b k n", b=2, k=KC)
        rz = sb("rz", [P, KC])
        ctxbd = sb("ctxbd", [P, KC, P])
        wqT, m_sb = (lent[2][:, i * KC * D:(i + 1) * KC * D].rearrange("p (k d) -> p k d", k=KC) for i in range(2))
        hg = sb("hg", [GATE_H, 4 * P])
        gate = sb("gate", [P, KC, 4 * P])
        prod = sb("prod", [P, KC, 4 * P])
        rows = sb("rows", [P, GT, 2 * D])
        mix = [ps(f"mx_ps{i}", [P, 512]) for i in range(2)]
        s_w, s_wq, s_wqc, s_kv, s_ev, s_ctx, s_bd, s_m, s_msb = (c.sem("mx_" + n) for n in (
            "w", "wq", "wqc", "kv", "ev", "ctx", "bd", "m", "msb"))
        s_xT = [c.sem(f"mx_xT{i}") for i in range(2)]
        s_in = [c.sem(f"mx_in{i}") for i in range(2)]
        s_rst = [c.sem(f"mx_rowst{i}") for i in range(2)]
        s_hgp, s_hg, s_gp, s_gate, s_at, s_prod, s_rows, s_copied = (c.sem("mx_" + n) for n in (
            "hgp", "hg", "gp", "gate", "at", "prod", "rows", "copied"))
        x_v = a["x"].rearrange("(t p) d -> p t d", p=P)
        rows_v = c.base_d.rearrange("(t p) d -> p t d", p=P)

        psS = ps("srt_ps", [P, LANE])
        srt = Sorter(c, "gatsort", sb, psS[:])
        dst = srt.buf[1][:].bitcast(I32)
        selves = sb("selves", [P, NS], I32)
        pad = sb("selves_pad", [P, NS], I32)
        tail = sb("sort_tail", [P, NS])
        upper = [sb(f"sort_upper{i}", [P, NS]) for i in range(2)]
        upper_t = [sb(f"sort_uppert{i}", [NS, P]) for i in range(2)]
        first = sb("sentinel", [1, P])
        s_edges, s_ids, s_sorted, s_tail, s_tail_ld, s_low, s_low_ld, s_up, s_all, s_out = (c.sem("srt_" + n) for n in (
            "in", "ids", "sorted", "tail", "tail_ld", "low", "low_ld", "up", "all", "out"))
        tail_lanes = P - SELF_N // LANE
        T_LAST = 2 * (MERGES - 1)

        def tile_of(u):
            i = int(u >= HALF[1][0])
            return i, (u - HALF[i][0]) * P

        with nc.Block() as block:
            @block.sync
            def _(sp):
                sp.dma_start(wqkv[:], a["wqkv"].rearrange("(k p) n -> p k n", p=P)).then_inc(s_w, 16)
                sp.dma_start(srt.buf[0][:].bitcast(I32), a["gat_src"]).then_inc(s_edges, 16)
                sp.dma_start(dst, a["gat_dst"]).then_inc(s_edges, 16)
                sp.dma_start(valid[:], a["valid"]).then_inc(s_w, 16)
                for to, src in ((wproj, "wproj"), (wself, "wself"), (wg1, "wg1")):
                    sp.dma_start(to[:], a[src].rearrange("(k p) n -> p k n", p=P)).then_inc(s_w, 16)
                for to, src in ((bg1, "bg1"), (bproj, "bproj")):
                    sp.dma_start(to[:], a[src]).then_inc(s_w, 16)
                for to, src, st in ((wg2, "wg2", s_rst[0]), (bg2, "bg2", s_rst[1])):
                    sp.dma_start(to[:], a[src]).then_inc(st, 16)
                with sp.Fori(0, GROUPS) as g:
                    for i, (u0, n) in enumerate(HALF):
                        sp.wait_ge(s_kv, g * GT + u0 + n)
                        sp.dma_start(xT[i][:], c.xnT_d[:, :, ds(g * GN + u0 * P, n * P)]).then_inc(s_xT[i], 16)
                sp.wait_ge(s_kv, TILES + GT)
                with sp.Fori(0, GROUPS) as g:
                    for i, (u0, n) in enumerate(HALF):
                        sp.wait_ge(s_rows, g * GT + u0 + n)
                        at = ds(g * GN + u0 * P, n * P)
                        sp.dma_start(xT[i][:], c.xnT_d[:, :, at]).then_inc(s_in[i], 16)
                        sp.dma_start(x2T[i][:], c.xn2T_d[:, :, at]).then_inc(s_in[i], 16)
                        sp.dma_start(xr[:, u0:u0 + n, :], x_v[:, ds(g * GT + u0, n), :]).then_inc(s_in[i], 16)
                sp.wait_ge(s_sorted, 1)
                sp.dma_start(c.tail_d.rearrange("(p j) -> p j", j=LANE), srt.buf[1][tail_lanes:P, :]).then_inc(s_tail, 16)
                sp.wait_ge(s_tail, 16)
                sp.dma_start(tail[:], c.tail_d.rearrange("(p j) -> p j", p=P)).then_inc(s_tail_ld, 16)
                sp.wait_ge(s_low, 1)
                sp.dma_start(c.low_d.rearrange("(p j) -> p j", p=P), upper[1][:]).then_inc(s_tail, 16)
                sp.wait_ge(s_tail, 32)
                sp.dma_start(srt.buf[1][tail_lanes:P, :], c.low_d.rearrange("(p j) -> p j", j=LANE)).then_inc(s_low_ld, 16)
                sp.dma_start(c.skey_gat[0:P].rearrange("(p j) -> p j", p=1), first[:]).then_inc(s_out, 16)
                sp.wait_ge(s_all, 1)
                sp.dma_start(c.skey_gat[P:P + SORT_N].rearrange("(p j) -> p j", p=P), srt.buf[1][:]).then_inc(s_out, 16)
                sp.wait_ge(s_up, 1)
                sp.dma_start(c.skey_gat[P + SORT_N:P + GAT_N].rearrange("(p j) -> p j", p=P), upper[1][:]).then_inc(s_out, 16)
                sp.wait_ge(s_out, 48)

            @block.gpsimd
            def _(pool):
                nc.gpsimd.iota(selves[:], pattern=[[-1, NS]], base=SELF_N - 1, channel_multiplier=-NS).then_inc(s_ids, 1)
                with pool.Fori(0, PAIRS) as p:
                    for q in range(QUART):
                        pool.wait_ge(s_ix, QUART * p + q + 1)
                        nc.gpsimd.tensor_tensor(tick[:, q:q + 1], c.eps[:], c.eps[:], ALU.add).then_inc(s_tick, SHALF)
                        for u in range(SHALF):
                            pool.indirect_dma_start(msg[:, q, u, 0:D], None, c.xn_tab,
                                                    bass.IndirectOffsetOnAxis(ap=ixs[:, q, u:u + 1], axis=0)).then_inc(s_g[q], 16)

            @block.vector
            def _(v):
                V = nc.vector

                def tiles_of(at):
                    return nc.values_load_multi_w_load_instructions(
                        t.tile[0:1, ds(at, SBLK)], engines=[DVE_ENGINE], min_val=0, max_val=TILES - 1,
                        skip_runtime_bounds_check_because="at most the last tile by a min")[1]

                def sums(at, odd, tiles, u0, u1):
                    for u in range(u0, u1):
                        v.wait_ge(s_mm, at + u + 1 + 2 * SBLK)
                        v.wait_ge(s_acc, at + u + BANKS)
                        own = acc[:, ds(tiles[u] * ROWW, ROWW)]
                        V.tensor_tensor(own, own, bank[u % BANKS][:, 0:ROWW], ALU.add).then_inc(s_acc, 1)
                        if u % SHALF == SHALF - 1:
                            v.wait_ge(s_tick, at + u + 1)
                            V.tensor_copy(ixs[:, 2 * odd + u // SHALF, :],
                                          t.idx[:, ds(at + u + 1 - SHALF + 2 * SBLK, SHALF)]).then_inc(s_ix, 1)

                def gated(g, i):
                    n = HALF[i][1] * P
                    v.wait_ge(s_gate, 4 * g + 2 * i + KC)
                    for h in range(KC):
                        v.wait_ge(s_at, 4 * g + 2 * i + h + 1)
                        last = V.tensor_tensor(prod[:, h, 0:n], mix[1 - h][:, 0:n], gate[:, h, 0:n], ALU.mult)
                    last.then_inc(s_prod, 1)

                for q in range(QUART):
                    V.tensor_copy(ixs[:, q, :], t.idx[:, q * SHALF:(q + 1) * SHALF]).then_inc(s_ix, 1)
                v.sem_inc(s_acc, BANKS)
                v.sem_inc(s_prod, 1)
                V.memset(msg[:, :, :, D:ROWW], 1.0)
                V.memset(zeros[:], 0.0)
                V.memset(first[:], SENTINEL)
                V.tensor_copy(blk_i[:], c.iota_row[:])
                V.tensor_scalar(own_i[:], c.iota_col[:], HD.bit_length() - 1, None, ALU.arith_shift_right)
                v.drain()
                v.sem_inc(s_init, 1)
                V.tensor_scalar(blk_i[:], blk_i[:], HD.bit_length() - 1, None, ALU.arith_shift_right)
                V.tensor_copy(own_f[:], own_i[:])
                v.drain()
                V.tensor_copy(blk_f[:], blk_i[:])
                v.drain()
                V.tensor_scalar(bd[:], blk_f[:], own_f[:], None, ALU.is_equal)
                v.wait_ge(s_edges, 32)
                V.tensor_scalar(dst, dst, SRC_BITS, OFF | EDGE, ALU.logical_shift_left, ALU.bitwise_or)
                v.drain()
                V.tensor_tensor(srt.buf[0][:].bitcast(I32), srt.buf[0][:].bitcast(I32), dst, ALU.bitwise_or)
                v.drain()
                srt.first_sign(v)

                stages = len(srt.STAGES)

                def lanes(at, i):
                    sums(at, i % 2, tiles_of(at), 0, SBLK)
                    for k in range(i * stages // SHARES, (i + 1) * stages // SHARES):
                        srt.lane_stage(v, k)

                for i in range(SHARES - 2):
                    lanes(i * SBLK, i)
                with v.Fori(SHARES // 2 - 1, MID_PAIR) as p:
                    for odd in range(2):
                        at = p * (2 * SBLK) + odd * SBLK
                        sums(at, odd, tiles_of(at), 0, SBLK)
                v.drain()
                v.wait_ge(s_ctx, TILES + 2)
                for h in range(KC):
                    V.reciprocal(rz[:, h:h + 1], mix[1][:, h * CW + P:h * CW + CW])
                v.drain()
                for h in range(KC):
                    last = V.scalar_tensor_tensor(ctxbd[:, h, :], mix[1][:, h * CW:h * CW + P], rz[:, h:h + 1],
                                                  bd[:], ALU.mult, ALU.mult)
                last.then_inc(s_bd, 1)
                for i in range(2):
                    lanes((2 * MID_PAIR + i) * SBLK, SHARES - 2 + i)
                v.wait_ge(s_m, 1)
                V.tensor_copy(m_sb[:], mix[0][:, :].rearrange("p (k d) -> p k d", k=KC)).then_inc(s_msb, 1)

                with v.Fori(0, GROUPS) as g:
                    m = g + 1
                    at = C_PAIR * 2 * SBLK + g * (4 * SBLK)
                    srt.ask(v, m)
                    tiles = tiles_of(at)
                    sums(at, 0, tiles, 0, 4)
                    v.drain()
                    v.wait_ge(srt.s_turned, 2 * m - 1)
                    srt.across_stage(v, m, 0)
                    for i in range(1, 4):
                        sums(at, 0, tiles, 4 * i, 4 * i + 4)
                        srt.across_stage(v, m, i)
                    gated(g, 0)
                    at = at + SBLK
                    tiles = tiles_of(at)
                    sums(at, 1, tiles, 0, 4)
                    srt.across_stage(v, m, 4)
                    srt.across_stage(v, m, 5)
                    sums(at, 1, tiles, 4, 8)
                    srt.across_stage(v, m, 6)
                    srt.ask_back(v)
                    sums(at, 1, tiles, 8, 16)
                    v.drain()
                    v.wait_ge(srt.s_turned, 2 * m)
                    srt.along_stage(v, 0)
                    at = at + SBLK
                    tiles = tiles_of(at)
                    for i in range(4):
                        sums(at, 0, tiles, 4 * i, 4 * i + 4)
                        srt.along_stage(v, 1 + i)
                    gated(g, 1)
                    at = at + SBLK
                    tiles = tiles_of(at)
                    for i in range(2):
                        sums(at, 1, tiles, 4 * i, 4 * i + 4)
                        srt.along_stage(v, 5 + 2 * i)
                        srt.along_stage(v, 6 + 2 * i)
                    sums(at, 1, tiles, 8, 12)
                    srt.along_stage(v, 9)
                    sums(at, 1, tiles, 12, 16)
                    v.drain()
                v.sem_inc(s_sorted, 1)

                v.wait_ge(s_ids, 1)
                V.tensor_scalar(pad[:], selves[:], N_NODES, PAD_DST, ALU.is_ge, ALU.mult)
                v.drain()
                V.tensor_tensor(selves[:], selves[:], pad[:], ALU.max)
                v.drain()
                V.tensor_scalar(selves[:], selves[:], SRC_BITS, OFF, ALU.logical_shift_left, ALU.bitwise_or)
                rest = R_PAIR * 2 * SBLK
                sums(rest, 0, tiles_of(rest), 0, SBLK)
                v.wait_ge(s_tail_ld, 16)
                V.tensor_tensor(upper[1][:], tail[:], selves[:].bitcast(F32), ALU.min)
                V.tensor_tensor(tail[:], tail[:], selves[:].bitcast(F32), ALU.max)
                v.drain()
                v.sem_inc(s_low, 1)
                sums(rest + SBLK, 1, tiles_of(rest + SBLK), 0, SBLK)
                v.drain()
                v.wait_ge(s_low_ld, 16)
                srt.ask(v, MERGES)
                v.wait_ge(srt.s_turned, T_LAST + 1)
                for i in range(LANE_BITS):
                    srt.across_stage(v, MERGES, i)
                srt.ask_back(v)
                sums(rest + 2 * SBLK, 0, tiles_of(rest + 2 * SBLK), 0, SBLK)
                v.drain()
                v.wait_ge(srt.s_turned, T_LAST + 2)
                for i in range(ALONG):
                    srt.along_stage(v, i)
                v.sem_inc(s_all, 1)
                v.sem_inc(srt.s_ready, 1)
                v.wait_ge(srt.s_turned, T_LAST + 3)
                srt.compare_psum(v, upper_t[0][:], psS[0:NS, 0:P], P >> 1)
                for i in range(1, LANE_BITS):
                    srt.compare(v, upper_t[i % 2][:], upper_t[1 - i % 2][:], P >> (i + 1))
                v.sem_inc(srt.s_ready, 1)
                v.wait_ge(srt.s_turned, T_LAST + 4)
                srt.compare_psum(v, upper[0][:], psS[:, 0:NS], NS >> 1)
                for i in range(1, NS.bit_length() - 1):
                    srt.compare(v, upper[i % 2][:], upper[1 - i % 2][:], NS >> (i + 1))
                v.sem_inc(s_up, 1)
                sums(rest + 3 * SBLK, 1, tiles_of(rest + 3 * SBLK), 0, SBLK)

            @block.tensor
            def _(pe):
                def steps(p, k, u0, u1):
                    half = QUART * p + k
                    if u0 == 0:
                        pe.wait_ge(s_hot, half + 1)
                        pe.wait_ge(s_g[k], 16 * SHALF * p + 16 * SHALF)
                    for u in range(u0, u1):
                        pe.wait_ge(s_acc, half * SHALF + u + 1)
                        nc.tensor.matmul(bank[u % BANKS][:, 0:ROWW], hot[:, k, u, :], msg[:, k, u, :],
                                         start=True, stop=True).then_inc(s_mm, 1)

                def pair(p):
                    for k in range(QUART):
                        steps(p, k, 0, SHALF)

                def kv(g, u):
                    i, at = tile_of(u)
                    if u in (0, HALF[1][0]):
                        pe.wait_ge(s_xT[i], 16 * g + 16)
                    pe.wait_ge(s_ev, g * GT + u + 1)
                    b = mix[0]
                    for k in range(KC):
                        nc.tensor.matmul(b[:, :], xT[i][:, k, at:at + P], wqkv[:, k, D:3 * D], start=(k == 0), stop=False,
                                         skip_group_check=True)
                    nc.tensor.matmul(b[:, 0:D], c.ones[0:1, :], ncm[:], start=False, stop=True,
                                     skip_group_check=True).then_inc(s_kv, 1)

                def context(g, u):
                    pe.wait_ge(s_ev, g * GT + u + 2)
                    for h in range(KC):
                        last = nc.tensor.matmul(mix[1][:, h * CW:(h + 1) * CW], ke[:, u % 2, h * P:(h + 1) * P], vm[:, u % 2, h, :],
                                                start=False, stop=False, skip_group_check=True)
                    last.then_inc(s_ctx, 1)

                def hidden(g, i):
                    n = HALF[i][1] * P
                    pe.wait_ge(s_in[i], 48 * g + 48)
                    pe.wait_ge(s_copied, g * GT + HALF[i][0] + GT)
                    for k in range(KC):
                        last = nc.tensor.matmul(mix[0][0:GATE_H, 0:n], wg1[:, k, :], x2T[i][:, k, :], start=(k == 0),
                                                stop=(k == KC - 1))
                    last.then_inc(s_hgp, 1)

                def gates(g, i, h):
                    n = HALF[i][1] * P
                    pe.wait_ge(s_hg, 2 * g + i + 1)
                    nc.tensor.matmul(mix[1 - h][:, 0:n], wg2[:, h * P:(h + 1) * P], hg[:, 0:n], start=True,
                                     stop=True).then_inc(s_gp, 1)

                def attention(g, i):
                    n = HALF[i][1] * P
                    for h in range(KC):
                        pe.wait_ge(s_gate, 4 * g + 2 * i + h + 1)
                        for k in range(KC):
                            last = nc.tensor.matmul(mix[1 - h][:, 0:n], m_sb[:, k, h * P:(h + 1) * P], xT[i][:, k, :],
                                                    start=(k == 0), stop=(k == KC - 1))
                        last.then_inc(s_at, 1)

                def output(g, i, j):
                    u = HALF[i][0] + j
                    at = j * P
                    b = mix[j % 2]
                    if j == 0:
                        pe.wait_ge(s_prod, 2 * g + i + 2)
                    elif j >= 2:
                        pe.wait_ge(s_copied, g * GT + u - 1 + GT)
                    for k in range(KC):
                        nc.tensor.matmul(b[:, D:2 * D], xT[i][:, k, at:at + P], wself[:, k, :], start=(k == 0), stop=(k == KC - 1))
                    nc.tensor.matmul(b[:, 0:D], c.ident[:], xr[:, u, :], start=True, stop=False)
                    nc.tensor.matmul(b[:, 0:D], c.ones[0:1, :], bproj[:], start=False, stop=False)
                    for k in range(KC):
                        last = nc.tensor.matmul(b[:, 0:D], prod[:, k, at:at + P], wproj[:, k, :], start=False, stop=(k == KC - 1))
                    last.then_inc(s_rows, 1)

                pe.sem_inc(s_mm, 2 * SBLK)
                pe.sem_inc(s_kv, GT)
                pe.sem_inc(s_ctx, 2)
                pe.sem_inc(s_rows, GT)
                pe.wait_ge(s_init, 1)
                nc.tensor.matmul(mix[1][:, 0:KC * CW], zeros[:, 0:P], zeros[:], start=True, stop=False,
                                 skip_group_check=True)
                pe.wait_ge(s_w, 112)
                for k in range(KC):
                    for h in range(KC):
                        last = nc.tensor.transpose(mix[0][:, h * D + k * P:h * D + (k + 1) * P], wqkv[:, k, h * P:(h + 1) * P], c.ident[:])
                last.then_inc(s_wq, 1)
                pe.wait_ge(s_wqc, 1)
                with pe.Fori(0, LANE_PAIRS) as p:
                    pair(p)
                with pe.Fori(0, GROUPS) as g:
                    for u in range(GT + 1):
                        steps(LANE_PAIRS + g, u // 2, u % 2 * 4, u % 2 * 4 + 4)
                        if u < GT:
                            kv(g, u)
                        if u:
                            context(g, u - 1)
                pair(MID_PAIR)
                pe.wait_ge(s_bd, 1)
                for k in range(KC):
                    for h in range(KC):
                        last = nc.tensor.matmul(mix[0][:, k * D + h * P:k * D + (h + 1) * P], wqT[:, h, k * P:(k + 1) * P], ctxbd[:, h, :],
                                                start=True, stop=True)
                last.then_inc(s_m, 1)
                pe.wait_ge(s_msb, 1)
                pe.wait_ge(s_rst[0], 16)
                with pe.Fori(0, GROUPS) as g:
                    srt.turn_from(pe, 0, 2 * g + 1)
                    for i in range(2):
                        p = C_PAIR + 2 * g + i
                        steps(p, 0, 0, 4)
                        hidden(g, i)
                        steps(p, 0, 4, 8)
                        gates(g, i, 0)
                        steps(p, 1, 0, 4)
                        gates(g, i, 1)
                        steps(p, 1, 4, 8)
                        attention(g, i)
                        for j in range(4):
                            steps(p, 2 + j // 2, j % 2 * 4, j % 2 * 4 + 4)
                            if j < HALF[i][1]:
                                output(g, i, j)
                            if i == 0 and j == 2:
                                srt.turn_from(pe, 1, 2 * g + 2)
                pair(R_PAIR)
                srt.turn_from(pe, 0, T_LAST + 1)
                srt.turn_from(pe, 1, T_LAST + 2)
                for k in range(2):
                    steps(R_PAIR + 1, k, 0, SHALF)
                pe.wait_ge(srt.s_ready, T_LAST + 3)
                nc.tensor.transpose(psS[0:NS, 0:P], tail[:], c.ident[:]).then_inc(srt.s_turned, 1)
                pe.wait_ge(srt.s_ready, T_LAST + 4)
                nc.tensor.transpose(psS[:, 0:NS], upper_t[0][:], c.ident[0:NS, 0:NS]).then_inc(srt.s_turned, 1)
                for k in range(2, QUART):
                    steps(R_PAIR + 1, k, 0, SHALF)

            @block.scalar
            def _(act):
                A = nc.scalar

                def prep(p, k):
                    half = QUART * p + k
                    act.drain()
                    act.wait_ge(s_mm, half * SHALF + SHALF)
                    for u in range(SHALF):
                        A.activation(dif[:, u, :], c.iota_row[:], ACT.Abs, bias=t.nloc[:, ds(half * SHALF + u, 1)])
                    act.drain()
                    A.activation(hot[:, k], dif[:], ACT.Relu, bias=c.ones[:, 0:1], scale=-1.0).then_inc(s_hot, 1)

                def taken(g, u):
                    b = u % 2
                    one = valid[:, ds(g * GT + u, 1)]
                    act.wait_ge(s_kv, g * GT + u + 1 + GT)
                    act.wait_ge(s_ctx, g * GT + u + (2 if u == 0 else 1))
                    A.activation(ke[:, b, :], mix[0][:, 0:D], ACT.Exp)
                    A.copy(vm[:, b, :, P:CW], bcast(one, 1, KC))
                    A.activation(vm[:, b, :, 0:P], mix[0][:, D:2 * D].rearrange("p (h d) -> p h d", h=KC), ACT.Copy,
                                 scale=one).then_inc(s_ev, 1)

                def gates(g, i):
                    n = HALF[i][1] * P
                    act.wait_ge(s_hgp, 2 * g + i + 1)
                    A.activation(hg[:, 0:n], mix[0][0:GATE_H, 0:n], ACT.Gelu, bias=bg1[:]).then_inc(s_hg, 1)
                    act.wait_ge(s_prod, 2 * g + i + 1)
                    for h in range(KC):
                        act.wait_ge(s_gp, 4 * g + 2 * i + h + 1)
                        A.activation(gate[:, h, 0:n], mix[1 - h][:, 0:n], ACT.Sigmoid, bias=bg2[:, h:h + 1]).then_inc(s_gate, 1)

                def copied(g, i, j):
                    u = HALF[i][0] + j
                    act.wait_ge(s_rows, g * GT + u + 1 + GT)
                    if j == 0:
                        act.wait_ge(s_rst[i], 16 * g + 16)
                    A.copy(rows[:, u, :], mix[j % 2][:, :]).then_inc(s_copied, 1)

                act.sem_inc(s_ev, 1)
                act.sem_inc(s_copied, GT)
                for k in range(2):
                    prep(0, k)
                act.wait_ge(s_wq, 1)
                A.copy(wqT[:], mix[0][:, :].rearrange("p (h d) -> p h d", h=KC)).then_inc(s_wqc, 1)
                act.wait_ge(s_w, 112)
                def pair(p):
                    for k in range(QUART):
                        prep(p + (k + 2) // QUART, (k + 2) % QUART)

                with act.Fori(0, LANE_PAIRS) as p:
                    pair(p)
                with act.Fori(0, GROUPS) as g:
                    for k in range(QUART):
                        prep(LANE_PAIRS + g + (k + 2) // QUART, (k + 2) % QUART)
                        for u in range(2 * k, min(2 * k + 2, GT)):
                            taken(g, u)
                pair(MID_PAIR)
                act.wait_ge(s_rst[0], 16)
                act.wait_ge(s_rst[1], 16)
                with act.Fori(0, GROUPS) as g:
                    for i, (u0, n) in enumerate(HALF):
                        p = C_PAIR + 2 * g + i
                        prep(p, 2)
                        gates(g, i)
                        prep(p, 3)
                        prep(p + 1, 0)
                        copied(g, i, 0)
                        copied(g, i, 1)
                        prep(p + 1, 1)
                        for j in range(2, n):
                            copied(g, i, j)
                        act.wait_ge(s_copied, g * GT + u0 + n + GT)
                        act.dma_start(rows_v[:, ds(g * GT + u0, n), :], rows[:, u0:u0 + n, :]).then_inc(s_rst[i], 16)
                with act.Fori(R_PAIR, PAIRS - 1) as p:
                    pair(p)
                for k in range(2, QUART):
                    prep(PAIRS - 1, k)
                for i in range(2):
                    act.wait_ge(s_rst[i], 16 * GROUPS + 16)


class GatPlan:

    def __init__(self, sb):
        self.width = sb("gat_width", [P, 2], I32)
        self.gap = sb("gat_gap", [P, 1])
        self.idx = sb("gat_src", [P, W + SBLK], I32)
        self.dst = sb("gat_dst", [P, W + 1])
        self.selfm = sb("gat_self", [P, W])
        self.first = sb("gat_first", [P, 1], I32)
        self.place = sb("gat_place", [P, TILES])
        self.lane = sb("gat_lane", [P, TILES])
        self.endpos = sb("gat_endpos", [P, TILES], I32)
        self.top = sb("gat_top", [P, HEADS])
        self.sums = sb("gat_sums", [P, NV])
        self.through = sb("gat_through", [P, 1])
        self.into = sb("gat_into", [P, 1])


def load_lanes(eng, wide, to, keys, c0, c1, sem):
    for w, case in ((W, wide > 0), (W_LOW, wide < 1)):
        with eng.If(case):
            n = min(c1, w)
            eng.dma_start(to[:, 0:n - c0], keys[0:P * w].rearrange("(p w) -> p w", p=P)[:, c0:n].bitcast(I32)).then_inc(sem, 16)


def gnn_out(c, a, acc, plan):
    nc = c.nc
    ROWW = D + 1
    ctx, sb, ps = c.open()
    with ctx:
        wneigh = sb("go_wneigh", [P, KC, D])
        wg = sb("go_wg", [P, KC, ROW])
        b_gnn = sb("go_b", [1, D])
        att = sb("go_att", [P, 2, HE])
        prod = sb("go_att_prod", [P, HE])
        rdeg = sb("go_rdeg", [P, TILES])
        hn = sb("go_hn", [P, GT, D])
        hnT = sb("go_hnT", [P, GT, KC, P])
        base = sb("go_base", [P, GT, 2 * D])
        z = sb("go_z", [P, 2, D])
        x2 = sb("go_x2", [P, GT, D])
        y = sb("go_y", [P, GT, D])
        yT = sb("go_yT", [P, KC, GN])
        hx = sb("go_hx", [P, GT, ROW])
        stats = sb("go_stats", [P, GT, 6])
        mv = sb("go_mv", [P, GT, 2])
        std = sb("go_std", [P, GT])
        rstd = sb("go_rstd", [P, GT])
        chunks = sb("go_chunks", [FENCE_P, FENCES // FENCE_P, P], I32)
        first_i = sb("go_first_i", [FENCE_P, FENCES // FENCE_P], I32)
        first_f = sb("go_first_f", [FENCE_P, FENCES // FENCE_P])
        first_row = sb("go_first_row", [P, FENCES])
        reached = sb("go_reached", [P, FENCES])
        reach = sb("go_reach", [P, GT])
        chunk_i = sb("go_chunk_i", [P, GT], I32)
        tick = sb("go_tick", [P, 1])
        ends = sb("go_ends", [P, GT, P])
        inside = sb("go_inside", [P, GT])
        node_i = sb("go_node_i", [P, TILES], I32)
        node_f = sb("go_node_f", [P, TILES])
        probe = sb("go_probe", [P, 1], I32)
        wide_f = sb("go_wide_f", [P, 1])
        keys = sb("go_keys", [P, W + 1], I32)
        src_i = sb("go_src_i", [P, W], I32)
        edge_i = sb("go_edge_i", [P, W], I32)
        edge_f = sb("go_edge_f", [P, W])
        s_probe, s_wide, s_keys, s_node, s_chunk, s_tick, s_ends = (c.sem("go_" + n) for n in (
            "probe", "wide", "keys", "node", "chunk", "tick", "ends"))
        s_chunks, s_first, s_first_st, s_firsts = (c.sem("go_" + n) for n in ("chunks", "first", "first_st", "firsts"))
        first_d = c.dram("go_first_d", [FENCES])
        psT = [ps(f"go_psT{i}", [P, 512]) for i in range(2)]
        psZ = [ps(f"go_psZ{i}", [P, 512]) for i in range(2)]
        psY = [ps(f"go_psY{i}", [P, 512]) for i in range(2)]
        psH = [ps(f"go_psH{i}", [P, 512]) for i in range(2)]
        s_base = [c.sem(f"go_base_in{i}") for i in range(2)]
        s_w, s_wg, s_hn, s_hnT, s_hnc, s_z, s_x2 = (c.sem("go_" + n) for n in (
            "w", "wg", "hn", "hnT", "hnc", "z", "x2"))
        s_mv, s_std, s_y, s_yT, s_yc, s_hx, s_hxc = (c.sem("go_" + n) for n in (
            "mv", "std", "y", "yT", "yc", "hx", "hxc"))
        s_yst, s_hxst = c.sem("go_yst"), c.sem("go_hxst")
        s_x2st = [c.sem(f"go_x2st{i}") for i in range(2)]
        base_v = c.base_d.rearrange("(t p) d -> p t d", p=P)
        x2_v = c.x2_d.rearrange("(t p) d -> p t d", p=P)
        hx_v = c.hx_d.rearrange("(t p) d -> p t d", p=P)
        acc_v = acc[:].rearrange("p (t d) -> p t d", t=TILES)

        def slot(g, u):
            return g * GT + u + (2 if u == 0 else 1)

        with nc.Block() as block:
            @block.sync
            def _(sp):
                sp.dma_start(chunks[:], c.skey_gat[P:P + GAT_N].rearrange("(p w e) -> p w e", p=FENCE_P, e=P).bitcast(I32)).then_inc(s_chunks, 16)
                at = P + P * W_LOW
                sp.dma_start(probe[:], c.skey_gat[at:at + 1].rearrange("(o n) -> o n", o=1).to_broadcast([P, 1]).bitcast(I32)).then_inc(s_probe, 16)
                sp.dma_start(att[:, 0, :], a["att_src"].to_broadcast([P, HE])).then_inc(s_w, 16)
                sp.dma_start(wneigh[:], a["wneigh"].rearrange("(k p) n -> p k n", p=P)).then_inc(s_x2st[0], 16)
                sp.dma_start(wg[:, :, 0:HE], a["w_gat"].rearrange("(k p) n -> p k n", p=P)).then_inc(s_x2st[1], 16)
                sp.dma_start(b_gnn[:], a["b_gnn"]).then_inc(s_yst, 16)
                sp.dma_start(att[:, 1, :], a["att_dst"].to_broadcast([P, HE])).then_inc(s_hxst, 16)
                for i, (u0, n) in enumerate(HALF):
                    sp.dma_start(base[:, u0:u0 + n, :], base_v[:, u0:u0 + n, :]).then_inc(s_base[i], 16)
                with sp.Fori(0, GROUPS - 1) as g:
                    for i, (u0, n) in enumerate(HALF):
                        sp.wait_ge(s_x2, g * GT + u0 + n + GT)
                        sp.dma_start(x2_v[:, ds(g * GT + u0, n), :], x2[:, u0:u0 + n, :]).then_inc(s_x2st[i], 16)
                        sp.dma_start(base[:, u0:u0 + n, :], base_v[:, ds(g * GT + u0 + GT, n), :]).then_inc(s_base[i], 16)
                for i, (u0, n) in enumerate(HALF):
                    sp.wait_ge(s_x2, TILES + u0 + n)
                    sp.dma_start(x2_v[:, TILES - GT + u0:TILES - GT + u0 + n, :], x2[:, u0:u0 + n, :]).then_inc(s_x2st[i], 16)
                for i in range(2):
                    sp.wait_ge(s_x2st[i], 16 * GROUPS + 16)

            @block.gpsimd
            def _(pool):
                nc.gpsimd.iota(node_i[:], pattern=[[P, TILES]], base=0, channel_multiplier=1).then_inc(s_node, 1)
                pool.wait_ge(s_first, 1)
                pool.dma_start(first_d.rearrange("(p w) -> p w", p=FENCE_P), first_f[:]).then_inc(s_first_st, 16)
                pool.wait_ge(s_first_st, 16)
                pool.dma_start(first_row[:], first_d.rearrange("(o n) -> o n", o=1).to_broadcast([P, FENCES])).then_inc(s_firsts, 16)
                pool.wait_ge(s_wide, 1)
                wide = pool.value_load(plan.width[0:1, 0:1], min_val=0, max_val=1)
                load_lanes(pool, wide, keys[:, 0:2], c.skey_gat[P - 1:P + GAT_N - 1], 0, 2, s_keys)
                load_lanes(pool, wide, keys[:, 2:W + 1], c.skey_gat[P:P + GAT_N], 1, W, s_keys)
                with pool.Fori(0, GROUPS) as g:
                    pool.wait_ge(s_chunk, g + 1)
                    nc.gpsimd.tensor_tensor(tick[:], c.eps[:], c.eps[:], ALU.add).then_inc(s_tick, 1)
                    for u in range(GT):
                        pool.indirect_dma_start(ends[:, u, :], None, c.skey_gat.rearrange("(c e) -> c e", e=P),
                                                bass.IndirectOffsetOnAxis(ap=chunk_i[:, u:u + 1], axis=0)).then_inc(s_ends, 16)

            @block.vector
            def _(v):
                v.sem_inc(s_x2, GT)
                nc.vector.tensor_scalar(rdeg[:], acc_v[:, :, D], 1.0, None, ALU.max)
                v.drain()
                nc.vector.reciprocal(rdeg[:], rdeg[:])
                for loaded in (s_w, s_yst, s_hxst, *s_x2st):
                    v.wait_ge(loaded, 16)
                for i in range(2):
                    for k in range(KC):
                        nc.vector.tensor_tensor(prod[:], wg[:, k, 0:HE], att[:, i, :], ALU.mult)
                        v.drain()
                        last = nc.vector.tensor_reduce(wg[:, k, HE + i * HEADS:HE + (i + 1) * HEADS],
                                                       prod[:].rearrange("p (h e) -> p h e", h=HEADS), AX_X, ALU.add)
                        v.drain()
                v.sem_inc(s_wg, 1)
                v.wait_ge(s_chunks, 16)
                nc.vector.tensor_scalar(first_i[:], chunks[:, :, 0], SRC_BITS, DST_MASK, ALU.logical_shift_right, ALU.bitwise_and)
                v.drain()
                nc.vector.tensor_copy(first_f[:], first_i[:]).then_inc(s_first, 1)
                nc.vector.memset(keys[:, W_LOW + 1:W + 1], 0)
                v.wait_ge(s_probe, 16)
                nc.vector.tensor_scalar(probe[:], probe[:], SRC_BITS, DST_MASK, ALU.logical_shift_right, ALU.bitwise_and)
                v.drain()
                nc.vector.tensor_scalar(wide_f[:], probe[:], float(N_NODES), None, ALU.is_lt)
                v.drain()
                nc.vector.tensor_copy(plan.width[:, 0:1], wide_f[:])
                nc.vector.tensor_scalar(plan.width[:, 1:2], wide_f[:], float(W - W_LOW), float(W_LOW - 1), ALU.mult, ALU.add)
                nc.vector.tensor_scalar(plan.gap[:], wide_f[:], -float(W - W_LOW), float(W - W_LOW), ALU.mult, ALU.add)
                v.wait_ge(s_node, 1)
                nc.vector.tensor_copy(node_f[:], node_i[:])
                v.drain()
                v.sem_inc(s_wide, 1)
                nc.vector.tensor_scalar(node_i[:], node_i[:], SRC_BITS, OFF | SRC_MASK, ALU.logical_shift_left, ALU.bitwise_or)
                v.drain()

                def places(g):
                    v.wait_ge(s_tick, g + 1)
                    v.wait_ge(s_ends, 16 * GT * g + 16 * GT)
                    nc.vector.tensor_tensor(ends[:], ends[:], bcast(node_i[:, ds(g * GT, GT)].bitcast(F32), 2, P), ALU.is_le)
                    v.drain()
                    nc.vector.tensor_reduce(inside[:], ends[:], AX_X, ALU.add)
                    v.drain()
                    place = plan.place[:, ds(g * GT, GT)]
                    nc.vector.tensor_tensor(place, place, inside[:], ALU.add)

                def group(g, first=False):
                    for u in range(GT):
                        for i, (u0, n) in enumerate(HALF):
                            if u == u0:
                                v.wait_ge(s_base[i], 16 * g + 16)
                                v.wait_ge(s_x2st[i], 16 * g + 16)
                        v.wait_ge(s_z, g * GT + u + 1 + GT)
                        nc.vector.tensor_tensor(z[:, u % 2, :], psZ[u % 2][:, 0:D], base[:, u, D:2 * D], ALU.add)
                        v.drain()
                        nc.vector.scalar_tensor_tensor(x2[:, u, :], z[:, u % 2, :], 0.0, base[:, u, 0:D], ALU.max,
                                                       ALU.add).then_inc(s_x2, 1)
                        nc.vector.tensor_scalar(reached[:], first_row[:], node_f[:, ds(g * GT + u, 1)], None, ALU.is_le, ALU.add,
                                                accum_out=reach[:, u:u + 1])
                        v.drain()
                        nc.vector.bn_stats(stats[:, u, :], x2[:, u, :])
                    nc.vector.tensor_scalar(plan.place[:, ds(g * GT, GT)], reach[:], float(P), None, ALU.mult)
                    v.drain()
                    for u in range(GT):
                        agg = nc.vector.bn_aggr(mv[:, u, :], stats[:, u, :])
                    agg.then_inc(s_mv, 1)
                    v.wait_ge(s_std, g + 1)
                    nc.vector.reciprocal(rstd[:], std[:])
                    v.drain()
                    v.wait_ge(s_yT, g * GT + 2)
                    for u in range(GT):
                        nc.vector.tensor_scalar(y[:, u, :], x2[:, u, :], mv[:, u, 0:1], rstd[:, u:u + 1],
                                                ALU.subtract, ALU.mult).then_inc(s_y, 1)
                    if not first:
                        places(g - 1)
                    nc.vector.tensor_copy(chunk_i[:], reach[:]).then_inc(s_chunk, 1)
                    v.drain()

                v.wait_ge(s_firsts, 16)
                group(0, first=True)
                with v.Fori(1, GROUPS - 1) as g:
                    group(g)
                group(GROUPS - 1)
                v.wait_ge(s_keys, 32)
                nc.vector.tensor_scalar(src_i[:], keys[:, 1:W + 1], EDGE - 1, None, ALU.bitwise_and)
                nc.vector.tensor_scalar(edge_i[:], keys[:, 1:W + 1], EDGE, None, ALU.bitwise_and)
                v.drain()
                nc.vector.tensor_scalar(keys[:], keys[:], SRC_BITS, DST_MASK, ALU.logical_shift_right, ALU.bitwise_and)
                v.drain()
                nc.vector.tensor_copy(plan.dst[:], keys[:])
                nc.vector.tensor_copy(edge_f[:], edge_i[:])
                nc.vector.tensor_copy(reached[:], src_i[:])
                v.drain()
                nc.vector.tensor_scalar(plan.selfm[:], edge_f[:], 0.0, None, ALU.is_equal)
                nc.vector.tensor_scalar(plan.first[:], plan.dst[:, 1:2], float(N_NODES - 1), None, ALU.min)
                v.drain()
                nc.vector.tensor_tensor(edge_f[:], plan.dst[:, 1:W + 1], plan.selfm[:], ALU.mult)
                v.drain()
                nc.vector.tensor_tensor(reached[:], reached[:], edge_f[:], ALU.add)
                v.drain()
                nc.vector.tensor_scalar(plan.idx[:, 0:W], reached[:], float(N_NODES - 1), None, ALU.min)
                nc.vector.memset(plan.idx[:, W:W + SBLK], 0)
                places(GROUPS - 1)
                v.drain()
                nc.vector.tensor_scalar(plan.place[:], plan.place[:], -float(P + 1), None, ALU.add)
                v.drain()

            @block.scalar
            def _(act):
                act.sem_inc(s_hnc, 2)
                act.sem_inc(s_yc, 2)
                act.sem_inc(s_hxc, 2)

                def means(g):
                    act.wait_ge(s_hnT, g * GT + 2)
                    for u in range(GT):
                        at = g * GT + u
                        nc.scalar.activation(hn[:, u, :], acc[:, ds(at * ROWW, D)], ACT.Copy,
                                             scale=rdeg[:, ds(at, 1)]).then_inc(s_hn, 1)

                def mean_out(g, u):
                    act.wait_ge(s_hnT, g * GT + u + 3)
                    act.wait_ge(s_z, g * GT + u + 1)
                    nc.scalar.copy(hnT[:, u], psT[u % 2][:, 0:D].rearrange("p (k n) -> p k n", k=KC)).then_inc(s_hnc, 1)

                def y_out(g, u):
                    if u == 0:
                        act.wait_ge(s_yst, 16 * g + 16)
                        act.wait_ge(s_hxst, 16 * g + 16)
                    act.wait_ge(s_yT, g * GT + u + 3)
                    nc.scalar.copy(yT[:, :, u * P:(u + 1) * P],
                                   psY[u % 2][:, 0:D].rearrange("p (k n) -> p k n", k=KC)).then_inc(s_yc, 1)

                def hx_out(g, u):
                    act.wait_ge(s_hx, g * GT + u + 1)
                    nc.scalar.copy(hx[:, u, :], psH[u % 2][:, 0:ROW]).then_inc(s_hxc, 1)

                def stored(g):
                    act.wait_ge(s_yc, g * GT + GT + 2)
                    act.dma_start(c.x2nT_d[:, :, ds(g * GN, GN)], yT[:]).then_inc(s_yst, 16)
                    act.wait_ge(s_hxc, g * GT + GT + 2)
                    act.dma_start(hx_v[:, ds(g * GT, GT), :], hx[:]).then_inc(s_hxst, 16)

                def root(g):
                    act.wait_ge(s_mv, g + 1)
                    nc.scalar.activation(std[:], mv[:, :, 1], ACT.Sqrt, bias=c.eps[:]).then_inc(s_std, 1)

                act.wait_ge(s_wg, 1)
                def beside(g, last=False):
                    mean_out(g, 0)
                    for u in range(GT):
                        if u + 1 < GT:
                            mean_out(g, u + 1)
                        y_out(g - 1, u)
                        if u:
                            hx_out(g - 1, u - 1)
                    hx_out(g - 1, GT - 1)
                    if not last:
                        means(g + 1)
                    root(g)
                    stored(g - 1)

                means(0)
                for u in range(GT):
                    mean_out(0, u)
                means(1)
                root(0)
                with act.Fori(1, GROUPS - 1) as g:
                    beside(g)
                beside(GROUPS - 1, last=True)
                for u in range(GT):
                    y_out(GROUPS - 1, u)
                    if u:
                        hx_out(GROUPS - 1, u - 1)
                hx_out(GROUPS - 1, GT - 1)
                stored(GROUPS - 1)
                act.wait_ge(s_yst, 16 * GROUPS + 16)
                act.wait_ge(s_hxst, 16 * GROUPS + 16)

            @block.tensor
            def _(pe):
                pe.sem_inc(s_hnT, 2)
                pe.sem_inc(s_z, GT)
                pe.sem_inc(s_yT, 2)
                pe.wait_ge(s_wg, 1)

                def turn_mean(g, u):
                    pe.wait_ge(s_hn, g * GT + u + 1)
                    pe.wait_ge(s_hnc, slot(g, u))
                    for k in range(KC):
                        last = nc.tensor.transpose(psT[u % 2][:, k * P:(k + 1) * P], hn[:, u, k * P:(k + 1) * P], c.ident[:])
                    last.then_inc(s_hnT, 1)

                def rows_of(g, u):
                    pe.wait_ge(s_yc, g * GT + u + 3)
                    pe.wait_ge(s_hxc, slot(g, u))
                    for k in range(KC):
                        last = nc.tensor.matmul(psH[u % 2][:, 0:ROW], yT[:, k, u * P:(u + 1) * P], wg[:, k, :],
                                                start=(k == 0), stop=(k == KC - 1))
                    last.then_inc(s_hx, 1)

                def neighbours(g, u):
                    pe.wait_ge(s_hnc, g * GT + u + 3)
                    pe.wait_ge(s_x2, slot(g, u) + GT - 2)
                    nc.tensor.matmul(psZ[u % 2][:, 0:D], c.ones[0:1, :], b_gnn[:], start=True, stop=False)
                    for k in range(KC):
                        last = nc.tensor.matmul(psZ[u % 2][:, 0:D], hnT[:, u, k, :], wneigh[:, k, :],
                                                start=False, stop=(k == KC - 1))
                    last.then_inc(s_z, 1)

                def turn_y(g, u):
                    pe.wait_ge(s_y, g * GT + u + 1)
                    pe.wait_ge(s_yc, slot(g, u))
                    for k in range(KC):
                        last = nc.tensor.transpose(psY[u % 2][:, k * P:(k + 1) * P], y[:, u, k * P:(k + 1) * P], c.ident[:])
                    last.then_inc(s_yT, 1)

                def both(first, second):
                    if first is not None:
                        turn_mean(first, 0)
                        turn_mean(first, 1)
                    for u in range(GT):
                        if first is not None and u + 2 < GT:
                            turn_mean(first, u + 2)
                        if second is not None:
                            turn_y(second, u)
                        if first is not None:
                            neighbours(first, u)
                        if second is not None and u:
                            rows_of(second, u - 1)
                    if second is not None:
                        rows_of(second, GT - 1)

                both(0, None)
                with pe.Fori(1, GROUPS) as g:
                    both(g, g - 1)
                both(None, GROUPS - 1)


def gat_gather_experts(c, a, plan):
    nc = c.nc
    FB, YB = 4, 4
    BLK_ITERS = BLOCK // SBLK
    BLOCKS = W_LOW // BLOCK
    AHEAD = 4
    tail = [(BLOCKS * BLOCK, LAST), (W_LOW, BLOCK), (W_LOW + BLOCK, BLOCK_MAX)]
    ctx, sb, ps = c.open()
    with ctx:
        G = sb("edge_rows", [P, W, ROW])
        ring = sb("gg_ring", [P, 2, SHALF, ROW])
        ixs = sb("gg_ixs", [P, 2, SHALF], I32)
        tick = sb("gg_tick", [P, 2])
        s_blank, s_ix, s_tick = (c.sem("gg_" + n) for n in ("blank", "ix", "tick_done"))
        s_g = [c.sem(f"gg_rows{h}") for h in range(2)]

        keep = sb("gs_keep", [P, W])
        start = sb("gs_start", [P, W])
        first_row = sb("gs_first_row", [P, ROW])
        dlast = sb("gs_dlast", [P, HEADS])
        own = sb("gs_own", [P, HEADS, BLOCK_MAX])
        dlog = sb("gs_dlog", [P, HEADS, BLOCK_MAX])
        logit = sb("gs_logit", [P, HEADS, BLOCK_MAX])
        top = sb("gs_top", [P, HEADS, BLOCK_MAX + 1])
        ex = sb("gs_ex", [P, 2, HEADS, BLOCK_MAX])
        bound = sb("gs_bound", [P, P])
        width_f = sb("gs_width_f", [P, 1])
        past = sb("gs_past", [P, GT, P])
        s_first, s_x, s_ex, s_done, s_st, s_blankst = (c.sem("gs_" + n) for n in (
            "first", "x", "ex", "done", "st", "blankst"))
        sums_v = c.sums_d.rearrange("(p w) r -> p w r", p=P)

        w1 = sb("ex_w1", [P, EXPERTS, KC, HID])
        w2 = sb("ex_w2", [P, EXPERTS, HC, D])
        b1 = sb("ex_b1", [P, EXPERTS * HC])
        yT = sb("ex_yT", [P, KC, GN])
        hh = sb("ex_hh", [P, HC, 2, GN // 2])
        yo = sb("ex_yo", [P, GT, D])
        psF = [ps(f"ex_psF{i}", [P, 512]) for i in range(FB)]
        psY = [ps(f"ex_psY{i}", [P, 512]) for i in range(YB)]
        s_w, s_yT, s_f, s_ge, s_s, s_yc, s_yst = (c.sem("ex_" + n) for n in (
            "w", "yT", "f", "ge", "s", "yc", "yst"))
        NF, NS = 2 * HC, GT
        with nc.Block() as block:
            @block.sync
            def _(sp):
                def store(at, n):
                    sp.dma_start(sums_v[:, ds(at, n), :], G[:, ds(at, n), :]).then_inc(s_st, 16)

                wide = sp.value_load(plan.width[0:1, 0:1], min_val=0, max_val=1)
                sp.dma_start(yT[:], c.x2nT_d[:, :, 0:GN]).then_inc(s_yT, 16)
                for e in range(EXPERTS):
                    sp.dma_start(w1[:, e], a["w1"][e].rearrange("(k p) n -> p k n", p=P)).then_inc(s_w, 16)
                    sp.dma_start(w2[:, e], a["w2"][e].rearrange("(k p) n -> p k n", p=P)).then_inc(s_w, 16)
                sp.dma_start(b1[:], a["b1"]).then_inc(s_w, 16)
                sp.wait_ge(s_blank, 1)
                sp.dma_start(sums_v[:, W_LOW:W, :], G[:, W_LOW:W, :]).then_inc(s_blankst, 16)
                with sp.Fori(1, GROUPS) as g:
                    sp.wait_ge(s_f, g * EXPERTS * NF)
                    sp.dma_start(yT[:], c.x2nT_d[:, :, ds(g * GN, GN)]).then_inc(s_yT, 16)
                    sp.wait_ge(s_done, g)
                    store((g - 1) * BLOCK, BLOCK)
                sp.wait_ge(s_done, BLOCKS)
                store((BLOCKS - 1) * BLOCK, BLOCK)
                sp.wait_ge(s_done, BLOCKS + 1)
                store(*tail[0])
                sp.wait_ge(s_blankst, 16)
                with sp.If(wide > 0):
                    for i in (1, 2):
                        sp.wait_ge(s_done, BLOCKS + 1 + i)
                        store(*tail[i])
                    sp.wait_ge(s_st, 16 * (BLOCKS + 3))
                sp.wait_ge(s_st, 16 * (BLOCKS + 1))

            @block.gpsimd
            def _(pool):
                pool.indirect_dma_start(first_row[:], None, c.hx_d,
                                        bass.IndirectOffsetOnAxis(ap=plan.first[:], axis=0)).then_inc(s_first, 16)

                def gathers(first, end):
                    with pool.Fori(first, end) as b:
                        for h in range(2):
                            pool.wait_ge(s_ix, 2 * b + h + 1)
                            nc.gpsimd.tensor_tensor(tick[:, h:h + 1], c.eps[:], c.eps[:], ALU.add).then_inc(s_tick, 1)
                            for u in range(SHALF):
                                pool.indirect_dma_start(ring[:, h, u, :], None, c.hx_d,
                                                        bass.IndirectOffsetOnAxis(ap=ixs[:, h, u:u + 1], axis=0)).then_inc(s_g[h], 16)

                gathers(0, LOW_ITERS)
                with pool.If(pool.value_load(plan.width[0:1, 0:1], min_val=0, max_val=1) > 0):
                    gathers(LOW_ITERS, G_ITERS)

            @block.vector
            def _(v):
                V = nc.vector
                wide = v.value_load(plan.width[0:1, 0:1], min_val=0, max_val=1)

                def take(b):
                    for h in range(2):
                        v.wait_ge(s_tick, 2 * b + h + 1)
                        v.wait_ge(s_g[h], 16 * SHALF * b + 16 * SHALF)
                        V.tensor_copy(G[:, ds(b * SBLK + h * SHALF, SHALF), :], ring[:, h])
                        V.tensor_copy(ixs[:, h, :], plan.idx[:, ds(b * SBLK + h * SHALF + SBLK, SHALF)]).then_inc(s_ix, 1)

                def heads(at, n, r0, r1):
                    return G[:, ds(at, n), r0:r1].rearrange("p w r -> p r w")

                def maxima(at, n):
                    kept, begun = keep[:, ds(at, n)], start[:, ds(at, n)]
                    v.drain()
                    V.tensor_tensor(own[:, :, 0:n], heads(at, n, HE + HEADS, ROW), bcast(plan.selfm[:, ds(at, n)], 1, HEADS), ALU.mult)
                    V.tensor_copy(top[:, :, 0], plan.top[:])
                    v.drain()
                    for h in range(HEADS):
                        V.tensor_tensor_scan(dlog[:, h, 0:n], kept, own[:, h, 0:n], dlast[:, h:h + 1], ALU.mult, ALU.add)
                    v.drain()
                    V.tensor_copy(dlast[:], dlog[:, :, n - 1])
                    V.tensor_tensor(own[:, :, 0:n], heads(at, n, HE, HE + HEADS), dlog[:, :, 0:n], ALU.add)
                    v.drain()
                    V.scalar_tensor_tensor(logit[:, :, 0:n], own[:, :, 0:n], 0.2, own[:, :, 0:n], ALU.mult, ALU.max)
                    v.drain()
                    for h in range(HEADS):
                        V.tensor_tensor_scan(top[:, h, 1:n + 1], begun, logit[:, h, 0:n], plan.top[:, h:h + 1], ALU.add, ALU.max)
                    v.drain()
                    V.tensor_tensor(ex[:, 0, :, 0:n], top[:, :, 0:n], bcast(begun, 1, HEADS), ALU.add)
                    V.tensor_tensor(ex[:, 1, :, 0:n], logit[:, :, 0:n], top[:, :, 1:n + 1], ALU.subtract)
                    V.tensor_copy(plan.top[:], top[:, :, n])
                    V.tensor_copy(heads(at, n, NV, ROW), top[:, :, 1:n + 1])
                    v.drain()
                    V.tensor_tensor(ex[:, 0, :, 0:n], ex[:, 0, :, 0:n], top[:, :, 1:n + 1], ALU.subtract).then_inc(s_x, 1)

                def sums(j, at, n):
                    v.wait_ge(s_ex, j + 1)
                    weights = ex[:, 1, :, 0:n]
                    rows = G[:, ds(at, n), 0:HE].rearrange("p w (h e) -> p w h e", h=HEADS)
                    V.tensor_tensor(rows, rows, bcast(weights.rearrange("p h w -> p w h"), 3, EXPERTS), ALU.mult)
                    V.tensor_copy(heads(at, n, HE, NV), weights)
                    v.drain()
                    for k in range(NV):
                        h = k // EXPERTS if k < HE else k - HE
                        V.tensor_tensor_scan(G[:, ds(at, n), k], ex[:, 0, h, 0:n], G[:, ds(at, n), k], plan.sums[:, k:k + 1],
                                             ALU.mult, ALU.add)
                    v.drain()
                    V.tensor_copy(plan.sums[:], G[:, ds(at + n - 1, 1), 0:NV].rearrange("p o r -> p (o r)")).then_inc(s_done, 1)

                for h in range(2):
                    V.tensor_copy(ixs[:, h, :], plan.idx[:, h * SHALF:(h + 1) * SHALF]).then_inc(s_ix, 1)
                V.tensor_tensor(keep[:], plan.dst[:, 1:W + 1], plan.dst[:, 0:W], ALU.is_equal)
                V.memset(plan.top[:], -BIG)
                V.memset(plan.sums[:], 0.0)
                V.memset(ex[:], 0.0)
                V.memset(G[:, W_LOW:W, :], 0.0).then_inc(s_blank, 1)
                v.drain()
                V.tensor_reduce(plan.through[:], keep[:, 0:W_LOW], AX_X, ALU.min)
                with v.If(wide > 0):
                    v.drain()
                    V.tensor_reduce(plan.through[:], keep[:], AX_X, ALU.min)
                V.tensor_scalar(plan.into[:], plan.dst[:, 1:2], 1.0, keep[:, 0:1], ALU.add, ALU.mult)
                v.drain()
                V.tensor_scalar(plan.into[:], plan.into[:], -1.0, None, ALU.add)
                V.tensor_scalar(start[:], keep[:], BIG, -BIG, ALU.mult, ALU.add)
                V.tensor_scalar(width_f[:], plan.gap[:], -1.0, float(W), ALU.mult, ALU.add)
                v.drain()
                V.tensor_scalar(bound[:], c.iota_row[:], width_f[:], None, ALU.mult)
                v.wait_ge(s_first, 16)
                V.tensor_copy(dlast[:], first_row[:, HE + HEADS:ROW])

                with v.Fori(0, BLK_ITERS) as b:
                    take(b)
                    v.drain()
                    V.tensor_tensor(past[:], bcast(plan.place[:, ds(b * GT, GT)], 2, P), bcast(bound[:], 1, GT), ALU.is_ge)
                    v.drain()
                    V.tensor_reduce(plan.lane[:, ds(b * GT, GT)], past[:], AX_X, ALU.add)
                v.drain()
                V.tensor_scalar(plan.lane[:], plan.lane[:], -1.0, None, ALU.add)
                v.drain()
                V.scalar_tensor_tensor(plan.place[:], plan.lane[:], plan.gap[:], plan.place[:], ALU.mult, ALU.add)
                v.drain()
                V.tensor_copy(plan.endpos[:], plan.place[:])
                maxima(0, BLOCK)
                with v.Fori(1, BLOCKS) as j:
                    with v.Fori(0, AHEAD) as i:
                        take(j * BLK_ITERS + i)
                    sums(j - 1, (j - 1) * BLOCK, BLOCK)
                    with v.Fori(AHEAD, BLK_ITERS) as i:
                        take(j * BLK_ITERS + i)
                    maxima(j * BLOCK, BLOCK)
                for b in range(BLOCKS * BLK_ITERS, LOW_ITERS):
                    take(b)
                    if b == BLOCKS * BLK_ITERS + 1:
                        sums(BLOCKS - 1, (BLOCKS - 1) * BLOCK, BLOCK)
                maxima(*tail[0])
                sums(BLOCKS, *tail[0])
                with v.If(wide > 0):
                    v.wait_ge(s_blankst, 16)
                    with v.Fori(LOW_ITERS, G_ITERS) as b:
                        take(b)
                    for i in (1, 2):
                        maxima(*tail[i])
                        sums(BLOCKS + i, *tail[i])
                with v.If(wide < 1):
                    v.sem_inc(s_x, 2)

            @block.tensor
            def _(pe):
                pe.sem_inc(s_s, 1)
                pe.wait_ge(s_w, 144)

                def first(g, e):
                    for i in range(NF):
                        n = (g * EXPERTS + e) * NF + i
                        pe.wait_ge(s_ge, n + 1)
                        for k in range(KC):
                            last = nc.tensor.matmul(psF[i % FB][:, 0:HB], w1[:, e, k, (i // 2) * P:(i // 2 + 1) * P],
                                                    yT[:, k, (i % 2) * HB:(i % 2 + 1) * HB], start=(k == 0), stop=(k == KC - 1))
                        last.then_inc(s_f, 1)

                def second(g, e):
                    pe.wait_ge(s_ge, (g * EXPERTS + e) * NF + NF + FB)
                    for u in range(NS):
                        n = (g * EXPERTS + e) * NS + u
                        bank = psY[(e * NS + u) % YB]
                        pe.wait_ge(s_yc, n + 1)
                        for k in range(HC):
                            last = nc.tensor.matmul(bank[:, 0:D], hh[:, k].rearrange("p a b -> p (a b)")[:, u * P:(u + 1) * P],
                                                    w2[:, e, k, :], start=(k == 0), stop=(k == HC - 1))
                        last.then_inc(s_s, 1)

                with pe.Fori(0, GROUPS) as g:
                    pe.wait_ge(s_yT, 16 * g + 16)
                    for e in range(EXPERTS):
                        first(g, e)
                        second(g, e)

            @block.scalar
            def _(act):
                act.sem_inc(s_ge, FB)
                act.sem_inc(s_yc, YB)
                act.wait_ge(s_w, 144)

                def expert(g, e):
                    n = g * EXPERTS + e
                    act.wait_ge(s_s, n * NS + 1)
                    for i in range(NF):
                        act.wait_ge(s_f, n * NF + i + 1)
                        nc.scalar.activation(hh[:, i // 2, i % 2, :], psF[i % FB][:, 0:HB], ACT.Gelu,
                                             bias=b1[:, e * HC + i // 2:e * HC + i // 2 + 1]).then_inc(s_ge, 1)
                    if not (isinstance(g, int) and n == 0):
                        act.wait_ge(s_yst, 16 * n)
                    for u in range(NS):
                        act.wait_ge(s_s, n * NS + u + 2)
                        nc.scalar.copy(yo[:, u, :], psY[(e * NS + u) % YB][:, 0:D]).then_inc(s_yc, 1)
                    act.wait_ge(s_yc, n * NS + NS + YB)
                    act.dma_start(c.y_d[e].rearrange("(t p) d -> p t d", p=P)[:, ds(g * GT, GT), :], yo[:]).then_inc(s_yst, 16)

                def exponentials(j, n):
                    act.drain()
                    act.wait_ge(s_x, j + 1)
                    nc.scalar.activation(ex[:, :, :, 0:n], ex[:, :, :, 0:n], ACT.Exp).then_inc(s_ex, 1)

                for e in range(EXPERTS):
                    expert(0, e)
                with act.Fori(1, GROUPS) as g:
                    for e in range(EXPERTS):
                        expert(g, e)
                        if e == EXPERTS // 2 - 1:
                            exponentials(g - 1, BLOCK)
                exponentials(BLOCKS - 1, BLOCK)
                for i, (_, n) in enumerate(tail):
                    exponentials(BLOCKS + i, n)
                act.wait_ge(s_yst, 16 * GROUPS * EXPERTS)


def gat_combine(c, a, out, plan):
    nc = c.nc
    CAR = NV + HEADS + 1
    ctx, sb, ps = c.open()
    with ctx:
        lanes = sb("gc_lanes", [P, 2, NV])
        turned = sb("gc_turned", [NV, 2, P])
        chain = sb("gc_chain", [NV, P + 1])
        carry = sb("gc_carry", [P, CAR])
        pen = sb("gc_pen", [P, 1])
        here = sb("gc_here", [P, HEADS])
        scale = sb("gc_scale", [P, 2, HEADS])
        hot = sb("gc_hot", [P, TILES, P])
        num = sb("gc_num", [P, TILES, ROW])
        got = sb("gc_got", [P, TILES, CAR])
        node_i = sb("gc_node_i", [P, TILES], I32)
        node_f = sb("gc_node_f", [P, TILES])
        same = sb("gc_same", [P, TILES])
        both = sb("gc_both", [P, TILES, HEADS])
        part = sb("gc_part", [P, 2, TILES, HEADS])
        den = sb("gc_den", [P, TILES, HEADS])
        par = sb("gc_par", [P, 3, HE])
        dev = sb("gc_dev", [P, TILES, HE])
        sq = sb("gc_sq", [P, TILES, HE])
        mu = sb("gc_mu", [P, TILES])
        var = sb("gc_var", [P, TILES])
        score = sb("gc_score", [P, TILES, EXPERTS])
        wins = sb("gc_wins", [P, TILES])
        rank = sb("gc_rank", [P, TILES, EXPERTS])
        gates = sb("gc_gates", [P, TILES, EXPERTS])
        ps_in = ps("gc_ps_in", [P, 512])
        ps_out = ps("gc_ps_out", [P, 512])
        s_in, s_lanes, s_turned, s_chain, s_back, s_exp_in, s_exp, s_std, s_node, s_hot, s_hotp, s_hotT, s_sel = (
            c.sem("gc_" + n) for n in ("in", "lanes", "turned", "chain", "back", "exp_in", "exp", "std", "node",
                                       "hot", "hotp", "hotT", "sel"))
        s_num = [c.sem(f"gc_num{i}") for i in range(2)]
        CUT = 4
        parts = [slice(0, CUT * GT), slice(CUT * GT, TILES)]
        widths = (HEADS, NV)

        NB = 4
        buf = [sb(f"co_rows{i}", [P, EXPERTS + 1, GT, D]) for i in range(NB)]
        gT = hot[0:EXPERTS, 0:GT, :].rearrange("p t l -> p (t l)")
        b2 = sb("co_b2", [EXPERTS, D])
        ps_gT = ps("co_ps_gT", [P, 1024])
        ps_b = ps("co_ps_b", [P, 2048])
        s_gTp, s_gT, s_bias, s_sum, s_out = (c.sem("co_" + n) for n in ("gTp", "gT", "bias", "sum", "out"))
        s_load = [c.sem(f"co_in{i}") for i in range(NB)]
        x2_v = c.x2_d.rearrange("(t p) d -> p t d", p=P)
        y_v = [c.y_d[e].rearrange("(t p) d -> p t d", p=P) for e in range(EXPERTS)]
        out_v = out.rearrange("(t p) d -> p t d", p=P)

        BATCHES = -(-TILES // 4)
        PER = 512 // CAR

        def sel(t):
            at = t // PER * 512 + t % PER * CAR
            return ps_b[:, at:at + CAR]

        with nc.Block() as block:
            @block.sync
            def _(sp):
                sp.dma_start(b2[:], a["b2"]).then_inc(s_in, 16)
                for i, name in enumerate(("b_gat", "gamma", "beta")):
                    sp.dma_start(par[:, i, :], a[name].to_broadcast([P, HE])).then_inc(s_in, 16)
                for g in range(GROUPS):
                    if g >= NB:
                        sp.wait_ge(s_out, 16 * (g - NB + 1))
                    at = slice(g * GT, (g + 1) * GT)
                    sp.dma_start(buf[g % NB][:, EXPERTS], x2_v[:, at, :]).then_inc(s_load[g % NB], 16)
                    for e in range(EXPERTS):
                        sp.dma_start(buf[g % NB][:, e], y_v[e][:, at, :]).then_inc(s_load[g % NB], 16)

            @block.gpsimd
            def _(pool):
                nc.gpsimd.iota(node_i[:], pattern=[[P, TILES]], base=0, channel_multiplier=1).then_inc(s_node, 1)
                for t in range(TILES):
                    pool.indirect_dma_start(num[:, t, :], None, c.sums_d,
                                            bass.IndirectOffsetOnAxis(ap=plan.endpos[:, t:t + 1], axis=0)).then_inc(s_num[t // (CUT * GT)], 16)

            @block.tensor
            def _(pe):
                for r, n in enumerate(widths):
                    pe.wait_ge(s_lanes, r + 1)
                    for i in range(2):
                        last = nc.tensor.transpose(ps_in[0:n, i * P:(i + 1) * P], lanes[:, i, 0:n], c.ident[:])
                    last.then_inc(s_turned, 1)
                    pe.wait_ge(s_chain, r + 1)
                    nc.tensor.transpose(ps_out[:, 0:n], chain[0:n, 0:P], c.ident[0:n, 0:n]).then_inc(s_back, 1)
                pe.wait_ge(s_hot, 1)
                for b in range(BATCHES):
                    if b >= 2:
                        pe.wait_ge(s_hotT, b - 1)
                    for t in range(4 * b, min(4 * b + 4, TILES)):
                        last = nc.tensor.transpose(ps_gT[:, b % 2 * 512 + t % 4 * P:b % 2 * 512 + (t % 4 + 1) * P], hot[:, t, :], c.ident[:])
                    last.then_inc(s_hotp, 1)
                pe.wait_ge(s_hotT, BATCHES)
                pe.wait_ge(s_lanes, 3)
                for t in range(TILES):
                    last = nc.tensor.matmul(sel(t), hot[:, t, :], carry[:], start=True, stop=True)
                last.then_inc(s_sel, 1)
                pe.wait_ge(s_in, 64)
                for g in range(GROUPS):
                    pe.wait_ge(s_exp_in, 4 if g < CUT else 7)
                    if g:
                        pe.wait_ge(s_gT, g)
                    for u in range(GT):
                        last = nc.tensor.transpose(ps_gT[0:EXPERTS, u * P:(u + 1) * P], gates[:, g * GT + u, :], c.ident[:])
                    last.then_inc(s_gTp, 1)
                    pe.wait_ge(s_gT, g + 1)
                    if g:
                        pe.wait_ge(s_sum, g)
                    for u in range(GT):
                        last = nc.tensor.matmul(ps_b[:, u * D:(u + 1) * D], gT[:, u * P:(u + 1) * P], b2[:], start=True, stop=True)
                    last.then_inc(s_bias, 1)

            @block.scalar
            def _(act):
                act.wait_ge(s_exp_in, 1)
                nc.scalar.activation(scale[:], scale[:], ACT.Exp).then_inc(s_exp, 1)
                for b in range(BATCHES):
                    act.wait_ge(s_hotp, b + 1)
                    n = min(4, TILES - 4 * b)
                    nc.scalar.copy(hot[:, 4 * b:4 * b + n, :].rearrange("p t l -> p (t l)"),
                                   ps_gT[:, b % 2 * 512:b % 2 * 512 + n * P]).then_inc(s_hotT, 1)

                def turned_gates(g):
                    act.wait_ge(s_gTp, g + 1)
                    nc.scalar.copy(gT, ps_gT[0:EXPERTS, 0:GN]).then_inc(s_gT, 1)

                for i, T in enumerate(parts):
                    act.wait_ge(s_exp_in, 3 * i + 2)
                    nc.scalar.activation(part[:, :, T], part[:, :, T], ACT.Exp).then_inc(s_exp, 1)
                    act.wait_ge(s_std, 2 * i + 1)
                    nc.scalar.activation(var[:, T], var[:, T], ACT.Sqrt, bias=c.eps[:], scale=1.0 / HE).then_inc(s_std, 1)
                    act.wait_ge(s_exp_in, 3 * i + 3)
                    nc.scalar.activation(score[:, T], score[:, T], ACT.Exp).then_inc(s_exp, 1)
                    if i == 0:
                        turned_gates(0)
                for g in range(GROUPS):
                    if g + 1 < GROUPS:
                        turned_gates(g + 1)
                    act.wait_ge(s_sum, g + 1)
                    act.dma_start(out_v[:, g * GT:(g + 1) * GT, :], buf[g % NB][:, EXPERTS]).then_inc(s_out, 16)
                    act.wait_ge(s_out, 16 * (g + 1))

            @block.vector
            def _(v):
                V = nc.vector

                def carries(r, op0, op1, first):
                    n = widths[r]
                    v.drain()
                    v.sem_inc(s_lanes, 1)
                    v.wait_ge(s_turned, r + 1)
                    V.tensor_copy(turned[0:n].rearrange("p a b -> p (a b)"), ps_in[0:n, 0:2 * P])
                    V.memset(chain[:, 0:1], first)
                    v.drain()
                    V.tensor_tensor_scan(chain[0:n, 1:P + 1], turned[0:n, 0, :], turned[0:n, 1, :], first, op0, op1)
                    v.drain()
                    v.sem_inc(s_chain, 1)
                    v.wait_ge(s_back, r + 1)

                V.tensor_tensor(hot[:], bcast(c.iota_row[:], 1, TILES), bcast(plan.lane[:], 2, P), ALU.is_equal).then_inc(s_hot, 1)
                V.tensor_scalar(pen[:], plan.through[:], BIG, -BIG, ALU.mult, ALU.add)
                v.drain()
                V.tensor_copy(lanes[:, 0, 0:HEADS], pen[:].to_broadcast([P, HEADS]))
                V.tensor_copy(lanes[:, 1, 0:HEADS], plan.top[:])
                carries(0, ALU.add, ALU.max, -BIG)
                V.tensor_copy(carry[:, NV:NV + HEADS], ps_out[:, 0:HEADS])
                V.tensor_copy(carry[:, NV + HEADS:CAR], plan.into[:])
                v.drain()
                V.tensor_scalar(scale[:, 0, :], carry[:, NV:NV + HEADS], pen[:], None, ALU.add)
                v.drain()
                V.tensor_tensor(here[:], scale[:, 0, :], plan.top[:], ALU.max)
                v.drain()
                V.tensor_tensor(scale[:, 0, :], scale[:, 0, :], here[:], ALU.subtract)
                V.tensor_tensor(scale[:, 1, :], plan.top[:], here[:], ALU.subtract)
                v.drain()
                v.sem_inc(s_exp_in, 1)
                v.wait_ge(s_exp, 1)
                V.tensor_copy(lanes[:, 0, 0:HE].rearrange("p (h e) -> p h e", h=HEADS), bcast(scale[:, 0, :], 2, EXPERTS))
                V.tensor_copy(lanes[:, 0, HE:NV], scale[:, 0, :])
                V.tensor_tensor(lanes[:, 1, 0:HE].rearrange("p (h e) -> p h e", h=HEADS),
                                plan.sums[:, 0:HE].rearrange("p (h e) -> p h e", h=HEADS), bcast(scale[:, 1, :], 2, EXPERTS), ALU.mult)
                V.tensor_tensor(lanes[:, 1, HE:NV], plan.sums[:, HE:NV], scale[:, 1, :], ALU.mult)
                carries(1, ALU.mult, ALU.add, 0.0)
                V.tensor_copy(carry[:, 0:NV], ps_out[:, 0:NV])
                v.drain()
                v.sem_inc(s_lanes, 1)

                v.wait_ge(s_node, 1)
                V.tensor_copy(node_f[:], node_i[:])
                v.wait_ge(s_sel, 1)
                for t in range(0, TILES, PER):
                    n = min(PER, TILES - t)
                    V.tensor_copy(got[:, t:t + n, :], ps_b[:, t // PER * 512:t // PER * 512 + n * CAR].rearrange("p (t r) -> p t r", r=CAR))
                v.drain()
                V.tensor_tensor(same[:], got[:, :, CAR - 1], node_f[:], ALU.is_equal)
                v.drain()
                V.tensor_scalar(same[:], same[:], BIG, -BIG, ALU.mult, ALU.add)
                v.drain()
                V.tensor_tensor(got[:, :, NV:NV + HEADS], got[:, :, NV:NV + HEADS], bcast(same[:], 2, HEADS), ALU.add)
                v.drain()

                def gates_of(i):
                    T = parts[i]
                    v.wait_ge(s_num[i], 16 * (T.stop - T.start))
                    V.tensor_tensor(both[:, T], got[:, T, NV:NV + HEADS], num[:, T, NV:ROW], ALU.max)
                    v.drain()
                    V.tensor_tensor(part[:, 0, T], got[:, T, NV:NV + HEADS], both[:, T], ALU.subtract)
                    V.tensor_tensor(part[:, 1, T], num[:, T, NV:ROW], both[:, T], ALU.subtract)
                    v.drain()
                    v.sem_inc(s_exp_in, 1)
                    v.wait_ge(s_exp, 2 * i + 2)
                    for j, x in enumerate((got, num)):
                        rows = x[:, T, 0:HE].rearrange("p t (h e) -> p t h e", h=HEADS)
                        V.tensor_tensor(rows, rows, bcast(part[:, j, T], 3, EXPERTS), ALU.mult)
                        V.tensor_tensor(x[:, T, HE:NV], x[:, T, HE:NV], part[:, j, T], ALU.mult)
                    v.drain()
                    V.tensor_tensor(num[:, T, 0:NV], num[:, T, 0:NV], got[:, T, 0:NV], ALU.add)
                    v.drain()
                    v.wait_ge(s_in, 64)
                    V.tensor_scalar(den[:, T], num[:, T, HE:NV], 1e-16, None, ALU.add)
                    v.drain()
                    V.reciprocal(den[:, T], den[:, T])
                    v.drain()
                    V.tensor_tensor(dev[:, T].rearrange("p t (h e) -> p t h e", h=HEADS),
                                    num[:, T, 0:HE].rearrange("p t (h e) -> p t h e", h=HEADS), bcast(den[:, T], 3, EXPERTS), ALU.mult)
                    v.drain()
                    V.tensor_tensor(dev[:, T], dev[:, T], bcast(par[:, 0, :], 1, T.stop - T.start), ALU.add)
                    v.drain()
                    V.tensor_reduce(mu[:, T], dev[:, T], AX_X, ALU.add)
                    v.drain()
                    V.scalar_tensor_tensor(dev[:, T], bcast(mu[:, T], 2, HE), -1.0 / HE, dev[:, T], ALU.mult, ALU.add)
                    v.drain()
                    V.tensor_tensor(sq[:, T], dev[:, T], dev[:, T], ALU.mult)
                    v.drain()
                    V.tensor_reduce(var[:, T], sq[:, T], AX_X, ALU.add).then_inc(s_std, 1)
                    v.wait_ge(s_std, 2 * i + 2)
                    V.reciprocal(var[:, T], var[:, T])
                    v.drain()
                    V.tensor_tensor(dev[:, T], dev[:, T], bcast(var[:, T], 2, HE), ALU.mult)
                    v.drain()
                    V.tensor_tensor(dev[:, T], dev[:, T], bcast(par[:, 1, :], 1, T.stop - T.start), ALU.mult)
                    v.drain()
                    V.tensor_tensor(dev[:, T], dev[:, T], bcast(par[:, 2, :], 1, T.stop - T.start), ALU.add)
                    v.drain()
                    V.tensor_reduce(score[:, T], dev[:, T].rearrange("p t (h e) -> p t e h", h=HEADS), AX_X, ALU.add)
                    v.drain()
                    V.tensor_scalar(score[:, T], score[:, T], 1.0 / HEADS, None, ALU.mult)
                    for e in range(EXPERTS):
                        V.memset(rank[:, T, e], float(e))
                    v.drain()
                    for e in range(EXPERTS):
                        for f in range(e + 1, EXPERTS):
                            V.tensor_tensor(wins[:, T], score[:, T, f], score[:, T, e], ALU.is_gt)
                            v.drain()
                            V.tensor_tensor(rank[:, T, e], rank[:, T, e], wins[:, T], ALU.add)
                            V.tensor_tensor(rank[:, T, f], rank[:, T, f], wins[:, T], ALU.subtract)
                            v.drain()
                    V.tensor_reduce(mu[:, T], score[:, T], AX_X, ALU.max)
                    V.tensor_scalar(rank[:, T], rank[:, T], 2.0, None, ALU.is_lt)
                    v.drain()
                    V.tensor_tensor(score[:, T], score[:, T], bcast(mu[:, T], 2, EXPERTS), ALU.subtract).then_inc(s_exp_in, 1)
                    v.wait_ge(s_exp, 2 * i + 3)
                    V.tensor_tensor(score[:, T], score[:, T], rank[:, T], ALU.mult)
                    v.drain()
                    V.tensor_reduce(mu[:, T], score[:, T], AX_X, ALU.add)
                    v.drain()
                    V.reciprocal(mu[:, T], mu[:, T])
                    v.drain()
                    V.tensor_tensor(gates[:, T], score[:, T], bcast(mu[:, T], 2, EXPERTS), ALU.mult)
                    v.drain()
                    v.sem_inc(s_exp_in, 1)

                def output(g):
                    b = buf[g % NB]
                    v.wait_ge(s_load[g % NB], 16 * (EXPERTS + 1) * (g // NB + 1))
                    for e in range(EXPERTS):
                        for u in range(GT):
                            V.scalar_tensor_tensor(b[:, EXPERTS, u, :], b[:, e, u, :], gates[:, g * GT + u, e:e + 1],
                                                   b[:, EXPERTS, u, :], ALU.mult, ALU.add)
                        v.drain()
                    v.wait_ge(s_bias, g + 1)
                    V.tensor_tensor(b[:, EXPERTS].rearrange("p t d -> p (t d)"), b[:, EXPERTS].rearrange("p t d -> p (t d)"),
                                    ps_b[:, 0:GT * D], ALU.add).then_inc(s_sum, 1)

                gates_of(0)
                output(0)
                gates_of(1)
                for g in range(1, GROUPS):
                    output(g)


def lay_out(inputs):
    col = lambda v: np.ascontiguousarray(v.reshape(-1, P).T)
    valid = np.zeros((N_PAD,), np.float32)
    valid[:N_NODES] = 1.0
    i = {k: np.asarray(v) for k, v in inputs.items()}
    pad = SORT_N - E_GNN
    edges = i["L0_ffn_edge_index"]
    return {
        "x": np.pad(i["x"], ((0, N_PAD - N_NODES), (0, 0)), mode="edge"),
        "src": np.pad(i["src"], (0, pad)).reshape(P, LANE),
        "dst": np.pad(i["dst"], (0, pad), constant_values=PAD_DST).reshape(P, LANE),
        "gat_src": edges[0].reshape(P, LANE), "gat_dst": edges[1].reshape(P, LANE),
        "ln_g": col(i["L0_mix_ln_g"]), "ln_b": col(i["L0_mix_ln_b"]),
        "wqkv": i["L0_mix_Wqkv"], "wproj": i["L0_mix_Wproj"], "wself": i["L0_gnn_W_self"],
        "wneigh": i["L0_gnn_W_neigh"], "wg1": i["L0_mix_Wg1"], "wg2": i["L0_mix_Wg2"],
        "bg1": i["L0_mix_bg1"].reshape(GATE_H, 1), "bg2": col(i["L0_mix_bg2"]),
        "bproj": i["L0_mix_bproj"].reshape(1, D), "b_gnn": i["L0_gnn_b"].reshape(1, D),
        "valid": col(valid),
        "w_gat": i["L0_ffn_W_gat"], "att_src": i["L0_ffn_att_src"].reshape(1, HE), "att_dst": i["L0_ffn_att_dst"].reshape(1, HE),
        "b_gat": i["L0_ffn_b_gat"].reshape(1, HE), "gamma": i["L0_ffn_ln_gamma"].reshape(1, HE),
        "beta": i["L0_ffn_ln_beta"].reshape(1, HE),
        "w1": i["L0_ffn_W1"], "w2": i["L0_ffn_W2"],
        "b1": col(i["L0_ffn_b1"]), "b2": i["L0_ffn_b2"],
    }




def program(nc, a, out):
    c = Core(nc)
    c.skey_gnn = c.dram("skey_gnn", [SORT_N])
    c.skey_gat = c.dram("skey_gat", [P + GAT_N])
    c.tail_d = c.dram("tail_d", [SELF_N])
    c.low_d = c.dram("low_d", [SELF_N])
    c.xn_tab = c.dram("xn_tab", [N_PAD, D])
    c.xnT_d = c.dram("xnT_d", [P, KC, N_PAD])
    c.xn2T_d = c.dram("xn2T_d", [P, KC, N_PAD])
    c.base_d = c.dram("base_d", [N_PAD, 2 * D])
    c.x2_d = c.dram("x2_d", [N_PAD, D])
    c.x2nT_d = c.dram("x2nT_d", [P, KC, N_PAD])
    c.hx_d = c.dram("hx_d", [N_PAD, ROW])
    c.y_d = c.dram("y_d", [EXPERTS, N_PAD, D])
    c.sums_d = c.dram("sums_d", [GAT_N, ROW])
    constants(c)
    key_tables(c)
    plan = GatPlan(lambda name, shape, dt=F32: nc.alloc_sbuf_tensor(name, shape, dt))
    ctx, sb, ps = c.open()
    with ctx:
        t = StepTables(sb)
        ncm = sb("ncm", [1, D])
        acc = sb("acc", [P, TILES * (D + 1)])
        prepare(c, a, t, ncm, acc)
        aggregate(c, a, t, ncm, acc, plan)
        gnn_out(c, a, acc, plan)
    gat_gather_experts(c, a, plan)
    gat_combine(c, a, out, plan)


def kernel(**inputs):
    import concourse.bacc as _bacc
    from concourse.bass_utils import run_bass_kernel_spmd as _run

    nc = _bacc.Bacc("TRN2", target_bir_lowering=False, num_devices=1)
    arrays, aps = {}, {}
    for name, array in lay_out(inputs).items():
        array = np.ascontiguousarray(array)
        arrays[f"in_{name}_dram"] = array
        aps[name] = nc.dram_tensor(f"in_{name}_dram", array.shape, mybir.dt.from_np(array.dtype), kind="ExternalInput").ap()
    out = nc.dram_tensor("out_0_dram", (N_PAD, D), F32, kind="ExternalOutput").ap()
    program(nc, aps, out)
    r = _run(nc, [arrays], core_ids=[0])
    return r.results[0]["out_0_dram"][:N_NODES]
```
